# Optimizing a Trainium2 kernel written in Bass

```python
import numpy as np
import jax
import jax.numpy as jnp

def _softmax(x, axis=-1):
    return jax.nn.softmax(x, axis=axis)

def _gelu(x):
    return jax.nn.gelu(x, approximate=True)

def _silu(x):
    return jax.nn.silu(x)

def _sigmoid(x):
    return jax.nn.sigmoid(x)

def _layernorm(x, axis=-1, eps=1e-05):
    m = jnp.mean(x, axis=axis, keepdims=True)
    v = jnp.var(x, axis=axis, keepdims=True)
    return (x - m) / jnp.sqrt(v + eps)

def _scatter_add(tgt, idx, src, axis=0):
    return tgt.at[idx].add(src)

def _segment_sum(src, seg, n):
    return jax.ops.segment_sum(src, seg, n)
kernel_name = 'mk_seq_postln_d2_jaxref_r4_a4c859'

def setup_inputs(seed: int=0):
    np.random.seed(seed)
    _w = jnp.asarray

    def _L0_attn_setup():
        import math
        import jax, jax.numpy as jnp
        import numpy as np
        D_MODEL = 256
        N_HEADS = 16
        HEAD_DIM = D_MODEL // N_HEADS
        B, L = (1, 1024)

        def _slopes(n_heads):
            ratio = 2.0 ** (-8.0 / n_heads)
            return jnp.asarray([ratio ** (i + 1) for i in range(n_heads)], dtype=jnp.float32)
        key = jax.random.key(seed)
        ks = jax.random.split(key, 5)
        scale = 1.0 / math.sqrt(D_MODEL)
        return {'x': jax.random.normal(ks[0], (B, L, D_MODEL), dtype=jnp.float32), 'q_w': jax.random.normal(ks[1], (D_MODEL, D_MODEL), dtype=jnp.float32) * scale, 'k_w': jax.random.normal(ks[2], (D_MODEL, D_MODEL), dtype=jnp.float32) * scale, 'v_w': jax.random.normal(ks[3], (D_MODEL, D_MODEL), dtype=jnp.float32) * scale, 'o_w': jax.random.normal(ks[4], (D_MODEL, D_MODEL), dtype=jnp.float32) * scale}
    _L0_attn_in = _L0_attn_setup()

    def _L0_ffn_setup():
        import jax, jax.numpy as jnp
        import numpy as np
        B, N, D = (4, 512, 256)
        SPARSITY = 0.01
        key = jax.random.key(seed)
        k1, k2, k3 = jax.random.split(key, 3)
        x = jax.random.normal(k1, (B, N, D), dtype=jnp.float32)
        spatial = jax.random.normal(k2, (D, D), dtype=jnp.float32) * 0.02
        freq = jnp.fft.fft(spatial, axis=-1)
        k = int(D * SPARSITY)
        mag = jnp.abs(freq)
        kth = jax.lax.top_k(mag, k)[0][:, -1:]
        w_sparse = jnp.where(mag >= kth, freq, 0.0 + 0j)
        bias = jax.random.normal(k3, (D,), dtype=jnp.float32) * 0.01
        return {'x': x, 'w_freq_real': jnp.real(w_sparse).astype(jnp.float32), 'w_freq_imag': jnp.imag(w_sparse).astype(jnp.float32), 'bias': bias}
    _L0_ffn_in = _L0_ffn_setup()

    def _L1_attn_setup():
        import jax, jax.numpy as jnp
        import numpy as np
        D_MODEL = 256
        N_HEAD = 8
        D_X = 64
        EPS = 1e-06
        key = jax.random.key(seed)
        ks = jax.random.split(key, 7)
        B, L = (4, 2048)
        x = jax.random.normal(ks[0], (B, L, D_MODEL), dtype=jnp.float32)
        s_qkv = 1.0 / np.sqrt(D_MODEL)
        w_qkv = jax.random.uniform(ks[1], (D_MODEL, 3 * N_HEAD * D_X), dtype=jnp.float32, minval=-s_qkv, maxval=s_qkv)
        b_qkv = jax.random.uniform(ks[2], (3 * N_HEAD * D_X,), dtype=jnp.float32, minval=-s_qkv, maxval=s_qkv)
        s_fc = 1.0 / np.sqrt(N_HEAD * D_X)
        w_fc = jax.random.uniform(ks[3], (N_HEAD * D_X, D_MODEL), dtype=jnp.float32, minval=-s_fc, maxval=s_fc)
        b_fc = jax.random.uniform(ks[4], (D_MODEL,), dtype=jnp.float32, minval=-s_fc, maxval=s_fc)
        gamma = jnp.ones((D_MODEL,), dtype=jnp.float32)
        beta = jnp.zeros((D_MODEL,), dtype=jnp.float32)
        return {'x': x, 'w_qkv': w_qkv, 'b_qkv': b_qkv, 'w_fc': w_fc, 'b_fc': b_fc, 'gamma': gamma, 'beta': beta}
    _L1_attn_in = _L1_attn_setup()

    def _L1_ffn_setup():
        import jax, jax.numpy as jnp
        import numpy as np
        B, S, D, F, E = (8, 256, 256, 1024, 8)
        EPS = 1e-05
        key = jax.random.key(seed)
        ks = jax.random.split(key, 4)
        s = 0.02
        return {'input_features': jax.random.normal(ks[0], (B, S, D), jnp.float32), 'centroids': jax.random.normal(ks[1], (E, D), jnp.float32) * 0.1, 'ln_g': jnp.ones((E, D), jnp.float32), 'ln_b': jnp.zeros((E, D), jnp.float32), 'w1': jax.random.normal(ks[2], (E, D, F), jnp.float32) * s, 'b1': jnp.zeros((E, F), jnp.float32), 'w2': jax.random.normal(ks[3], (E, F, D), jnp.float32) * s, 'b2': jnp.zeros((E, D), jnp.float32)}
    _L1_ffn_in = _L1_ffn_setup()
    _d = {'L0_attn_x': _L0_attn_in['x'], 'L0_attn_q_w': _L0_attn_in['q_w'], 'L0_attn_k_w': _L0_attn_in['k_w'], 'L0_attn_v_w': _L0_attn_in['v_w'], 'L0_attn_o_w': _L0_attn_in['o_w'], 'L0_ffn_w_freq_real': _L0_ffn_in['w_freq_real'], 'L0_ffn_w_freq_imag': _L0_ffn_in['w_freq_imag'], 'L0_ffn_bias': _L0_ffn_in['bias'], 'L1_attn_w_qkv': _L1_attn_in['w_qkv'], 'L1_attn_b_qkv': _L1_attn_in['b_qkv'], 'L1_attn_w_fc': _L1_attn_in['w_fc'], 'L1_attn_b_fc': _L1_attn_in['b_fc'], 'L1_attn_gamma': _L1_attn_in['gamma'], 'L1_attn_beta': _L1_attn_in['beta'], 'L1_ffn_centroids': _L1_ffn_in['centroids'], 'L1_ffn_ln_g': _L1_ffn_in['ln_g'], 'L1_ffn_ln_b': _L1_ffn_in['ln_b'], 'L1_ffn_w1': _L1_ffn_in['w1'], 'L1_ffn_b1': _L1_ffn_in['b1'], 'L1_ffn_w2': _L1_ffn_in['w2'], 'L1_ffn_b2': _L1_ffn_in['b2']}
    _x0 = _d['L0_attn_x']
    _d['L0_attn_x'] = jax.random.normal(jax.random.fold_in(jax.random.key(seed), 1), (2, 2048, 256), dtype=_x0.dtype)
    del _x0
    return _d

def reference(L0_attn_x, L0_attn_q_w, L0_attn_k_w, L0_attn_v_w, L0_attn_o_w, L0_ffn_w_freq_real, L0_ffn_w_freq_imag, L0_ffn_bias, L1_attn_w_qkv, L1_attn_b_qkv, L1_attn_w_fc, L1_attn_b_fc, L1_attn_gamma, L1_attn_beta, L1_ffn_centroids, L1_ffn_ln_g, L1_ffn_ln_b, L1_ffn_w1, L1_ffn_b1, L1_ffn_w2, L1_ffn_b2):

    def _L0_attn_ref(x, q_w, k_w, v_w, o_w):
        import math
        import jax, jax.numpy as jnp
        import numpy as np
        D_MODEL = 256
        N_HEADS = 16
        HEAD_DIM = D_MODEL // N_HEADS
        B, L = (1, 1024)

        def _slopes(n_heads):
            ratio = 2.0 ** (-8.0 / n_heads)
            return jnp.asarray([ratio ** (i + 1) for i in range(n_heads)], dtype=jnp.float32)
        b, l, _ = x.shape

        def proj(w):
            return (x @ w).reshape(b, l, N_HEADS, HEAD_DIM).transpose(0, 2, 1, 3)
        q, k, v = (proj(q_w), proj(k_w), proj(v_w))
        scale = math.sqrt(HEAD_DIM)
        scores = jnp.einsum('bhid,bhjd->bhij', q, k) / scale
        pos = jnp.arange(l)
        distance = jnp.abs(pos[None, :] - pos[:, None]).astype(jnp.float32)
        alibi = -distance[None, :, :] * _slopes(N_HEADS)[:, None, None]
        scores = scores + alibi[None]
        causal = pos[None, :] <= pos[:, None]
        scores = jnp.where(causal[None, None], scores, -jnp.inf)
        attn = jax.nn.softmax(scores, axis=-1)
        out = jnp.einsum('bhij,bhjd->bhid', attn, v)
        out = out.transpose(0, 2, 1, 3).reshape(b, l, D_MODEL)
        return out @ o_w

    def _L0_ffn_ref(x, w_freq_real, w_freq_imag, bias):
        import jax, jax.numpy as jnp
        import numpy as np
        B, N, D = (4, 512, 256)
        SPARSITY = 0.01
        w = jax.lax.complex(w_freq_real, w_freq_imag)
        x_freq = jnp.fft.fft(x, axis=-1)
        y_freq = jnp.einsum('bnd,do->bno', x_freq, w)
        y = jnp.real(jnp.fft.ifft(y_freq, axis=-1))
        return y + bias

    def _L1_attn_ref(x, w_qkv, b_qkv, w_fc, b_fc, gamma, beta):
        import jax, jax.numpy as jnp
        import numpy as np
        D_MODEL = 256
        N_HEAD = 8
        D_X = 64
        EPS = 1e-06
        B, L, D = x.shape
        H, dx = (N_HEAD, D_X)
        qkv = x @ w_qkv + b_qkv
        q, k, v = jnp.split(qkv, 3, axis=-1)
        q = q.reshape(B, L, H, dx).transpose(0, 2, 1, 3)
        k = k.reshape(B, L, H, dx).transpose(0, 2, 1, 3)
        v = v.reshape(B, L, H, dx).transpose(0, 2, 1, 3)
        scores = jnp.einsum('bhld,bhle->bhde', q, k) / jnp.sqrt(jnp.asarray(dx, x.dtype))
        attn = jax.nn.softmax(scores, axis=-1)
        out = jnp.einsum('bhld,bhde->bhle', v, attn)
        out = out.transpose(0, 2, 1, 3).reshape(B, L, H * dx)
        out = out @ w_fc + b_fc
        out = out + x
        mu = jnp.mean(out, axis=-1, keepdims=True)
        var = jnp.mean(jnp.square(out - mu), axis=-1, keepdims=True)
        out = (out - mu) * jax.lax.rsqrt(var + EPS) * gamma + beta
        return out

    def _L1_ffn_ref(input_features, centroids, ln_g, ln_b, w1, b1, w2, b2):
        import jax, jax.numpy as jnp
        import numpy as np
        B, S, D, F, E = (8, 256, 256, 1024, 8)
        EPS = 1e-05
        x = input_features.reshape(-1, D)
        aff = jax.lax.stop_gradient(x @ centroids.T)
        eid = jnp.argmax(aff, axis=-1)
        alpha = jax.nn.sigmoid(jnp.sum(x * centroids[eid], axis=-1, keepdims=True))
        mu = jnp.mean(x, axis=-1, keepdims=True)
        var = jnp.mean((x - mu) ** 2, axis=-1, keepdims=True)
        xn = (x - mu) * jax.lax.rsqrt(var + EPS)
        xln = xn * ln_g[eid] + ln_b[eid]
        onehot = jax.nn.one_hot(eid, E, dtype=x.dtype)
        ffn = jnp.zeros_like(x)
        for e in range(E):
            h = jax.nn.relu(xln @ w1[e] + b1[e])
            ffn = ffn + onehot[:, e:e + 1] * (h @ w2[e] + b2[e])
        out = x + alpha * ffn
        return out.reshape(input_features.shape)
    x = L0_attn_x
    x = _layernorm(x + _L0_attn_ref(x, L0_attn_q_w, L0_attn_k_w, L0_attn_v_w, L0_attn_o_w), axis=-1)
    x = _layernorm(x + _L0_ffn_ref(x, L0_ffn_w_freq_real, L0_ffn_w_freq_imag, L0_ffn_bias), axis=-1)
    x = _layernorm(x + _L1_attn_ref(x, L1_attn_w_qkv, L1_attn_b_qkv, L1_attn_w_fc, L1_attn_b_fc, L1_attn_gamma, L1_attn_beta), axis=-1)
    x = _layernorm(x + _L1_ffn_ref(x, L1_ffn_centroids, L1_ffn_ln_g, L1_ffn_ln_b, L1_ffn_w1, L1_ffn_b1, L1_ffn_w2, L1_ffn_b2), axis=-1)
    return x

_drawn_inputs = setup_inputs


def setup_inputs(seed=0):
    import zlib

    import numpy as np

    out = dict(_drawn_inputs(seed))
    spreads = {'L1_attn_gamma': (1.0, 0.2),
     'L1_attn_beta': (0.0, 0.1),
     'L1_ffn_ln_g': (1.0, 0.6),
     'L1_ffn_ln_b': (0.0, 0.8),
     'L1_ffn_b1': (0.0, 0.408),
     'L1_ffn_b2': (0.0, 0.1)}
    factors = {'L0_ffn_bias': 4.929, 'L1_attn_b_fc': 3.332}
    for name, (base, spread) in spreads.items():
        noise = np.random.default_rng([zlib.crc32(name.encode()), seed]).standard_normal(out[name].shape)
        drawn = base * np.exp(spread * noise) if base else spread * noise
        out[name] = jnp.asarray(drawn.astype(out[name].dtype))
    for name, factor in factors.items():
        out[name] = (out[name] * factor).astype(out[name].dtype)
    return out
```

```python
from contextlib import ExitStack

import numpy as np
import concourse.bass as bass
from concourse import mybir

F32 = mybir.dt.float32
BF16 = mybir.dt.bfloat16
I32 = mybir.dt.int32
ALU = mybir.AluOpType
ACTF = mybir.ActivationFunctionType
X = mybir.AxisListType.X

P = 128
BATCHES, LENGTH, D = 2, 2048, 256
TOKENS = BATCHES * LENGTH
KC = D // P
BLOCKS = TOKENS // P
TILE = 512
BPT = TILE // P
TILES = TOKENS // TILE
HEADS, HD = 16, 16
GH = 4
GROUPS = HEADS // GH
BPB = LENGTH // P
QT = LENGTH // TILE
EXTRA = 32
TERMS = [(0, 0), (0, 1), (0, 2), (1, 0), (1, 1), (2, 0)]
MAX_ROWS = (1, 3, 5)
H1, DX = 8, 64
EXPERTS, FF = 8, 1024
FC = FF // P
SLOT_TILES = BLOCKS + EXPERTS - 1
ROW = D + 2
MASKED = -1e30
NO_TOKEN = 1 << 20


class Signal:

    def __init__(self, nc, ctx, name, step=1):
        self.sem, self.step, self.n = ctx.enter_context(nc.semaphore(name)), step, 0

    def done(self, ins):
        ins.then_inc(self.sem, self.step)
        self.n += self.step
        return (self, self.n)


class Both:

    def __init__(self, *marks):
        self.marks = marks


class Waits:

    def __init__(self):
        self.seen = {}

    def __call__(self, engine, *marks):
        need = {}
        flat = [one for m in marks if m is not None for one in (m.marks if isinstance(m, Both) else (m,))]
        for signal, n in flat:
            need[signal] = max(n, need.get(signal, 0))
        for signal, n in need.items():
            if self.seen.get((id(engine), signal), 0) < n:
                engine.wait_ge(signal.sem, n)
                self.seen[(id(engine), signal)] = n


def program(nc, t, out):
    ctx = ExitStack()
    with ctx:
        pe, act, dve, pool, sp = nc.tensor, nc.scalar, nc.vector, nc.gpsimd, nc.sync
        wait = Waits()

        def signal(name, step=1):
            return Signal(nc, ctx, name, step)

        def sb(name, shape, dt=F32):
            return ctx.enter_context(nc.sbuf_tensor(name, shape, dt))

        by_pe, by_act, by_dve, by_pool = (signal(n) for n in ("by_pe", "by_act", "by_dve", "by_pool"))

        OPS = 2 * GH * LENGTH * 2
        PRING = 2 * GH
        VBYTES = BLOCKS * HEADS * (HD + 1) * 4
        big = sb("big", [P, (3 * OPS + PRING * 4096 + VBYTES) // 4])

        def carve(at, shape, dt=F32, parts=P):
            size = 2 if dt == BF16 else 4
            n = int(np.prod(shape))
            assert at % 4 == 0 and at + n * size <= 3 * OPS + PRING * 4096 + VBYTES
            v = big[0:parts, at // 4:(at + n * size) // 4]
            if dt != F32:
                v = v.bitcast(dt)
            if len(shape) > 1:
                names = " ".join(f"a{i}" for i in range(len(shape)))
                v = v.rearrange(f"p ({names}) -> p {names}", **{f"a{i}": s for i, s in enumerate(shape)})
            return v

        AT_P, AT_V = 3 * OPS, 3 * OPS + PRING * 4096
        tok = sb("tok", [P, BLOCKS, ROW])
        v_aug = carve(AT_V, [BLOCKS, HEADS, HD + 1])
        q_op = [carve(s * OPS, [QT, GH, TILE], BF16) for s in range(3)]
        k_op = [carve(s * OPS + OPS // 2, [GH, LENGTH], BF16) for s in range(3)]
        p_ring = [carve(AT_P + i * 4096, [1024]) for i in range(PRING)]

        ident = sb("ident", [P, P])
        ident_b = sb("ident_b", [P, P], BF16)
        masks = sb("masks", [P, 2, P], BF16)
        ones = sb("ones", [P, P])
        eps_col = sb("eps_col", [P, 3])
        spectral = sb("spectral", [P, KC, D])
        acc_t = [sb(f"acc_t{i}", [P, TILE]) for i in range(2)]
        part_max = [sb(f"part_max{i}", [P, BPT, GH, 4]) for i in range(2)]
        neg_max = sb("neg_max", [P, GH * BPT])
        max_rest = sb("max_rest", [P, GH * BPT])
        max_parts = [sb(f"max_parts{i}", [P, 3, GH * BPT], BF16) for i in range(2)]
        max_t = [sb(f"max_t{i}", [3 * GH * BPT, P], BF16) for i in range(2)]
        recip_l = sb("recip_l", [P, BPT, GH])
        stats = sb("stats", [P, 2, BPT, 6])
        moments = sb("moments", [P, 2, BPT, 2])
        std = sb("std", [P, 2, BPT])
        rstd = sb("rstd", [P, 2, BPT])

        pair = [ctx.enter_context(nc.psum_tensor(f"pair{i}", [P, 2 * TILE], F32)) for i in range(2)]
        single = [ctx.enter_context(nc.psum_tensor(f"single{i}", [P, TILE], F32)) for i in range(4)]
        bank = [pair[0][:, 0:TILE], pair[0][:, TILE:], pair[1][:, 0:TILE], pair[1][:, TILE:]] + \
               [s[:, :] for s in single]

        split_dram = nc.dram_tensor("split_dram", [2, 3, D, TOKENS], BF16).ap()
        routed_dram = nc.dram_tensor("routed_dram", [SLOT_TILES * P, ROW], F32).ap()

        def load(dst, src, name, engine=sp):
            s = signal(name, 16)
            return s.done(engine.dma_start(dst, src))

        x_view = t["L0_attn_x"].rearrange("b (n p) d -> p (b n) d", p=P)
        ident_in = load(ident[:, :], t["c_ident"], "ident_in")
        x_in = []
        for i in range(4):
            n = BLOCKS // 4
            x_in.append(load(tok[:, i * n:(i + 1) * n, 0:D], x_view[:, i * n:(i + 1) * n, :], f"x_in{i}"))
        AT_A = 2 * OPS
        w_qkv0 = [carve(AT_A + i * 2048, [KC, D]) for i in range(3)]
        w0_in = [load(w_qkv0[i][:, :, :], t[n].rearrange("(c p) n -> p c n", p=P), f"w0_in{i}", act)
                 for i, n in enumerate(("L0_attn_q_w", "L0_attn_k_w", "L0_attn_v_w"))]
        AT_SPEC = 0
        cos_m, sin_m, nsin_m, wr_m, wi_m, art_m, ait_m = (carve(AT_SPEC + i * 2048, [KC, D]) for i in range(7))
        spec_in = signal("spec_in", 16)
        for dst, src in ((cos_m, "c_cos"), (sin_m, "c_sin"), (nsin_m, "c_nsin"), (wr_m, "L0_ffn_w_freq_real"),
                         (wi_m, "L0_ffn_w_freq_imag")):
            spec_loaded = spec_in.done(act.dma_start(dst[:, :, :], t[src].rearrange("(c p) n -> p c n", p=P)))
        identb_in = load(ident_b[:, :], t["c_ident_b"].bitcast(BF16), "identb_in", act)
        masks_in = load(masks[:, :, :], t["c_masks"].bitcast(BF16).rearrange("a p n -> p a n"), "masks_in", act)

        ones_set = by_dve.done(dve.memset(ones[:, :], 1.0))
        by_dve.done(dve.memset(eps_col[:, 0:1], 1e-5))
        by_dve.done(dve.memset(eps_col[:, 1:2], 1e-6))
        eps_set = by_dve.done(dve.memset(eps_col[:, 2:3], 1e-5 / 4))
        pad_row = carve(2 * OPS + 26624, [ROW])
        by_pool.done(pool.memset(pad_row[:, 0:D + 1], 0.0))
        pad_set = by_pool.done(pool.memset(pad_row[:, D + 1:ROW].bitcast(I32), NO_TOKEN))
        v_ones = by_pool.done(pool.memset(v_aug[:, :, :, :], 1.0))

        wait(sp, pad_set)
        padded = load(routed_dram.rearrange("(n p) d -> p n d", p=P),
                      pad_row.unsqueeze(1).broadcast_to([P, SLOT_TILES, ROW]), "padded")

        wait(pe, spec_loaded)
        folds = []
        for dst, terms, b in ((art_m, ((wr_m, cos_m), (wi_m, sin_m)), 0), (ait_m, ((wi_m, cos_m), (wr_m, nsin_m)), 1)):
            for m in range(KC):
                for i, (l, r) in enumerate(terms):
                    for c in range(KC):
                        mm = pe.matmul(bank[b][:, m * D:(m + 1) * D], l[:, c, m * P:(m + 1) * P], r[:, c, :],
                                       start=(i == 0 and c == 0), stop=(i == 1 and c == KC - 1))
            folded = by_pe.done(mm)
            wait(dve, folded)
            folds.append(by_dve.done(dve.tensor_scalar(dst[:, :, :].rearrange("p c n -> p (c n)"), bank[b], 1.0 / D,
                                                       None, ALU.mult)))
        wait(pe, *folds)
        for m in range(KC):
            for i, (l, r) in enumerate(((art_m, cos_m), (ait_m, nsin_m))):
                for c in range(KC):
                    mm = pe.matmul(bank[2][:, m * D:(m + 1) * D], l[:, c, m * P:(m + 1) * P], r[:, c, :],
                                   start=(i == 0 and c == 0), stop=(i == 1 and c == KC - 1))
        folded = by_pe.done(mm)
        wait(dve, folded, ident_in)
        spec_copied = by_dve.done(dve.tensor_copy(spectral[:, :, :].rearrange("p c n -> p (c n)"), bank[2]))
        wait(dve, spec_copied)
        for m in range(KC):
            spectral_ready = by_dve.done(dve.tensor_tensor(spectral[:, m, m * P:(m + 1) * P],
                                                           spectral[:, m, m * P:(m + 1) * P], ident[:, :], ALU.add))

        x_t = carve(AT_P, [KC, TOKENS])
        parts = [carve(AT_A + 6144 + i * 3072, [3, TILE], BF16) for i in range(4)]
        rest = [carve(AT_A + 6144 + 12288 + i * 2048, [TILE]) for i in range(4)]
        part_free = [None] * 4
        store_sig = [signal(f"split_store{i}", 16) for i in range(4)]
        stored = {}
        xt_copied = {}
        bank_free = [None] * 8
        for b in (0, 1, 2):
            bank_free[b] = spec_copied
        n_split = 0
        n_bank = 0

        def transpose_x(tile):
            for half in range(2):
                b = (2 * tile + half) % 4
                wait(pe, x_in[(tile * BPT + 2 * half) * 4 // BLOCKS], ident_in, bank_free[b])
                for j in range(2):
                    blk = tile * BPT + half * 2 + j
                    for c in range(KC):
                        o = (j * KC + c) * P
                        mm = pe.transpose(bank[b][:, o:o + P], tok[:, blk, c * P:(c + 1) * P], ident[:, :])
                turned = by_pe.done(mm)
                t0 = (tile * BPT + half * 2) * P
                src = bank[b].rearrange("p (j c n) -> p c j n", j=2, c=KC)
                dst = x_t[:, :, t0:t0 + 2 * P].rearrange("p c (j n) -> p c j n", j=2)
                if half == 0:
                    wait(act, turned)
                    xt_copied[tile, half] = bank_free[b] = by_act.done(act.activation(dst, src, ACTF.Copy))
                else:
                    wait(dve, turned)
                    xt_copied[tile, half] = bank_free[b] = by_dve.done(dve.tensor_copy(dst, src))

        transpose_x(0)
        for tile in range(TILES):
            if tile + 1 < TILES:
                transpose_x(tile + 1)
            cols = slice(tile * TILE, (tile + 1) * TILE)
            wait(pe, xt_copied[tile, 0], xt_copied[tile, 1], *w0_in)
            for side, scale in ((0, 1.0 / np.sqrt(HD)), (1, 1.0)):
                for m in range(KC):
                    b = 4 + n_bank % 4
                    n_bank += 1
                    wait(pe, bank_free[b])
                    for c in range(KC):
                        mm = pe.matmul(bank[b], w_qkv0[side][:, c, m * P:(m + 1) * P], x_t[:, c, cols],
                                       start=(c == 0), stop=(c == KC - 1))
                    projected = by_pe.done(mm)
                    s = n_split % 4
                    n_split += 1
                    wait(act, projected, part_free[s])
                    high = by_act.done(act.activation(parts[s][:, 0, :], bank[b], ACTF.Copy, scale=float(scale)))
                    wait(dve, high, part_free[s])
                    rested = by_dve.done(dve.scalar_tensor_tensor(rest[s][:, :], bank[b], float(scale),
                                                                  parts[s][:, 0, :], ALU.mult, ALU.subtract))
                    bank_free[b] = rested
                    wait(act, rested)
                    middle = by_act.done(act.activation(parts[s][:, 1, :], rest[s][:, :], ACTF.Copy))
                    wait(pool, middle)
                    low = by_pool.done(pool.tensor_tensor(parts[s][:, 2, :], rest[s][:, :], parts[s][:, 1, :],
                                                          ALU.subtract))
                    wait(sp, low)
                    part_free[s] = store_sig[s].done(sp.dma_start(
                        split_dram[side, :, m * P:(m + 1) * P, cols].rearrange("a p n -> p a n"), parts[s][:, :, :]))
                    stored[side, m, tile] = part_free[s]
            for half in range(2):
                b = 4 + n_bank % 4
                n_bank += 1
                wait(pe, bank_free[b])
                for j in range(2):
                    blk = tile * BPT + half * 2 + j
                    for c in range(KC):
                        mm = pe.matmul(bank[b][:, j * D:(j + 1) * D], x_t[:, c, blk * P:(blk + 1) * P],
                                       w_qkv0[2][:, c, :], start=(c == 0), stop=(c == KC - 1))
                projected = by_pe.done(mm)
                blk = tile * BPT + half * 2
                src = bank[b].rearrange("p (j h d) -> p j h d", j=2, h=HEADS)
                wait(act, projected, v_ones)
                v_ready = bank_free[b] = by_act.done(act.activation(v_aug[:, blk:blk + 2, :, 0:HD], src, ACTF.Copy))
        a_pe_done = projected

        units = [(b, g) for b in range(BATCHES) for g in range(GROUPS)]
        op_sig = [signal(f"op_in{s}", 16) for s in range(3)]
        op_free = [spectral_ready, None, (a_pe_done, part_free)]
        op_ready = {}

        def load_operands(u):
            b, g = units[u]
            s = u % 3
            chunk = g * GH * HD // P
            first_tile = b * LENGTH // TILE
            wait(sp, *[stored[side, chunk, first_tile + i] for side in range(2) for i in range(LENGTH // TILE)])
            if u < 3:
                if s == 0:
                    wait(sp, spectral_ready)
                if s == 2:
                    wait(sp, a_pe_done, *part_free, by_act_done_a, low, padded)
                sp_src = t["c_key_rows"].bitcast(BF16)
                for h in range(GH):
                    op_sig[s].done(sp.dma_start(k_op[s][0:EXTRA, h, :], sp_src))
            else:
                wait(sp, op_free[s])
            op_sig[s].done(sp.dma_start(q_op[s][0:EXTRA, :, :, :], t["c_query_rows"].bitcast(BF16)[:, g, :, :, :]))
            for i, (q_part, k_part) in enumerate(TERMS):
                rows = slice(EXTRA + i * HD, EXTRA + (i + 1) * HD)
                q_src, k_src = (split_dram[side, part, g * GH * HD:(g + 1) * GH * HD, b * LENGTH:(b + 1) * LENGTH]
                                .rearrange("(h r) n -> r h n", h=GH) for side, part in ((0, q_part), (1, k_part)))
                op_sig[s].done(sp.dma_start(k_op[s][rows, :, :], k_src))
                for qt in range(QT):
                    op_ready[u] = op_sig[s].done(sp.dma_start(q_op[s][rows, qt, :, :],
                                                              q_src[:, :, qt * TILE:(qt + 1) * TILE]))

        by_act_done_a = v_ready
        for u in range(3):
            load_operands(u)

        ring_free = [bank_free[4], bank_free[5], bank_free[6]]
        ring_at = 0

        def ring():
            nonlocal ring_at
            i = ring_at % 3
            ring_at += 1
            wait(pe, ring_free[i])
            return 4 + i, i

        max_sig = [signal(f"max_rows{s}", 16) for s in range(2)]
        max_rows_in = {}
        max_t_free = [None, None]
        n_max = 0
        last_low = None

        def max_chunks(u):
            nonlocal n_max, last_low
            s = u % 3
            for qt in range(QT):
                pm = part_max[n_max % 2]
                reduced = None
                for r in range(BPT):
                    qb = qt * BPT + r
                    left = (r + 1) * P
                    per = max(1, TILE // left)
                    pieces = [([h], c, TILE) for h in range(GH) for c in range(qt)]
                    pieces += [(list(range(h, h + per)), qt, left) for h in range(0, GH, per)] if per in (1, 2, 4) \
                        else [([h], qt, left) for h in range(GH)]
                    for heads, c, width in pieces:
                        b, i = ring()
                        wait(pe, op_ready[u], masks_in, identb_in)
                        for n, h in enumerate(heads):
                            mm = pe.matmul(bank[b][:, n * width:(n + 1) * width],
                                           q_op[s][:, qt, h, r * P:(r + 1) * P],
                                           k_op[s][:, h, c * TILE:c * TILE + width], start=True, stop=True)
                            if c == qt:
                                mm = pe.matmul(bank[b][:, (n + 1) * width - P:(n + 1) * width], ident_b[:, :],
                                               masks[:, 1, :], start=False, stop=True, skip_group_check=True)
                        scored = by_pe.done(mm)
                        wait(dve, scored)
                        reduced = ring_free[i] = by_dve.done(dve.tensor_reduce(
                            pm[:, r, heads[0]:heads[0] + len(heads), c],
                            bank[b][:, 0:len(heads) * width].rearrange("p (h n) -> p h n", n=width), X, ALU.max))
                        yield
                wait(dve, reduced, last_low)
                m = n_max % 2
                n_max += 1
                negated = by_dve.done(dve.tensor_reduce(
                    neg_max[:, :].rearrange("p (h r) -> p r h", h=GH), pm[:, :, :, 0:qt + 1], X, ALU.max, negate=True))
                mp = max_parts[m]
                wait(dve, negated)
                high = by_dve.done(dve.tensor_copy(mp[:, 0, :], neg_max[:, :]))
                wait(dve, high)
                rested = by_dve.done(dve.tensor_tensor(max_rest[:, :], neg_max[:, :], mp[:, 0, :], ALU.subtract))
                wait(dve, rested)
                middle = by_dve.done(dve.tensor_copy(mp[:, 1, :], max_rest[:, :]))
                wait(dve, middle)
                low = last_low = by_dve.done(dve.tensor_tensor(mp[:, 2, :], max_rest[:, :], mp[:, 1, :], ALU.subtract))
                yield
                b, i = ring()
                wait(pe, low)
                n = 3 * GH * BPT
                turned = by_pe.done(pe.transpose(bank[b].bitcast(BF16)[0:n, 0:P],
                                                 mp[:, :, :].rearrange("p a n -> p (a n)"), ident_b[:, :]))
                wait(dve, turned, max_t_free[m])
                copied = ring_free[i] = by_dve.done(dve.tensor_copy(max_t[m][:, :], bank[b].bitcast(BF16)[0:n, 0:P]))
                wait(sp, copied)
                for a, row in enumerate(MAX_ROWS):
                    dst = q_op[s][row:row + 1, qt, :, :].rearrange("o h n -> o (h n)")
                    src = max_t[m][a * GH * BPT:(a + 1) * GH * BPT, :]
                    sent = max_sig[m].done(sp.dma_start(dst, src))
                max_rows_in[u, qt] = max_t_free[m] = sent
                yield

        pair_free = [bank_free[1], bank_free[3]]
        for b in (0, 2):
            wait(pe, bank_free[b])
        p_free = [v_ready] * PRING
        sums = bank[7]
        wait(dve, bank_free[7])
        sums_zeroed = by_dve.done(dve.memset(sums, 0.0))
        sums_free = sums_zeroed
        acc_free = [None, None]
        n_pair = n_p = n_acc = 0
        last_normalized = None
        normalized = {}

        def pairs_of(qt):
            out = [[(2 * i, 0, 0), (2 * i + 1, 0, TILE)] for i in range(2 * qt)]
            k = qt * BPT
            return out + [[(k, 0, 0), (k + 1, P, TILE)], [(k + 2, 2 * P, 2 * P), (k + 3, 3 * P, TILE)]]

        def pull(source, n):
            for _ in range(n):
                if next(source, StopIteration) is StopIteration:
                    return

        def products(job):
            nonlocal sums_free
            u, qt, pieces, tiles, exps, first, last = job
            b, g = units[u]
            if first:
                wait(pe, sums_free)
            for n, (kb, q0, at) in enumerate(pieces):
                wait(pe, *exps, v_ready)
                for h in range(GH):
                    mm = pe.matmul(sums[32 * h:32 * h + HD + 1, q0:TILE], v_aug[:, b * BPB + kb, g * GH + h, :],
                                   p_ring[tiles[h]][:, at:at + TILE - q0], start=(first and n == 0),
                                   stop=(last and n == 1), skip_group_check=True)
                done = by_pe.done(mm)
                if n == 1:
                    for i in tiles:
                        p_free[i] = done
                    if last:
                        finish_tile(u, qt, done)
                yield

        def finish_tile(u, qt, summed):
            nonlocal sums_free, n_acc, last_normalized
            b, g = units[u]
            a = n_acc % 2
            n_acc += 1
            wait(act, summed, acc_free[a])
            sums_free = copied = by_act.done(act.activation(acc_t[a][:, :], sums, ACTF.Copy))
            bk, i = ring()
            wait(pe, copied)
            for r in range(BPT):
                mm = pe.transpose(bank[bk][:, r * P:(r + 1) * P], acc_t[a][:, r * P:(r + 1) * P], ident[:, :])
            turned = acc_free[a] = by_pe.done(mm)
            wait(dve, turned, a_pe_done, last_normalized)
            view = bank[bk].rearrange("p (r h n) -> p r h n", r=BPT, h=GH)
            inverse = by_dve.done(dve.reciprocal(recip_l[:, :, :], view[:, :, :, HD]))
            wait(dve, inverse)
            blk = b * BPB + qt * BPT
            dst = tok[:, blk:blk + BPT, g * GH * HD:(g + 1) * GH * HD].rearrange("p r (h n) -> p r h n", h=GH)
            normalized[u, qt] = last_normalized = ring_free[i] = by_dve.done(dve.tensor_tensor(
                dst, view[:, :, :, 0:HD], recip_l[:, :, :].unsqueeze(3).broadcast_to([P, BPT, GH, HD]), ALU.mult))

        pull(max_chunks(0), 10 ** 6)
        for u in range(len(units)):
            s = u % 3
            ahead = max_chunks(u + 1) if u + 1 < len(units) else iter(())
            n_step = 0
            waiting = None
            for qt in range(QT):
                pairs = pairs_of(qt)
                for n_pairs, pieces in enumerate(pairs):
                    lo, hi = pieces[0][2], pieces[1][2] + TILE - pieces[1][1]
                    work = products(waiting) if waiting else iter(())
                    tiles, exps = [], []
                    for h in range(GH):
                        ps = n_pair % 2
                        n_pair += 1
                        wait(pe, pair_free[ps], max_rows_in[u, qt])
                        for kb, q0, at in pieces:
                            diagonal = kb >= qt * BPT
                            mm = pe.matmul(pair[ps][:, at:at + TILE - q0], k_op[s][:, h, kb * P:(kb + 1) * P],
                                           q_op[s][:, qt, h, q0:TILE],
                                           start=True, stop=True)
                            if diagonal:
                                mm = pe.matmul(pair[ps][:, at:at + P], ident_b[:, :], masks[:, 0, :],
                                               start=False, stop=True, skip_group_check=True)
                        scored = by_pe.done(mm)
                        pt = n_p % PRING
                        n_p += 1
                        wait(act, scored, p_free[pt])
                        pair_free[ps] = by_act.done(act.activation(p_ring[pt][:, lo:hi], pair[ps][:, lo:hi], ACTF.Exp))
                        tiles.append(pt)
                        exps.append(pair_free[ps])
                        pull(ahead, 2)
                        if h % 2:
                            pull(work, 1)
                    pull(work, 10)
                    waiting = (u, qt, pieces, tiles, exps, n_pairs == 0, n_pairs == len(pairs) - 1)
                    n_step += 1
            pull(products(waiting), 10)
            pull(ahead, 10 ** 6)
            op_free[s] = scored
            if u + 3 < len(units):
                load_operands(u + 3)
        attention_done = normalized[len(units) - 1, QT - 1]
        by_pe_last = acc_free[(n_acc - 1) % 2]

        small = sb("small", [P, 8 + 32 + 64 + 40])
        bias_rows = sb("bias_rows", [1, 2, D])
        columns = sb("columns", [P, 2 * EXPERTS * KC + EXPERTS * FC])
        cent_t = sb("cent_t", [P, KC, EXPERTS])
        tile_expert = sb("tile_expert", [1, 40], I32)
        position = sb("position", [P, BLOCKS], I32)
        scores1_stat = sb("scores1_stat", [DX, 3, H1])
        shift = sb("shift", [P, 2, BPT])
        bv_t = sb("bv_t", [DX, H1])

        W_BYTES = EXPERTS * KC * FF * 4
        w1 = carve(0, [EXPERTS, KC, FF])
        w2 = carve(W_BYTES, [EXPERTS, FC, D])
        EARLY = (AT_P - W_BYTES) * EXPERTS // W_BYTES
        wqk = carve(AT_P, [KC, 2 * H1 * DX])
        wfc = carve(AT_P + 8192, [H1, D], parts=DX)
        folded_fc = carve(AT_P + 16384, [H1, D], parts=DX)
        wv = carve(AT_P + 16384, [KC, H1 * DX])
        gram_k = carve(AT_P + 24576, [KC, H1 * DX])
        gram = carve(AT_P + 28672, [KC, D + 1])
        gram_row = carve(AT_P + 28672 + KC * (D + 1) * 4, [D + 1], parts=1)
        turned_x = [carve(AT_V + i * 4096, [KC, TILE]) for i in range(2)]
        ow = carve(AT_V + 8192, [KC, D])
        bv = carve(AT_V + 8192, [H1 * DX], parts=1)
        channel = [carve(AT_V + 10240 + b * 2048, [KC, D]) for b in range(BATCHES)]
        res = [carve(AT_V + 14336 + i * 4096, [BPT, D]) for i in range(2)]
        attn1 = carve(AT_V + 14336, [H1, DX], parts=DX)
        attn1_t = carve(AT_V + 16384, [H1, DX], parts=DX)
        wv_t = carve(AT_V + 22528, [H1, D], parts=DX)
        bqk = carve(AT_V + 30720, [2 * H1 * DX], parts=1)
        gram_k_row = acc_t[0][0:1, :]
        channel_row = [acc_t[1][0:1, b * D:(b + 1) * D] for b in range(BATCHES)]
        gamma = carve(AT_P, [D])
        beta = carve(AT_P + 1024, [D])

        later = attention_done
        wait(sp, later, by_pe_last)
        wait(act, later, by_pe_last)
        wait(pool, later)
        ow_in = load(ow[:, :, :], t["L0_attn_o_w"].rearrange("(c p) n -> p c n", p=P), "ow_in")
        res_sig = [signal(f"res_in{i}", 16) for i in range(2)]
        res_in = {}

        def load_x(g):
            res_in[g] = res_sig[g % 2].done(sp.dma_start(res[g % 2][:, :, :], x_view[:, g * BPT:(g + 1) * BPT, :]))

        load_x(0)
        load_x(1)
        rows_in = signal("rows_in", 16)
        rows_in.done(sp.dma_start(bias_rows[:, 0, :], t["L0_ffn_bias"].unsqueeze(0)))
        bias_in = rows_in.done(sp.dma_start(bias_rows[:, 1, :], t["L1_attn_b_fc"].unsqueeze(0)))
        ch_in = signal("channel_in", 16)
        w_qkv1 = t["L1_attn_w_qkv"].rearrange("(c p) n -> p c n", p=P)
        ch_in.done(act.dma_start(wqk[:, :, :], w_qkv1[:, :, 0:2 * H1 * DX]))
        ch_in.done(act.dma_start(wv[:, :, :], w_qkv1[:, :, 2 * H1 * DX:]))
        ch_in.done(act.dma_start(wfc[:, :, :], t["L1_attn_w_fc"].rearrange("(h e) n -> e h n", e=DX)))
        channel_in = ch_in.done(act.dma_start(bqk, t["L1_attn_b_qkv"][0:2 * H1 * DX].unsqueeze(0)))
        small_in = load(small[:, :], t["c_small"], "small_in", act)
        w_sig = signal("experts_in", 16)
        for e in range(EXPERTS):
            w_sig.done(act.dma_start(w1[:, e, :, :], t["L1_ffn_w1"][e].rearrange("(c p) f -> p c f", p=P)))
        w2_view = t["L1_ffn_w2"].rearrange("e (c p) n -> p e c n", p=P)
        for e in range(EARLY):
            w_sig.done(act.dma_start(w2[:, e, :, :], w2_view[:, e, :, :]))

        turn_free = [None, None]
        n_turn = n_mult = n_norm = 0
        for b in range(8):
            bank_free[b] = attention_done

        def turn(g, ready):
            nonlocal n_turn
            slot = n_turn % 2
            n_turn += 1
            wait(pe, ready)
            for c in range(KC):
                b = 2 * slot + c
                wait(pe, bank_free[b])
                for r in range(BPT):
                    mm = pe.transpose(bank[b][:, r * P:(r + 1) * P], tok[:, g * BPT + r, c * P:(c + 1) * P], ident[:, :])
                turned = by_pe.done(mm)
                engine, by = ((act, by_act), (dve, by_dve))[c]
                wait(engine, turned, turn_free[slot])
                copy = act.activation(turned_x[slot][:, c, :], bank[b], ACTF.Copy) if c == 0 else \
                    dve.tensor_copy(turned_x[slot][:, c, :], bank[b])
                bank_free[b] = by.done(copy)
            return slot, bank_free[2 * slot], bank_free[2 * slot + 1]

        def multiply(turned, weight, row, *ready):
            nonlocal n_mult
            slot, *copied = turned
            b0 = 4 + 2 * (n_mult % 2)
            n_mult += 1
            wait(pe, *copied, *ready)
            out_marks = []
            for half in range(2):
                wait(pe, bank_free[b0 + half])
                for j in range(2):
                    r = 2 * half + j
                    dst = bank[b0 + half][:, j * D:(j + 1) * D]
                    for c in range(KC):
                        mm = pe.matmul(dst, turned_x[slot][:, c, r * P:(r + 1) * P], weight[:, c, :],
                                       start=(c == 0), stop=(c == KC - 1 and row is None))
                    if row is not None:
                        mm = pe.matmul(dst, ones[0:1, :], row, start=False, stop=True)
                out_marks.append(by_pe.done(mm))
            turn_free[slot] = out_marks[-1]
            return b0, out_marks

        def block_of(b0, r):
            return bank[b0 + r // 2][:, (r % 2) * D:(r % 2 + 1) * D]

        def layer_norm(srcs, dsts, eps, ready):
            nonlocal n_norm
            m = n_norm % 2
            n_norm += 1
            n = len(srcs)
            for r in range(n):
                wait(dve, ready[r])
                stat = by_dve.done(dve.bn_stats(stats[:, m, r, :], srcs[r]))
            wait(dve, stat)
            for r in range(n):
                moment = by_dve.done(dve.bn_aggr(moments[:, m, r, :], stats[:, m, r, :]))
            wait(act, moment, eps_set)
            rooted = by_act.done(act.activation(std[:, m, 0:n], moments[:, m, 0:n, 1], ACTF.Sqrt,
                                                bias=eps_col[:, eps:eps + 1]))
            wait(dve, rooted)
            inverse = by_dve.done(dve.reciprocal(rstd[:, m, 0:n], std[:, m, 0:n]))
            wait(dve, inverse)
            shifted = by_dve.done(dve.scalar_tensor_tensor(shift[:, m, 0:n], moments[:, m, 0:n, 0], -1.0,
                                                           rstd[:, m, 0:n], ALU.mult, ALU.mult))
            wait(act, shifted)
            marks = []
            for r in range(n):
                if r >= 2:
                    marks.append(by_act.done(act.activation(dsts[r], srcs[r], ACTF.Identity,
                                                            bias=shift[:, m, r:r + 1], scale=rstd[:, m, r:r + 1])))
                else:
                    marks.append(by_dve.done(dve.tensor_scalar(dsts[r], srcs[r], moments[:, m, r, 0:1],
                                                               rstd[:, m, r:r + 1], ALU.subtract, ALU.mult)))
            return marks

        def blocks(g):
            return [tok[:, g * BPT + r, 0:D] for r in range(BPT)]

        def project(g, b0, summed):
            marks = []
            for half in range(2):
                dst = tok[:, g * BPT + 2 * half:g * BPT + 2 * half + 2, 0:D]
                wait(dve, summed[half], res_in[g])
                bank_free[b0 + half] = added = by_dve.done(dve.tensor_tensor(
                    dst, bank[b0 + half].rearrange("p (j n) -> p j n", j=2), res[g % 2][:, 2 * half:2 * half + 2, :],
                    ALU.add))
                marks += [added, added]
            if g + 2 < TILES:
                wait(sp, added)
                load_x(g + 2)
            wait(act, added)
            return layer_norm(blocks(g), blocks(g), 0, marks)

        def spectral_norm(g, b0, summed):
            marks = layer_norm([block_of(b0, r) for r in range(BPT)], blocks(g), 0,
                               [summed[r // 2] for r in range(BPT)])
            bank_free[b0], bank_free[b0 + 1] = Both(marks[0], marks[1]), Both(marks[2], marks[3])
            return marks

        x1_done, x2_done = {}, {}
        for g in range(TILES + 1):
            if g < TILES:
                projected = multiply(turn(g, attention_done), ow, None, ow_in)
            if g >= 1:
                turned = turn(g - 1, Both(*x1_done[g - 1]))
            if g < TILES:
                x1_done[g] = project(g, *projected)
            if g >= 1:
                x2_done[g - 1] = spectral_norm(g - 1, *multiply(turned, spectral, bias_rows[:, 0, :], bias_in,
                                                                spectral_ready))
        x2_all = [m for g in range(TILES) for m in x2_done[g]]

        stage_in = signal("stage_in", 16)
        staged = res[1][:, :, :].rearrange("p a n -> p (a n)")
        wait(sp, *x1_done[TILES - 1])
        stage_in.done(sp.dma_start(staged[0:EXPERTS * KC, 0:P], t["L1_ffn_ln_g"].rearrange("e (c p) -> (e c) p", p=P)))
        stage_in.done(sp.dma_start(staged[0:EXPERTS * KC, P:2 * P],
                                   t["L1_ffn_ln_b"].rearrange("e (c p) -> (e c) p", p=P)))
        stage_in.done(sp.dma_start(staged[0:EXPERTS * FC, 2 * P:3 * P],
                                   t["L1_ffn_b1"].rearrange("e (c p) -> (e c) p", p=P)))
        stage_in.done(sp.dma_start(staged[0:EXPERTS, 3 * P:5 * P], t["L1_ffn_centroids"]))
        params_in = stage_in.done(sp.dma_start(bv, t["L1_attn_b_qkv"][2 * H1 * DX:].unsqueeze(0)))
        wait(pe, params_in, channel_in, bank_free[0], bank_free[1], bank_free[2], bank_free[3])
        n_g, n_f = EXPERTS * KC, EXPERTS * FC
        pe.transpose(bank[0][:, 0:n_g], staged[0:n_g, 0:P], ident[0:n_g, 0:n_g])
        pe.transpose(bank[0][:, n_g:2 * n_g], staged[0:n_g, P:2 * P], ident[0:n_g, 0:n_g])
        pe.transpose(bank[0][:, 2 * n_g:2 * n_g + n_f], staged[0:n_f, 2 * P:3 * P], ident[0:n_f, 0:n_f])
        for c in range(KC):
            o = 2 * n_g + n_f + c * EXPERTS
            mm = pe.transpose(bank[0][:, o:o + EXPERTS], staged[0:EXPERTS, (3 + c) * P:(4 + c) * P],
                              ident[0:EXPERTS, 0:EXPERTS])
        turned = by_pe.done(mm)
        wait(dve, turned)
        columns_set = by_dve.done(dve.tensor_copy(columns[:, :], bank[0][:, 0:2 * n_g + n_f]))
        cent_set = bank_free[0] = by_dve.done(dve.tensor_copy(
            cent_t[:, :, :].rearrange("p c e -> p (c e)"), bank[0][:, 2 * n_g + n_f:2 * n_g + n_f + KC * EXPERTS]))
        wvt_marks = []
        for h in range(H1):
            b = 1 + h // 2 % 3
            if h % 2 == 0:
                wait(pe, bank_free[b])
            for c in range(KC):
                mm = pe.transpose(bank[b][0:DX, (h % 2) * D + c * P:(h % 2) * D + (c + 1) * P],
                                  wv[:, c, h * DX:(h + 1) * DX], ident[:, :])
            if h % 2:
                turned = by_pe.done(mm)
                wait(act, turned)
                bank_free[b] = by_act.done(act.activation(wv_t[:, h - 1:h + 1, :].rearrange("p h n -> p (h n)"),
                                                          bank[b][0:DX, :], ACTF.Copy))
                wvt_marks.append(bank_free[b])
        wait(pe, bank_free[0])
        for h in range(H1):
            mm = pe.matmul(bank[0][0:DX, h:h + 1], bv[:, h * DX:(h + 1) * DX], ones[0:1, 0:1], start=True, stop=True)
        turned = by_pe.done(mm)
        wait(dve, turned)
        bv_set = bank_free[0] = by_dve.done(dve.tensor_copy(bv_t[:, :], bank[0][0:DX, 0:H1]))
        length_set = by_dve.done(dve.memset(gram_row[:, D:D + 1], float(LENGTH)))

        for batch in range(BATCHES):
            wait(pe, *x2_all, *bank_free)
            for i in range(BPB):
                blk = batch * BPB + i
                for m in range(KC):
                    lhs = tok[:, blk, m * P:(m + 1) * P]
                    pe.matmul(bank[m][:, 0:D], lhs, tok[:, blk, 0:D], start=(i == 0), stop=(i == BPB - 1))
                    mm = pe.matmul(bank[2 + m][:, 0:1], lhs, ones[:, 0:1], start=(i == 0), stop=(i == BPB - 1))
            summed = by_pe.done(mm)
            wait(dve, summed)
            wait(act, summed)
            by_dve.done(dve.tensor_copy(gram[:, 0, 0:D], bank[0][:, 0:D]))
            by_dve.done(dve.tensor_copy(gram[:, 0, D:D + 1], bank[2][:, 0:1]))
            gram0 = by_dve.done(dve.tensor_copy(gram[:, 1, D:D + 1], bank[3][:, 0:1]))
            gram1 = by_act.done(act.activation(gram[:, 1, 0:D], bank[1][:, 0:D], ACTF.Copy))
            wait(pe, gram0, gram1)
            for m in range(KC):
                mm = pe.matmul(bank[4][0:1, m * P:(m + 1) * P], gram[:, m, D:D + 1], ident[:, :], start=True, stop=True)
            rowed = by_pe.done(mm)
            wait(dve, rowed)
            row_set = by_dve.done(dve.tensor_copy(gram_row[:, 0:D], bank[4][0:1, 0:D]))
            wait(pe, row_set, length_set)
            hk = slice(H1 * DX, 2 * H1 * DX)
            for m in range(KC + 1):
                rows = P if m < KC else 1
                cols = slice(m * P, m * P + rows)
                for c in range(KC):
                    pe.matmul(bank[5 + m][0:rows, :], gram[:, c, cols], wqk[:, c, hk], start=(c == 0), stop=False)
                mm = pe.matmul(bank[5 + m][0:rows, :], gram_row[:, cols], bqk[:, hk], start=False, stop=True)
            multiplied = by_pe.done(mm)
            wait(dve, multiplied)
            wait(act, multiplied)
            k0 = by_dve.done(dve.tensor_copy(gram_k[:, 0, :], bank[5]))
            k1 = by_act.done(act.activation(gram_k[:, 1, :], bank[6], ACTF.Copy))
            k2 = by_dve.done(dve.tensor_copy(gram_k_row, bank[7][0:1, :]))
            wait(pe, k0, k1, k2)
            for h in range(H1):
                cols = slice(h * DX, (h + 1) * DX)
                for c in range(KC):
                    pe.matmul(bank[0][0:DX, cols], wqk[:, c, cols], gram_k[:, c, cols], start=(c == 0), stop=False)
                mm = pe.matmul(bank[0][0:DX, cols], bqk[:, cols], gram_k_row[:, cols], start=False, stop=True)
            scored = by_pe.done(mm)
            view = bank[0][0:DX, :].rearrange("p (h n) -> p h n", h=H1)
            wait(dve, scored)
            most = by_dve.done(dve.tensor_reduce(scores1_stat[:, 0, :], view, X, ALU.max))
            wait(dve, most)
            below = by_dve.done(dve.tensor_tensor(attn1[:, :, :], view, scores1_stat[:, 0, :].unsqueeze(2)
                                                  .broadcast_to([DX, H1, DX]), ALU.subtract))
            wait(act, below)
            exped = by_act.done(act.activation(attn1[:, :, :], attn1[:, :, :], ACTF.Exp, scale=1.0 / DX ** 0.5))
            wait(dve, exped)
            total = by_dve.done(dve.tensor_reduce(scores1_stat[:, 1, :], attn1[:, :, :], X, ALU.add))
            wait(dve, total)
            inverse = by_dve.done(dve.reciprocal(scores1_stat[:, 2, :], scores1_stat[:, 1, :]))
            wait(dve, inverse)
            attended = by_dve.done(dve.tensor_tensor(attn1[:, :, :], attn1[:, :, :], scores1_stat[:, 2, :].unsqueeze(2)
                                                     .broadcast_to([DX, H1, DX]), ALU.mult))
            wait(pe, attended)
            for h in range(H1):
                mm = pe.transpose(bank[1][0:DX, h * DX:(h + 1) * DX], attn1[:, h, :], ident[0:DX, 0:DX])
            turned = by_pe.done(mm)
            wait(dve, turned)
            attn_t_set = by_dve.done(dve.tensor_copy(attn1_t[:, :, :].rearrange("p h n -> p (h n)"), bank[1][0:DX, :]))
            wait(pe, attn_t_set)
            fc_marks = list(wvt_marks)
            for h in range(H1):
                b = (2, 3, 5, 6)[h // 2]
                mm = pe.matmul(bank[b][0:DX, (h % 2) * D:(h % 2 + 1) * D], attn1_t[:, h, :], wfc[:, h, :],
                               start=True, stop=True)
                if h % 2:
                    multiplied = by_pe.done(mm)
                    wait(act, multiplied)
                    fc_marks.append(by_act.done(act.activation(
                        folded_fc[:, h - 1:h + 1, :].rearrange("p h n -> p (h n)"), bank[b][0:DX, :], ACTF.Copy)))
            wait(pe, *fc_marks, bv_set)
            for m in range(KC + 1):
                rows = P if m < KC else 1
                b = (0, 1, 4)[m]
                for h in range(H1):
                    lhs = wv_t[:, h, m * P:(m + 1) * P] if m < KC else bv_t[:, h:h + 1]
                    mm = pe.matmul(bank[b][0:rows, 0:D], lhs, folded_fc[:, h, :], start=(h == 0), stop=(h == H1 - 1))
            folded = by_pe.done(mm)
            wait(dve, folded)
            for m in range(KC):
                copied = by_dve.done(dve.tensor_copy(channel[batch][:, m, :], bank[m][:, 0:D]))
            row_added = by_dve.done(dve.tensor_tensor(channel_row[batch], bank[4][0:1, 0:D], bias_rows[:, 1, :], ALU.add))
            wait(dve, copied)
            for m in range(KC):
                channel_ready = by_dve.done(dve.tensor_tensor(channel[batch][:, m, m * P:(m + 1) * P],
                                                              channel[batch][:, m, m * P:(m + 1) * P], ident[:, :],
                                                              ALU.add))
            for b in range(8):
                bank_free[b] = channel_ready

        affinity = carve(AT_P + 2048, [BLOCKS, EXPERTS])
        wait(sp, channel_ready)
        ln_sig = signal("ln1_in", 16)
        ln_sig.done(sp.dma_start(gamma, t["L1_attn_gamma"].unsqueeze(0).broadcast_to([P, D])))
        ln1_in = ln_sig.done(sp.dma_start(beta, t["L1_attn_beta"].unsqueeze(0).broadcast_to([P, D])))
        before = carve(AT_P + 2048 + 1024, [P])
        before_in = load(before, t["c_before"], "before_in")
        res_free = [channel_ready, channel_ready]

        def channel_norm(g, b0, summed):
            y = res[g % 2]
            ready = [summed[r // 2] for r in range(BPT)]
            wait(dve, res_free[g % 2])
            wait(act, res_free[g % 2])
            marks = layer_norm([block_of(b0, r) for r in range(BPT)], [y[:, r, :] for r in range(BPT)], 1, ready)
            bank_free[b0], bank_free[b0 + 1] = Both(marks[0], marks[1]), Both(marks[2], marks[3])
            wait(pool, *marks, ln1_in)
            scaled = by_pool.done(pool.tensor_tensor(y[:, :, :], y[:, :, :], gamma.unsqueeze(1)
                                                     .broadcast_to([P, BPT, D]), ALU.mult))
            wait(pool, scaled)
            moved = by_pool.done(pool.tensor_tensor(y[:, :, :], y[:, :, :], beta.unsqueeze(1)
                                                    .broadcast_to([P, BPT, D]), ALU.add))
            return moved

        def second_norm(g, moved):
            wait(dve, moved)
            dst = tok[:, g * BPT:(g + 1) * BPT, 0:D]
            res_free[g % 2] = added = by_dve.done(dve.tensor_tensor(dst, dst, res[g % 2][:, :, :], ALU.add))
            wait(act, added)
            return layer_norm(blocks(g), blocks(g), 0, [added] * BPT)

        def affinities(g, turned):
            nonlocal n_mult
            slot, *copied = turned
            b = 4 + 2 * (n_mult % 2)
            n_mult += 1
            wait(pe, *copied, bank_free[b], cent_set)
            for r in range(BPT):
                for c in range(KC):
                    mm = pe.matmul(bank[b][:, r * EXPERTS:(r + 1) * EXPERTS], turned_x[slot][:, c, r * P:(r + 1) * P],
                                   cent_t[:, c, :], start=(c == 0), stop=(c == KC - 1))
            turn_free[slot] = multiplied = by_pe.done(mm)
            wait(dve, multiplied)
            bank_free[b] = by_dve.done(dve.tensor_copy(
                affinity[:, g * BPT:(g + 1) * BPT, :].rearrange("p b e -> p (b e)"), bank[b][:, 0:BPT * EXPERTS]))
            return bank_free[b]

        moved_at, x3_done = {}, {}
        for g in range(TILES + 2):
            if g < TILES:
                batch = g * TILE // LENGTH
                multiplied = multiply(turn(g, None), channel[batch], channel_row[batch], channel_ready)
            if g >= 2:
                turned = turn(g - 2, Both(*x3_done[g - 2]))
            if g < TILES:
                moved_at[g] = channel_norm(g, *multiplied)
            if 1 <= g <= TILES:
                x3_done[g - 1] = second_norm(g - 1, moved_at[g - 1])
            if g >= 2:
                affine = affinities(g - 2, turned)
        x3_all = [m for g in range(TILES) for m in x3_done[g]]

        rank, k128, earlier, numbers = small[:, 0:8], small[:, 8:40], small[:, 40:104], small[:, 104:144]
        AT_E = AT_V + 3096 + 2048 + 2048
        flat = [carve(AT_E + i * 1024, [BLOCKS, EXPERTS]) for i in range(6)]
        best, order, tiles_of, first_tile = (carve(AT_E + 6144 + i * 128, [n]) for i, n in
                                             enumerate((BLOCKS, BLOCKS, EXPERTS, EXPERTS)))
        over = carve(AT_E + 6656, [40, EXPERTS])
        tile_f = carve(AT_E + 6656 + 1280, [40])
        used = carve(AT_E + 6656 + 1440, [EXPERTS, 32])
        last = None

        def step(ins):
            nonlocal last
            last = by_dve.done(ins)
            wait(dve, last)
            return last

        def wide(ap, shape, axis):
            return ap.unsqueeze(axis).broadcast_to(shape)

        all_b = [P, BLOCKS, EXPERTS]
        wait(dve, affine, small_in, turn_free[0], turn_free[1], *x3_all)
        step(dve.tensor_reduce(best, affinity[:, :, :], X, ALU.max))
        best_set = last
        step(dve.tensor_tensor(flat[0][:, :, :], affinity[:, :, :], wide(best, all_b, 2), ALU.is_equal))
        step(dve.tensor_tensor(flat[0][:, :, :], flat[0][:, :, :], wide(rank, all_b, 1), ALU.mult))
        step(dve.tensor_reduce(order, flat[0][:, :, :], X, ALU.max))
        onehot = flat[1]
        step(dve.tensor_tensor(onehot[:, :, :], wide(rank, all_b, 1), wide(order, all_b, 2), ALU.is_equal))
        onehot_set = last
        wait(act, best_set)
        exped = by_act.done(act.activation(flat[5][:, 0:4, :].rearrange("p a e -> p (a e)"), best, ACTF.Exp, scale=-1.0))
        wait(dve, exped)
        step(dve.tensor_scalar(flat[5][:, 0:4, :], flat[5][:, 0:4, :], 1.0, 2.0, ALU.add, ALU.mult))
        step(dve.reciprocal(tok[:, :, D], flat[5][:, 0:4, :].rearrange("p a e -> p (a e)")))
        gate_set = last
        wait(pool, *x3_all)
        numbered = by_pool.done(pool.iota(tok[:, :, D + 1].bitcast(I32), pattern=[[P, BLOCKS]], base=0,
                                          channel_multiplier=1))
        wait(pe, onehot_set, before_in, bank_free[0], bank_free[1])
        hot = onehot[:, :, :].rearrange("p b e -> p (b e)")
        pe.matmul(bank[0][:, 0:BLOCKS * EXPERTS], before, hot, start=True, stop=True)
        counted = by_pe.done(pe.matmul(bank[1][:, 0:BLOCKS * EXPERTS], ones[:, :], hot, start=True, stop=True))
        wait(dve, counted)
        sums_a, sums_b = flat[2], flat[3]
        step(dve.tensor_copy(sums_a[:, :, :].rearrange("p b e -> p (b e)"), bank[1][:, 0:BLOCKS * EXPERTS]))
        by = 1
        while by < BLOCKS:
            step(dve.tensor_copy(sums_b[:, 0:by, :], sums_a[:, 0:by, :]))
            step(dve.tensor_tensor(sums_b[:, by:, :], sums_a[:, by:, :], sums_a[:, :BLOCKS - by, :], ALU.add))
            sums_a, sums_b = sums_b, sums_a
            by *= 2
        shape = [P, EXPERTS, 32]
        step(dve.tensor_tensor(used[:, :, :], wide(sums_a[:, BLOCKS - 1, :], shape, 2), wide(k128, shape, 1), ALU.is_gt))
        step(dve.tensor_reduce(tiles_of, used[:, :, :], X, ALU.add))
        shape = [P, EXPERTS, EXPERTS]
        cross = sums_b[:, 0:EXPERTS, :]
        step(dve.tensor_tensor(cross, wide(tiles_of, shape, 1), earlier.rearrange("p (a b) -> p a b", a=EXPERTS),
                               ALU.mult))
        step(dve.tensor_reduce(first_tile, cross, X, ALU.add))
        step(dve.tensor_tensor(tiles_of, tiles_of, first_tile, ALU.add))
        shape = [P, 40, EXPERTS]
        step(dve.tensor_tensor(over[:, :, :], wide(tiles_of, shape, 1), wide(numbers, shape, 2), ALU.is_le))
        step(dve.tensor_reduce(tile_f, over[:, :, :], X, ALU.add))
        expert_set = step(dve.tensor_scalar(tile_expert[:, :], tile_f[0:1, :], float(EXPERTS - 1), None, ALU.min))
        step(dve.tensor_scalar(first_tile, first_tile, float(P), None, ALU.mult))
        place = flat[4]
        step(dve.tensor_copy(place[:, 0, :], first_tile))
        step(dve.tensor_tensor(place[:, 1:, :], sums_a[:, :BLOCKS - 1, :], wide(first_tile, [P, BLOCKS - 1, EXPERTS], 1),
                               ALU.add))
        step(dve.tensor_tensor(place[:, :, :], bank[0][:, 0:BLOCKS * EXPERTS].rearrange("p (b e) -> p b e", e=EXPERTS),
                               place[:, :, :], ALU.add))
        step(dve.tensor_tensor(place[:, :, :], place[:, :, :], onehot[:, :, :], ALU.mult))
        step(dve.tensor_reduce(best, place[:, :, :], X, ALU.add))
        placed = step(dve.tensor_copy(position[:, :], best))
        wait(act, placed, before_in)
        for e in range(EARLY, EXPERTS):
            experts_in = w_sig.done(act.dma_start(w2[:, e, :, :], w2_view[:, e, :, :]))
        b2_row = carve(AT_V + 34816 - 8192, [EXPERTS, D], parts=1)
        b2_in = load(b2_row, t["L1_ffn_b2"].unsqueeze(0), "b2_in", act)
        wait(pool, placed, gate_set, numbered, padded)
        scatter = signal("scatter", 16)
        for blk in range(BLOCKS):
            scattered = scatter.done(pool.indirect_dma_start(
                routed_dram, bass.IndirectOffsetOnAxis(ap=position[:, blk:blk + 1], axis=0), tok[:, blk, :], None))

        at = AT_V
        xs = [carve(at + i * ROW * 4, [ROW]) for i in range(3)]
        at += 3 * ROW * 4
        xn = [carve(at + i * 1024, [D]) for i in range(2)]
        at += 2048
        xln_t = [carve(at + i * 1024, [KC, P]) for i in range(2)]
        at += 2048
        hidden = carve(at, [FF])
        at += 4096
        hidden_t = [carve(at + i * 4096, [FC, P]) for i in range(2)]
        at += 8192
        mixed = [carve(at + i * 1024, [D]) for i in range(2)]
        at += 2048
        final = [carve(at + i * 1024, [D]) for i in range(2)]
        at += 2048
        assert at <= AT_V + VBYTES - 8192
        out_rows = out.rearrange("b n d -> (b n) d")
        xs_sig = [signal(f"rows_in{i}", 16) for i in range(3)]
        xs_in, turned_at, hid_at, hidt_at = {}, {}, {}, {}
        xs_free, xln_free, hid_free, hidt_free, final_free = [placed] * 3, [None] * 2, None, [None] * 2, [None] * 2
        for b in range(8):
            bank_free[b] = placed
        out_sig = [signal(f"out{i}", 16) for i in range(2)]
        regs = {}

        def expert(engine, name, i):
            if (name, i) not in regs:
                wait(engine, expert_set)
                regs[name, i] = engine.value_load(tile_expert[0:1, i:i + 1], min_val=0, max_val=EXPERTS - 1)
            return regs[name, i]

        def fetch(i):
            wait(sp, scattered, xs_free[i % 3])
            xs_in[i] = xs_sig[i % 3].done(sp.dma_start(xs[i % 3], routed_dram[i * P:(i + 1) * P, :]))

        def normalise(i):
            s = i % 2
            marks = layer_norm([xs[i % 3][:, 0:D]], [xn[s]], 0, [xs_in[i]])
            b = s
            wait(pe, bank_free[b], *marks)
            for c in range(KC):
                mm = pe.transpose(bank[b][:, c * P:(c + 1) * P], xn[s][:, c * P:(c + 1) * P], ident[:, :])
            turned = by_pe.done(mm)
            e = expert(dve, "dve", i)
            wait(dve, turned, xln_free[s])
            cols_g = columns[:, 0:n_g].rearrange("p (e c) -> p c e", c=KC)
            cols_b = columns[:, n_g:2 * n_g].rearrange("p (e c) -> p c e", c=KC)
            for c in range(KC):
                bank_free[b] = by_dve.done(dve.tensor_scalar(
                    xln_t[s][:, c, :], bank[b][:, c * P:(c + 1) * P], cols_g[:, c, bass.ds(e, 1)],
                    cols_b[:, c, bass.ds(e, 1)], ALU.mult, ALU.add))
            turned_at[i] = bank_free[b]

        def hide(i):
            nonlocal hid_free
            s = i % 2
            e = expert(pe, "pe", i)
            wait(pe, turned_at[i], experts_in)
            copies = []
            for half in range(2):
                b = 2 + half
                wait(pe, bank_free[b])
                for c in range(KC):
                    w = w1[:, bass.ds(e, 1), c, half * TILE:(half + 1) * TILE].rearrange("p a n -> p (a n)")
                    mm = pe.matmul(bank[b], xln_t[s][:, c, :], w, start=(c == 0), stop=(c == KC - 1))
                multiplied = by_pe.done(mm)
                xln_free[s] = multiplied
                dst = hidden[:, half * TILE:(half + 1) * TILE]
                if half:
                    wait(dve, multiplied, hid_free)
                    bank_free[b] = by_dve.done(dve.tensor_copy(dst, bank[b]))
                else:
                    wait(act, multiplied, hid_free)
                    bank_free[b] = by_act.done(act.activation(dst, bank[b], ACTF.Copy))
                copies.append(bank_free[b])
            hid_at[i] = copies

        def turn_hidden(i):
            nonlocal hid_free
            s = i % 2
            marks = []
            col = columns[:, 2 * n_g:2 * n_g + n_f].rearrange("p (e c) -> p c e", c=FC)
            for half in range(2):
                b = 4 + half
                wait(pe, bank_free[b], *hid_at[i])
                for j in range(FC // 2):
                    f = half * FC // 2 + j
                    mm = pe.transpose(bank[b][:, j * P:(j + 1) * P], hidden[:, f * P:(f + 1) * P], ident[:, :])
                turned = hid_free = by_pe.done(mm)
                for j in range(FC // 2):
                    f = half * FC // 2 + j
                    src = bank[b][:, j * P:(j + 1) * P]
                    if half:
                        e = expert(dve, "dve", i)
                        wait(dve, turned, hidt_free[s])
                        m = by_dve.done(dve.tensor_scalar(hidden_t[s][:, f, :], src, col[:, f, bass.ds(e, 1)], 0.0,
                                                          ALU.add, ALU.max))
                    else:
                        e = expert(act, "act", i)
                        wait(act, turned, hidt_free[s])
                        m = by_act.done(act.activation(hidden_t[s][:, f, :], src, ACTF.Relu,
                                                       bias=col[:, f, bass.ds(e, 1)]))
                bank_free[b] = m
                marks.append(m)
            hidt_at[i] = marks

        def unhide(i):
            s = i % 2
            b = 6 + s
            e = expert(pe, "pe", i)
            wait(pe, bank_free[b], *hidt_at[i], b2_in)
            for f in range(FC):
                pe.matmul(bank[b][:, 0:D], hidden_t[s][:, f, :],
                          w2[:, bass.ds(e, 1), f, :].rearrange("p a n -> p (a n)"), start=(f == 0), stop=False)
            mm = pe.matmul(bank[b][:, 0:D], ones[0:1, :], b2_row[:, bass.ds(e, 1), :].rearrange("p a n -> p (a n)"),
                           start=False, stop=True)
            hidt_free[s] = summed = by_pe.done(mm)
            return summed

        def finish(i, summed):
            s = i % 2
            row = xs[i % 3]
            wait(dve, summed)
            added = bank_free[6 + s] = by_dve.done(dve.scalar_tensor_tensor(
                mixed[s], bank[6 + s][:, 0:D], row[:, D:D + 1], row[:, 0:D], ALU.mult, ALU.add))
            wait(dve, final_free[s])
            marks = layer_norm([mixed[s]], [final[s]], 2, [added])
            wait(pool, *marks)
            final_free[s] = xs_free[i % 3] = out_sig[s].done(pool.indirect_dma_start(
                out_rows, bass.IndirectOffsetOnAxis(ap=row[:, D + 1:D + 2].bitcast(I32), axis=0), final[s], None,
                bounds_check=TOKENS - 1, oob_is_err=False))

        for i in range(3):
            fetch(i)
        normalise(0)
        hide(0)
        normalise(1)
        for i in range(SLOT_TILES):
            turn_hidden(i)
            if i + 1 < SLOT_TILES:
                hide(i + 1)
            summed = unhide(i)
            if i + 2 < SLOT_TILES:
                normalise(i + 2)
            finish(i, summed)
            if i + 3 < SLOT_TILES:
                fetch(i + 3)
        wait(pool, *final_free)
        wait(sp, *final_free)


def bf16_bits(a):
    return (np.ascontiguousarray(a, np.float32).view(np.uint32) >> 16).astype(np.uint16)


def bf16_parts(a):
    out = []
    for _ in range(3):
        part = (np.asarray(a, np.float32).view(np.uint32) & np.uint32(0xFFFF0000)).view(np.float32)
        out.append(part)
        a = (np.asarray(a, np.float32) - part).astype(np.float32)
    return out


def constants():
    i = np.arange(P)
    slopes = np.array([(2.0 ** (-8.0 / HEADS)) ** (h + 1) for h in range(HEADS)], np.float32)
    position = np.arange(LENGTH)
    key_rows = np.zeros((EXTRA, LENGTH), np.float32)
    query_rows = np.zeros((EXTRA, HEADS, LENGTH), np.float32)
    for n, part in enumerate(bf16_parts(slopes)):
        key_rows[2 * n] = position // P * P
        query_rows[2 * n] = part[:, None]
        key_rows[2 * n + 1] = 1.0
        key_rows[6 + n] = position % P
        query_rows[6 + n] = part[:, None]
    angle = 2 * np.pi * (np.outer(np.arange(D), np.arange(D)) % D) / D
    small = np.zeros((P, 8 + 32 + 64 + 40), np.float32)
    small[:, 0:8] = 8 - np.arange(8)
    small[:, 8:40] = P * np.arange(32)
    small[:, 40:104] = (np.arange(8)[None, :] < np.arange(8)[:, None]).reshape(-1)
    small[:, 104:144] = np.arange(40)
    return {
        "c_ident": np.eye(P, dtype=np.float32),
        "c_ident_b": bf16_bits(np.eye(P)),
        "c_masks": bf16_bits(np.stack([np.where(i[:, None] > i[None, :], MASKED, 0.0),
                                       np.where(i[None, :] > i[:, None], MASKED, 0.0)])),
        "c_key_rows": bf16_bits(key_rows), "c_query_rows": bf16_bits(query_rows.reshape(EXTRA, GROUPS, GH, QT, TILE).transpose(0, 1, 3, 2, 4)),
        "c_cos": np.cos(angle).astype(np.float32), "c_sin": np.sin(angle).astype(np.float32),
        "c_nsin": (-np.sin(angle)).astype(np.float32),
        "c_before": (i[:, None] < i[None, :]).astype(np.float32), "c_small": small,
    }


def kernel(**inputs):
    import numpy as _np
    import concourse.bacc as _bacc
    from concourse.bass_utils import run_bass_kernel_spmd as _run

    nc = _bacc.Bacc("TRN2", target_bir_lowering=False, num_devices=1)
    arrays, t = {}, {}
    for name, a in {**inputs, **constants()}.items():
        arrays[f"in_{name}"] = a = _np.ascontiguousarray(a)
        t[name] = nc.dram_tensor(f"in_{name}", a.shape, mybir.dt.from_np(a.dtype), kind="ExternalInput").ap()
    out = nc.dram_tensor("out", (BATCHES, LENGTH, D), F32, kind="ExternalOutput").ap()
    program(nc, t, out)
    r = _run(nc, [arrays], core_ids=[0])
    return r.results[0]["out"]
```

```python
from contextlib import ExitStack
import functools

import numpy as np
import concourse.bass as bass
from concourse import mybir

F32 = mybir.dt.float32
BF16 = mybir.dt.bfloat16
I32 = mybir.dt.int32
ALU = mybir.AluOpType
ACTF = mybir.ActivationFunctionType
X = mybir.AxisListType.X

P = 128
BATCHES, LENGTH, D = 2, 2048, 256
TOKENS = BATCHES * LENGTH
KC = D // P
BLOCKS = TOKENS // P
TILE = 512
BPT = TILE // P
TILES = TOKENS // TILE
HEADS, HD = 16, 16
GH = 4
GROUPS = HEADS // GH
BPB = LENGTH // P
QT = LENGTH // TILE
EXTRA = 32
TERMS = [(0, 0), (0, 1), (0, 2), (1, 0), (1, 1), (2, 0)]
MAX_ROWS = (1, 3, 5)
H1, DX = 8, 64
EXPERTS, FF = 8, 1024
FC = FF // P
SLOT_TILES = BLOCKS + EXPERTS - 1
ROW = D + 2
MASKED = -1e30
FOLD_PULL = 3
TURN_LAG = 6
PULL_A, PULL_B = 3, 1.7
NO_TOKEN = 1 << 20


class Signal:

    def __init__(self, nc, ctx, name, step=1):
        self.sem, self.step, self.n = ctx.enter_context(nc.semaphore(name)), step, 0

    def done(self, ins):
        ins.then_inc(self.sem, self.step)
        self.n += self.step
        return (self, self.n)


class Waits:

    def __init__(self):
        self.seen = {}

    def __call__(self, engine, *marks):
        need = {}
        for signal, n in [m for m in marks if m is not None]:
            need[signal] = max(n, need.get(signal, 0))
        for signal, n in need.items():
            if self.seen.get((id(engine), signal), 0) < n:
                engine.wait_ge(signal.sem, n)
                self.seen[(id(engine), signal)] = n


def program(nc, t, out):
    ctx = ExitStack()
    with ctx:
        pe, act, dve, pool, sp = nc.tensor, nc.scalar, nc.vector, nc.gpsimd, nc.sync
        wait = Waits()

        def signal(name, step=1):
            return Signal(nc, ctx, name, step)

        def sb(name, shape, dt=F32):
            return ctx.enter_context(nc.sbuf_tensor(name, shape, dt))

        by_pe, by_act, by_dve, by_pool = (signal(n) for n in ("by_pe", "by_act", "by_dve", "by_pool"))

        OPS = 2 * GH * LENGTH * 2
        PRING = 2 * GH
        VBYTES = BLOCKS * HEADS * (HD + 1) * 4
        big = sb("big", [P, (3 * OPS + PRING * 4096 + VBYTES) // 4])

        def carve(at, shape, dt=F32, parts=P):
            size = 2 if dt == BF16 else 4
            n = int(np.prod(shape))
            assert at % 4 == 0 and at + n * size <= 3 * OPS + PRING * 4096 + VBYTES
            v = big[0:parts, at // 4:(at + n * size) // 4]
            if dt != F32:
                v = v.bitcast(dt)
            if len(shape) > 1:
                names = " ".join(f"a{i}" for i in range(len(shape)))
                v = v.rearrange(f"p ({names}) -> p {names}", **{f"a{i}": s for i, s in enumerate(shape)})
            return v

        AT_P, AT_V = 3 * OPS, 3 * OPS + PRING * 4096
        tok = sb("tok", [P, BLOCKS, ROW])
        v_aug = carve(AT_V, [BLOCKS, HEADS, HD + 1])
        q_op = [carve(s * OPS, [QT, GH, TILE], BF16) for s in range(3)]
        k_op = [carve(s * OPS + OPS // 2, [GH, LENGTH], BF16) for s in range(3)]
        p_ring = [carve(AT_P + i * 4096, [1024]) for i in range(PRING)]

        ident = sb("ident", [P, P])
        ident_b = sb("ident_b", [P, P], BF16)
        masks = sb("masks", [P, 2, P], BF16)
        ones = sb("ones", [P, P])
        eps_col = sb("eps_col", [P, 3])
        spectral = sb("spectral", [P, KC, D])
        acc_t = [sb(f"acc_t{i}", [P, TILE]) for i in range(2)]
        part_max = [sb(f"part_max{i}", [P, BPT, GH, 4]) for i in range(2)]
        neg_max = sb("neg_max", [P, GH * BPT])
        max_rest = sb("max_rest", [P, GH * BPT])
        max_parts = [sb(f"max_parts{i}", [P, 3, GH * BPT], BF16) for i in range(2)]
        max_t = [sb(f"max_t{i}", [3 * GH * BPT, P], BF16) for i in range(2)]
        recip_l = sb("recip_l", [P, BPT, GH])
        stats = sb("stats", [P, 2, BPT, 6])
        moments = sb("moments", [P, 2, BPT, 2])
        std = sb("std", [P, 2, BPT])
        rstd = sb("rstd", [P, 2, BPT])

        pair = [ctx.enter_context(nc.psum_tensor(f"pair{i}", [P, 2 * TILE], F32)) for i in range(2)]
        single = [ctx.enter_context(nc.psum_tensor(f"single{i}", [P, TILE], F32)) for i in range(4)]
        bank = [pair[0][:, 0:TILE], pair[0][:, TILE:], pair[1][:, 0:TILE], pair[1][:, TILE:]] + \
               [s[:, :] for s in single]

        split_dram = nc.dram_tensor("split_dram", [2, 3, D, TOKENS], BF16).ap()
        routed_dram = nc.dram_tensor("routed_dram", [SLOT_TILES * P, ROW], F32).ap()

        def load(dst, src, name, engine=sp):
            s = signal(name, 16)
            return s.done(engine.dma_start(dst, src))

        x_view = t["L0_attn_x"].rearrange("b (n p) d -> p (b n) d", p=P)
        ident_in = load(ident[:, :], t["c_ident"], "ident_in")
        x_in = [load(tok[:, i * BPT:(i + 1) * BPT, 0:D], x_view[:, i * BPT:(i + 1) * BPT, :], f"x_in{i}")
                for i in range(TILES)]
        AT_A = 2 * OPS
        w_qkv0 = [carve(AT_A + i * 2048, [KC, D]) for i in range(3)]
        w0_in = [load(w_qkv0[i][:, :, :], t[n].rearrange("(c p) n -> p c n", p=P), f"w0_in{i}", act)
                 for i, n in enumerate(("L0_attn_q_w", "L0_attn_k_w", "L0_attn_v_w"))]
        identb_in = load(ident_b[:, :], t["c_ident_b"].bitcast(BF16), "identb_in", act)
        masks_in = load(masks[:, :, :], t["c_masks"].bitcast(BF16).rearrange("a p n -> p a n"), "masks_in", act)
        AT_SPEC = OPS
        cos_m, sin_m, nsin_m, wr_m, wi_m, art_m, ait_m = (carve(AT_SPEC + i * 2048, [KC, D]) for i in range(7))
        spec_in = signal("spec_in", 16)
        for dst, src in ((cos_m, "c_cos"), (sin_m, "c_sin"), (nsin_m, "c_nsin"), (wr_m, "L0_ffn_w_freq_real"),
                         (wi_m, "L0_ffn_w_freq_imag")):
            spec_loaded = spec_in.done(act.dma_start(dst[:, :, :], t[src].rearrange("(c p) n -> p c n", p=P)))

        ones_set = by_dve.done(dve.memset(ones[:, :], 1.0))
        by_dve.done(dve.memset(eps_col[:, 0:1], 1e-5))
        by_dve.done(dve.memset(eps_col[:, 1:2], 1e-6))
        eps_set = by_dve.done(dve.memset(eps_col[:, 2:3], 1e-5 / 4))
        pad_row = carve(2 * OPS + 26624, [ROW])
        by_pool.done(pool.memset(pad_row[:, 0:D + 1], 0.0))
        pad_set = by_pool.done(pool.memset(pad_row[:, D + 1:ROW].bitcast(I32), NO_TOKEN))
        ones_column = by_pool.done(pool.memset(tok[:, :, D:D + 1], 1.0))
        v_ones = by_pool.done(pool.memset(v_aug[:, :, :, :], 1.0))

        x_t = carve(AT_P, [KC, TOKENS])
        parts = [carve(AT_A + 6144 + i * 3072, [3, TILE], BF16) for i in range(4)]
        rest = [carve(AT_A + 6144 + 12288 + i * 2048, [TILE]) for i in range(4)]
        part_free = [None] * 4
        store_sig = [signal(f"split_store{i}", 16) for i in range(4)]
        stored = {}
        xt_copied = {}
        bank_free = [None] * 8
        PROJECT_BANKS = (2, 3, 7)
        v_ready, projected_at, part_last = {}, {}, None
        n_split = 0
        n_bank = 0

        def transpose_x(tile):
            for half in range(2):
                b = half
                wait(pe, x_in[tile], ident_in, bank_free[b])
                for j in range(2):
                    blk = tile * BPT + half * 2 + j
                    for c in range(KC):
                        o = (j * KC + c) * P
                        mm = pe.transpose(bank[b][:, o:o + P], tok[:, blk, c * P:(c + 1) * P], ident[:, :])
                turned = by_pe.done(mm)
                t0 = (tile * BPT + half * 2) * P
                src = bank[b].rearrange("p (j c n) -> p c j n", j=2, c=KC)
                dst = x_t[:, :, t0:t0 + 2 * P].rearrange("p c (j n) -> p c j n", j=2)
                if half == 0:
                    wait(act, turned)
                    xt_copied[tile, half] = bank_free[b] = by_act.done(act.activation(dst, src, ACTF.Copy))
                else:
                    wait(dve, turned)
                    xt_copied[tile, half] = bank_free[b] = by_dve.done(dve.tensor_copy(dst, src))

        def fold_spectral():
            wait(pe, spec_loaded, *[bank_free[b] for b in (2, 3, 7)])
            folds = []
            for dst, terms, b in ((art_m, ((wr_m, cos_m), (wi_m, sin_m)), 2), (ait_m, ((wi_m, cos_m), (wr_m, nsin_m)), 3)):
                for m in range(KC):
                    for i, (l, r) in enumerate(terms):
                        for c in range(KC):
                            mm = pe.matmul(bank[b][:, m * D:(m + 1) * D], l[:, c, m * P:(m + 1) * P], r[:, c, :],
                                           start=(i == 0 and c == 0), stop=(i == 1 and c == KC - 1))
                folded = by_pe.done(mm)
                wait(dve, folded)
                folds.append(by_dve.done(dve.tensor_scalar(dst[:, :, :].rearrange("p c n -> p (c n)"), bank[b], 1.0 / D,
                                                           None, ALU.mult)))
            wait(pe, *folds)
            for m in range(KC):
                for i, (l, r) in enumerate(((art_m, cos_m), (ait_m, nsin_m))):
                    for c in range(KC):
                        mm = pe.matmul(bank[7][:, m * D:(m + 1) * D], l[:, c, m * P:(m + 1) * P], r[:, c, :],
                                       start=(i == 0 and c == 0), stop=(i == 1 and c == KC - 1))
            folded = by_pe.done(mm)
            wait(dve, folded, ident_in)
            spec_copied = by_dve.done(dve.tensor_copy(spectral[:, :, :].rearrange("p c n -> p (c n)"), bank[7]))
            wait(dve, spec_copied)
            for m in range(KC):
                spectral_ready = by_dve.done(dve.tensor_tensor(spectral[:, m, m * P:(m + 1) * P],
                                                               spectral[:, m, m * P:(m + 1) * P], ident[:, :], ALU.add))
            for b in (2, 3, 7):
                bank_free[b] = spec_copied
            return spectral_ready

        def project_tile(tile):
            nonlocal n_split, n_bank, part_last
            cols = slice(tile * TILE, (tile + 1) * TILE)
            transpose_x(tile)
            wait(pe, xt_copied[tile, 0], xt_copied[tile, 1], *w0_in)
            for side, scale in ((0, 1.0 / np.sqrt(HD)), (1, 1.0)):
                for m in range(KC):
                    b = PROJECT_BANKS[n_bank % 3]
                    n_bank += 1
                    wait(pe, bank_free[b])
                    for c in range(KC):
                        mm = pe.matmul(bank[b], w_qkv0[side][:, c, m * P:(m + 1) * P], x_t[:, c, cols],
                                       start=(c == 0), stop=(c == KC - 1))
                    projected = by_pe.done(mm)
                    s = n_split % 4
                    n_split += 1
                    wait(act, projected, part_free[s])
                    high = by_act.done(act.activation(parts[s][:, 0, :], bank[b], ACTF.Copy, scale=float(scale)))
                    wait(dve, high, part_free[s])
                    rested = by_dve.done(dve.scalar_tensor_tensor(rest[s][:, :], bank[b], float(scale),
                                                                  parts[s][:, 0, :], ALU.mult, ALU.subtract))
                    bank_free[b] = rested
                    wait(act, rested)
                    middle = by_act.done(act.activation(parts[s][:, 1, :], rest[s][:, :], ACTF.Copy))
                    wait(pool, middle)
                    low = by_pool.done(pool.tensor_tensor(parts[s][:, 2, :], rest[s][:, :], parts[s][:, 1, :],
                                                          ALU.subtract))
                    wait(sp, low)
                    part_free[s] = store_sig[s].done(sp.dma_start(
                        split_dram[side, :, m * P:(m + 1) * P, cols].rearrange("a p n -> p a n"), parts[s][:, :, :]))
                    stored[side, m, tile] = part_free[s]
                    part_last = low
                    yield
            for half in range(2):
                b = PROJECT_BANKS[n_bank % 3]
                n_bank += 1
                wait(pe, bank_free[b])
                for j in range(2):
                    blk = tile * BPT + half * 2 + j
                    for c in range(KC):
                        mm = pe.matmul(bank[b][:, j * D:(j + 1) * D], x_t[:, c, blk * P:(blk + 1) * P],
                                       w_qkv0[2][:, c, :], start=(c == 0), stop=(c == KC - 1))
                projected = by_pe.done(mm)
                blk = tile * BPT + half * 2
                src = bank[b].rearrange("p (j h d) -> p j h d", j=2, h=HEADS)
                wait(act, projected, v_ones)
                v_ready[tile] = bank_free[b] = by_act.done(act.activation(v_aug[:, blk:blk + 2, :, 0:HD], src, ACTF.Copy))
                projected_at[tile] = projected
                yield

        units = [(b, g) for b in range(BATCHES) for g in range(GROUPS)]
        op_sig = [signal(f"op_in{s}", 16) for s in range(3)]
        op_free = [None] * 3
        op_ready = {}

        def load_operands(u):
            b, g = units[u]
            s = u % 3
            chunk = g * GH * HD // P
            first_tile = b * LENGTH // TILE
            wait(sp, *[stored[side, chunk, first_tile + i] for side in range(2) for i in range(LENGTH // TILE)])
            if u < 3:
                if s == 1:
                    wait(sp, spectral_ready)
                if s == 2:
                    wait(sp, projected_at[TILES - 1], *part_free, v_ready[TILES - 1], part_last, padded)
                sp_src = t["c_key_rows"].bitcast(BF16)
                for h in range(GH):
                    op_sig[s].done(sp.dma_start(k_op[s][0:EXTRA, h, :], sp_src))
            else:
                wait(sp, op_free[s])
            op_sig[s].done(sp.dma_start(q_op[s][0:EXTRA, :, :, :], t["c_query_rows"].bitcast(BF16)[:, g, :, :, :]))
            for i, (q_part, k_part) in enumerate(TERMS):
                rows = slice(EXTRA + i * HD, EXTRA + (i + 1) * HD)
                q_src, k_src = (split_dram[side, part, g * GH * HD:(g + 1) * GH * HD, b * LENGTH:(b + 1) * LENGTH]
                                .rearrange("(h r) n -> r h n", h=GH) for side, part in ((0, q_part), (1, k_part)))
                op_sig[s].done(sp.dma_start(k_op[s][rows, :, :], k_src))
                for qt in range(QT):
                    op_ready[u] = op_sig[s].done(sp.dma_start(q_op[s][rows, qt, :, :],
                                                              q_src[:, :, qt * TILE:(qt + 1) * TILE]))

        ring_free = [None] * 3
        ring_at = 0

        def ring():
            nonlocal ring_at
            i = ring_at % 3
            ring_at += 1
            wait(pe, ring_free[i])
            return 4 + i, i

        max_sig = [signal(f"max_rows{s}", 16) for s in range(2)]
        max_rows_in = {}
        max_t_free = [None, None]
        parts_read = [None, None]
        later = []
        n_max = max_unit = 0
        last_low = None

        def max_chunks(u):
            nonlocal n_max, last_low, max_unit
            max_unit = u
            s = u % 3
            for qt in range(QT):
                pm = part_max[n_max % 2]
                reduced = None
                for r in range(BPT):
                    qb = qt * BPT + r
                    left = (r + 1) * P
                    per = max(1, TILE // left)
                    pieces = [([h], c, TILE) for h in range(GH) for c in range(qt)]
                    pieces += [(list(range(h, h + per)), qt, left) for h in range(0, GH, per)] if per in (1, 2, 4) \
                        else [([h], qt, left) for h in range(GH)]
                    for heads, c, width in pieces:
                        b, i = ring()
                        wait(pe, op_ready[u], masks_in, identb_in)
                        for n, h in enumerate(heads):
                            mm = pe.matmul(bank[b][:, n * width:(n + 1) * width],
                                           q_op[s][:, qt, h, r * P:(r + 1) * P],
                                           k_op[s][:, h, c * TILE:c * TILE + width], start=True, stop=True)
                            if c == qt:
                                mm = pe.matmul(bank[b][:, (n + 1) * width - P:(n + 1) * width], ident_b[:, :],
                                               masks[:, 1, :], start=False, stop=True, skip_group_check=True)
                        scored = by_pe.done(mm)
                        wait(dve, scored)
                        reduced = ring_free[i] = by_dve.done(dve.tensor_reduce(
                            pm[:, r, heads[0]:heads[0] + len(heads), c],
                            bank[b][:, 0:len(heads) * width].rearrange("p (h n) -> p h n", n=width), X, ALU.max))
                        for n in [n for n, (at, _) in enumerate(later) if at <= ring_at][::-1]:
                            later.pop(n)[1]()
                        yield
                wait(dve, reduced, last_low)
                m = n_max % 2
                n_max += 1
                negated = by_dve.done(dve.tensor_reduce(
                    neg_max[:, :].rearrange("p (h r) -> p r h", h=GH), pm[:, :, :, 0:qt + 1], X, ALU.max, negate=True))
                mp = max_parts[m]
                wait(dve, negated)
                wait(pool, negated, parts_read[m])
                high = by_pool.done(pool.tensor_copy(mp[:, 0, :], neg_max[:, :]))
                wait(pool, high)
                rested = by_pool.done(pool.tensor_tensor(max_rest[:, :], neg_max[:, :], mp[:, 0, :], ALU.subtract))
                wait(pool, rested)
                middle = by_pool.done(pool.tensor_copy(mp[:, 1, :], max_rest[:, :]))
                wait(pool, middle)
                low = last_low = by_pool.done(pool.tensor_tensor(mp[:, 2, :], max_rest[:, :], mp[:, 1, :],
                                                                 ALU.subtract))
                later.append((ring_at + TURN_LAG, functools.partial(send_maxima, u, qt, m, low)))

        def send_maxima(u, qt, m, low):
            b, i = ring()
            wait(pe, low)
            n = 3 * GH * BPT
            turned = parts_read[m] = by_pe.done(pe.transpose(bank[b].bitcast(BF16)[0:n, 0:P],
                                                             max_parts[m][:, :, :].rearrange("p a n -> p (a n)"),
                                                             ident_b[:, :]))
            wait(dve, turned, max_t_free[m])
            copied = ring_free[i] = by_dve.done(dve.tensor_copy(max_t[m][:, :], bank[b].bitcast(BF16)[0:n, 0:P]))
            wait(sp, copied)
            for a, row in enumerate(MAX_ROWS):
                dst = q_op[u % 3][row:row + 1, qt, :, :].rearrange("o h n -> o (h n)")
                sent = max_sig[m].done(sp.dma_start(dst, max_t[m][a * GH * BPT:(a + 1) * GH * BPT, :]))
            max_rows_in[u, qt] = max_t_free[m] = sent

        pair_free = [None, None]
        p_free = [None] * PRING
        sums = bank[7]
        sums_free = None
        acc_free = [None, None]
        n_pair = n_p = n_acc = 0
        last_normalized = None
        normalized = {}

        def pairs_of(qt):
            out = [[(2 * i, 0, 0), (2 * i + 1, 0, TILE)] for i in range(2 * qt)]
            k = qt * BPT
            return out + [[(k, 0, 0), (k + 1, P, TILE)], [(k + 2, 2 * P, 2 * P), (k + 3, 3 * P, TILE)]]

        def pull(source, n):
            for _ in range(n):
                if next(source, StopIteration) is StopIteration:
                    return

        def products(job):
            nonlocal sums_free
            u, qt, pieces, tiles, exps, first, last = job
            b, g = units[u]
            if first:
                wait(pe, sums_free)
            for n, (kb, q0, at) in enumerate(pieces):
                wait(pe, *exps)
                for h in range(GH):
                    mm = pe.matmul(sums[32 * h:32 * h + HD + 1, q0:TILE], v_aug[:, b * BPB + kb, g * GH + h, :],
                                   p_ring[tiles[h]][:, at:at + TILE - q0], start=(first and n == 0),
                                   stop=(last and n == 1), skip_group_check=True)
                done = by_pe.done(mm)
                if n == 1:
                    for i in tiles:
                        p_free[i] = done
                    if last:
                        finish_tile(u, qt, done)
                yield

        def finish_tile(u, qt, summed):
            nonlocal sums_free, n_acc
            b, g = units[u]
            a = n_acc % 2
            n_acc += 1
            wait(act, summed, acc_free[a])
            sums_free = copied = by_act.done(act.activation(acc_t[a][:, :], sums, ACTF.Copy))
            put_off.append([3, functools.partial(divide_tile, u, qt, a, copied)])

        def divide_tile(u, qt, a, copied):
            nonlocal last_normalized
            b, g = units[u]
            bk, i = ring()
            wait(pe, copied)
            for r in range(BPT):
                mm = pe.transpose(bank[bk][:, r * P:(r + 1) * P], acc_t[a][:, r * P:(r + 1) * P], ident[:, :])
            turned = acc_free[a] = by_pe.done(mm)
            wait(dve, turned, last_normalized)
            view = bank[bk].rearrange("p (r h n) -> p r h n", r=BPT, h=GH)
            inverse = by_dve.done(dve.reciprocal(recip_l[:, :, :], view[:, :, :, HD]))
            wait(dve, inverse)
            blk = b * BPB + qt * BPT
            dst = tok[:, blk:blk + BPT, g * GH * HD:(g + 1) * GH * HD].rearrange("p r (h n) -> p r h n", h=GH)
            normalized[u, qt] = last_normalized = ring_free[i] = by_dve.done(dve.tensor_tensor(
                dst, view[:, :, :, 0:HD], recip_l[:, :, :].unsqueeze(3).broadcast_to([P, BPT, GH, HD]), ALU.mult))

        def all_max_chunks():
            for u in range(len(units)):
                yield from max_chunks(u)
            while later:
                later.pop(0)[1]()

        def run_put_off(force=False):
            for entry in list(put_off):
                entry[0] -= 1
                if force or entry[0] <= 0:
                    put_off.remove(entry)
                    entry[1]()

        for tile in range(QT):
            for _ in project_tile(tile):
                pass
        load_operands(0)
        spectral_ready = fold_spectral()
        load_operands(1)
        ahead = all_max_chunks()
        for tile in range(QT, TILES):
            for _ in project_tile(tile):
                pull(ahead, PULL_A)
        wait(sp, pad_set)
        padded = load(routed_dram.rearrange("(n p) d -> p n d", p=P),
                      pad_row.unsqueeze(1).broadcast_to([P, SLOT_TILES, ROW]), "padded")

        load_operands(2)
        wait(dve, bank_free[7])
        sums_free = by_dve.done(dve.memset(sums, 0.0))
        for i in range(PRING):
            p_free[i] = v_ready[TILES - 1]
        for b in range(4):
            wait(pe, bank_free[b])
        waiting, put_off = None, []
        owed = 0.0
        for u in range(len(units)):
            s = u % 3
            for qt in range(QT):
                while (u, qt) not in max_rows_in:
                    pull(ahead, 1)
                pairs = pairs_of(qt)
                for n_pairs, pieces in enumerate(pairs):
                    lo, hi = pieces[0][2], pieces[1][2] + TILE - pieces[1][1]
                    work = products(waiting) if waiting else iter(())
                    tiles, exps = [], []
                    for h in range(GH):
                        ps = n_pair % 2
                        n_pair += 1
                        wait(pe, pair_free[ps], max_rows_in[u, qt])
                        for kb, q0, at in pieces:
                            mm = pe.matmul(pair[ps][:, at:at + TILE - q0], k_op[s][:, h, kb * P:(kb + 1) * P],
                                           q_op[s][:, qt, h, q0:TILE], start=True, stop=True)
                            if kb >= qt * BPT:
                                mm = pe.matmul(pair[ps][:, at:at + P], ident_b[:, :], masks[:, 0, :],
                                               start=False, stop=True, skip_group_check=True)
                        scored = by_pe.done(mm)
                        pt = n_p % PRING
                        n_p += 1
                        wait(act, scored, p_free[pt])
                        pair_free[ps] = by_act.done(act.activation(p_ring[pt][:, lo:hi], pair[ps][:, lo:hi], ACTF.Exp))
                        tiles.append(pt)
                        exps.append(pair_free[ps])
                        owed += PULL_B
                        while owed >= 1:
                            if max_unit <= u + 1:
                                pull(ahead, 1)
                            owed -= 1
                        run_put_off()
                        if h % 2:
                            pull(work, 1)
                    pull(work, 10)
                    waiting = (u, qt, pieces, tiles, exps, n_pairs == 0, n_pairs == len(pairs) - 1)
            op_free[s] = scored
            if u + 3 < len(units):
                load_operands(u + 3)
        pull(products(waiting), 10)
        run_put_off(True)
        attention_done = normalized[len(units) - 1, QT - 1]
        by_pe_last = acc_free[(n_acc - 1) % 2]

        small = sb("small", [P, 8 + 32 + 64 + 40])
        spectral_bias = sb("spectral_bias", [P, D])
        fc_bias = sb("fc_bias", [1, D])
        columns = sb("columns", [P, 2 * EXPERTS * KC + EXPERTS * FC])
        cent_t = sb("cent_t", [P, KC, EXPERTS])
        tile_expert = sb("tile_expert", [1, 40], I32)
        position = sb("position", [P, BLOCKS], I32)
        scores1_stat = sb("scores1_stat", [DX, 3, H1])
        shift = sb("shift", [P, 2, BPT])
        bv_t = sb("bv_t", [DX, H1])

        W_BYTES = EXPERTS * KC * FF * 4
        w1 = carve(0, [EXPERTS, KC, FF])
        w2 = carve(W_BYTES, [EXPERTS, FC, D])
        AT_X = AT_P - W_BYTES // EXPERTS
        EARLY = (AT_X - W_BYTES) * EXPERTS // W_BYTES
        attn1 = carve(AT_X, [H1, DX], parts=DX)
        attn1_t = carve(AT_X + 2048, [H1, DX], parts=DX)
        staged = carve(AT_X, [1024])
        gamma = carve(AT_X + 4096, [D])
        beta = carve(AT_X + 5120, [D])
        bv = carve(AT_X + 6144, [H1 * DX], parts=1)
        wqk = carve(AT_P, [KC, 2 * H1 * DX])
        wfc = carve(AT_P + 8192, [H1, D], parts=DX)
        folded_fc = carve(AT_P + 16384, [H1, D], parts=DX)
        wv = carve(AT_P + 16384, [KC, H1 * DX])
        gram_k = carve(AT_P + 24576, [KC, H1 * DX])
        gram = carve(AT_P + 28672, [KC, D + 1])
        gram_row = carve(AT_P + 28672 + KC * (D + 1) * 4, [D + 1], parts=1)
        turned_x = [carve(AT_V + i * 4096, [KC, TILE]) for i in range(2)]
        ow = carve(AT_V + 8192, [KC, D])
        channel = [carve(AT_V + 10240 + b * 2048, [KC, D]) for b in range(BATCHES)]
        res = [carve(AT_V + 14336 + i * 4096, [BPT, D]) for i in range(2)]
        wv_t = carve(AT_V + 22528, [H1, D], parts=DX)
        bqk = carve(AT_V + 30720, [2 * H1 * DX], parts=1)
        gram_k_row = acc_t[0][0:1, :]
        channel_bias = [acc_t[1][:, b * D:(b + 1) * D] for b in range(BATCHES)]
        affinity = carve(AT_X + 6144, [BLOCKS, EXPERTS])

        wait(sp, attention_done, by_pe_last)
        wait(act, attention_done, by_pe_last)
        ow_in = load(ow[:, :, :], t["L0_attn_o_w"].rearrange("(c p) n -> p c n", p=P), "ow_in", act)
        res_sig = [signal(f"res_in{i}", 16) for i in range(2)]
        res_in = {}

        def load_x(g):
            res_in[g] = res_sig[g % 2].done(sp.dma_start(res[g % 2][:, :, :], x_view[:, g * BPT:(g + 1) * BPT, :]))

        load_x(0)
        load_x(1)
        bias_in = load(spectral_bias[:, :], t["L0_ffn_bias"].unsqueeze(0).broadcast_to([P, D]), "bias_in", act)
        stage_in = signal("stage_in", 16)
        n_g, n_f = EXPERTS * KC, EXPERTS * FC
        for rows, at, src in ((n_g, 0, t["L1_ffn_ln_g"].rearrange("e (c p) -> (e c) p", p=P)),
                              (n_g, P, t["L1_ffn_ln_b"].rearrange("e (c p) -> (e c) p", p=P)),
                              (n_f, 2 * P, t["L1_ffn_b1"].rearrange("e (c p) -> (e c) p", p=P)),
                              (EXPERTS, 3 * P, t["L1_ffn_centroids"])):
            stage_in.done(act.dma_start(staged[0:rows, at:at + src.shape[1]], src))
        params_in = stage_in.done(act.dma_start(bv, t["L1_attn_b_qkv"][2 * H1 * DX:].unsqueeze(0)))
        ch_in = signal("channel_in", 16)
        w_qkv1 = t["L1_attn_w_qkv"].rearrange("(c p) n -> p c n", p=P)
        ch_in.done(act.dma_start(wv[:, :, :], w_qkv1[:, :, 2 * H1 * DX:]))
        ch_in.done(act.dma_start(wqk[:, :, :], w_qkv1[:, :, 0:2 * H1 * DX]))
        ch_in.done(act.dma_start(wfc[:, :, :], t["L1_attn_w_fc"].rearrange("(h e) n -> e h n", e=DX)))
        ch_in.done(act.dma_start(bqk, t["L1_attn_b_qkv"][0:2 * H1 * DX].unsqueeze(0)))
        ch_in.done(act.dma_start(gamma, t["L1_attn_gamma"].unsqueeze(0).broadcast_to([P, D])))
        ch_in.done(act.dma_start(beta, t["L1_attn_beta"].unsqueeze(0).broadcast_to([P, D])))
        ch_in.done(act.dma_start(fc_bias[:, :], t["L1_attn_b_fc"].unsqueeze(0)))
        channel_in = ch_in.done(act.dma_start(small[:, :], t["c_small"]))
        w_sig = signal("experts_in", 16)
        w2_view = t["L1_ffn_w2"].rearrange("e (c p) n -> p e c n", p=P)

        def load_experts(first):
            mark = None
            if first:
                for e in range(EXPERTS):
                    mark = w_sig.done(sp.dma_start(w1[:, e, :, :],
                                                   t["L1_ffn_w1"][e].rearrange("(c p) f -> p c f", p=P)))
            for e in range(EARLY) if first else range(EARLY, EXPERTS):
                mark = w_sig.done(sp.dma_start(w2[:, e, :, :], w2_view[:, e, :, :]))
            return mark

        TURN_BANKS, PRODUCT_BANKS, FOLD_BANKS = (0, 1), ((2, 3), (4, 5)), (6, 7)
        turn_free = [None, None]
        n_turn = n_mult = n_norm = 0
        for b in range(8):
            bank_free[b] = attention_done

        def turn(g, ready):
            nonlocal n_turn
            slot = n_turn % 2
            n_turn += 1
            wait(pe, ready)
            for c, b in enumerate(TURN_BANKS):
                wait(pe, bank_free[b])
                for r in range(BPT):
                    mm = pe.transpose(bank[b][:, r * P:(r + 1) * P], tok[:, g * BPT + r, c * P:(c + 1) * P], ident[:, :])
                turned = by_pe.done(mm)
                wait(act, turned, turn_free[slot])
                bank_free[b] = by_act.done(act.activation(turned_x[slot][:, c, :], bank[b], ACTF.Copy))
            return slot, bank_free[TURN_BANKS[1]]

        def multiply(turned, weight, *ready):
            nonlocal n_mult
            slot, copied = turned
            banks = PRODUCT_BANKS[n_mult % 2]
            n_mult += 1
            wait(pe, copied, *ready)
            marks = []
            for half, b in enumerate(banks):
                wait(pe, bank_free[b])
                for j in range(2):
                    r = 2 * half + j
                    for c in range(KC):
                        mm = pe.matmul(bank[b][:, j * D:(j + 1) * D], turned_x[slot][:, c, r * P:(r + 1) * P],
                                       weight[:, c, :], start=(c == 0), stop=(c == KC - 1))
                marks.append(by_pe.done(mm))
            turn_free[slot] = marks[-1]
            return banks, marks

        def add_to(dst, banks, summed, addend, *ready):
            for half, b in enumerate(banks):
                wait(dve, summed[half], *ready)
                bank_free[b] = by_dve.done(dve.tensor_tensor(
                    dst[:, 2 * half:2 * half + 2, :], bank[b].rearrange("p (j n) -> p j n", j=2), addend(half), ALU.add))
            return bank_free[banks[1]]

        def layer_norm(srcs, dsts, eps, ready, engine=None):
            nonlocal n_norm
            m = n_norm % 2
            n_norm += 1
            n = len(srcs)
            wait(dve, ready)
            for r in range(n):
                stat = by_dve.done(dve.bn_stats(stats[:, m, r, :], srcs[r]))
            wait(dve, stat)
            for r in range(n):
                moment = by_dve.done(dve.bn_aggr(moments[:, m, r, :], stats[:, m, r, :]))
            wait(act, moment, eps_set)
            rooted = by_act.done(act.activation(std[:, m, 0:n], moments[:, m, 0:n, 1], ACTF.Sqrt,
                                                bias=eps_col[:, eps:eps + 1]))
            wait(dve, rooted)
            inverse = by_dve.done(dve.reciprocal(rstd[:, m, 0:n], std[:, m, 0:n]))
            wait(dve, inverse)
            if engine is dve:
                for r in range(n):
                    mark = by_dve.done(dve.tensor_scalar(dsts[r], srcs[r], moments[:, m, r, 0:1], rstd[:, m, r:r + 1],
                                                         ALU.subtract, ALU.mult))
                return mark
            shifted = by_dve.done(dve.scalar_tensor_tensor(shift[:, m, 0:n], moments[:, m, 0:n, 0], -1.0,
                                                           rstd[:, m, 0:n], ALU.mult, ALU.mult))
            wait(act, shifted)
            for r in range(n):
                mark = by_act.done(act.activation(dsts[r], srcs[r], ACTF.Identity, bias=shift[:, m, r:r + 1],
                                                  scale=rstd[:, m, r:r + 1]))
            return mark

        def group_of(g):
            return tok[:, g * BPT:(g + 1) * BPT, 0:D]

        def blocks(g):
            return [tok[:, g * BPT + r, 0:D] for r in range(BPT)]

        x1_done, x2_done, x3_done = {}, {}, {}
        channel_ready = {}
        res_free = [None, None]

        class OutputProjection:
            def __init__(self, g):
                self.g = g

            def turn(self):
                self.turned = turn(self.g, attention_done)

            def rest(self):
                g = self.g
                banks, summed = multiply(self.turned, ow, ow_in)
                added = add_to(group_of(g), banks, summed, lambda h: res[g % 2][:, 2 * h:2 * h + 2, :], res_in[g])
                if g + 2 < TILES:
                    wait(sp, added)
                    load_x(g + 2)
                res_free[g % 2] = added
                x1_done[g] = layer_norm(blocks(g), blocks(g), 0, added)

        class SpectralMap:
            def __init__(self, g):
                self.g = g

            def turn(self):
                self.turned = turn(self.g, x1_done[self.g])

            def rest(self):
                g = self.g
                banks, summed = multiply(self.turned, spectral, spectral_ready)
                added = add_to(group_of(g), banks, summed,
                               lambda h: spectral_bias[:, :].unsqueeze(1).broadcast_to([P, 2, D]), bias_in, x1_done[g])
                x2_done[g] = layer_norm(blocks(g), blocks(g), 0, added)

        class ChannelMap:
            def __init__(self, g):
                self.g, self.batch = g, g * TILE // LENGTH

            def turn(self):
                if self.batch not in channel_ready:
                    pull(folds, 10 ** 6, lambda: self.batch in channel_ready)
                self.turned = turn(self.g, x2_done[self.g])

            def rest(self):
                g, y = self.g, res[self.g % 2]
                banks, summed = multiply(self.turned, channel[self.batch], channel_ready[self.batch])
                added = add_to(y, banks, summed,
                               lambda h: channel_bias[self.batch].unsqueeze(1).broadcast_to([P, 2, D]), res_free[g % 2])
                wait(pool, summed[1], gram_read[self.batch], channel_in)
                shifted = by_pool.done(pool.tensor_tensor(group_of(g), group_of(g), beta.unsqueeze(1)
                                                          .broadcast_to([P, BPT, D]), ALU.add))
                normed = layer_norm([y[:, r, :] for r in range(BPT)], [y[:, r, :] for r in range(BPT)], 1, added)
                wait(pool, normed)
                self.scaled = by_pool.done(pool.tensor_tensor(y[:, :, :], y[:, :, :], gamma.unsqueeze(1)
                                                              .broadcast_to([P, BPT, D]), ALU.mult))
                self.shifted = shifted

        class SecondNorm:
            def __init__(self, first):
                self.first = first

            def rest(self):
                g = self.first.g
                wait(dve, self.first.scaled, self.first.shifted)
                res_free[g % 2] = added = by_dve.done(dve.tensor_tensor(group_of(g), group_of(g), res[g % 2][:, :, :],
                                                                        ALU.add))
                x3_done[g] = layer_norm(blocks(g), blocks(g), 0, added)

        class Affinities:
            def __init__(self, g):
                self.g = g

            def turn(self):
                self.turned = turn(self.g, x3_done[self.g])

            def rest(self):
                nonlocal n_mult, affine
                slot, copied = self.turned
                b = PRODUCT_BANKS[n_mult % 2][0]
                n_mult += 1
                wait(pe, copied, bank_free[b], cent_set)
                for r in range(BPT):
                    for c in range(KC):
                        mm = pe.matmul(bank[b][:, r * EXPERTS:(r + 1) * EXPERTS],
                                       turned_x[slot][:, c, r * P:(r + 1) * P], cent_t[:, c, :],
                                       start=(c == 0), stop=(c == KC - 1))
                turn_free[slot] = multiplied = by_pe.done(mm)
                wait(dve, multiplied, *bv_marks)
                affine = bank_free[b] = by_dve.done(dve.tensor_copy(
                    affinity[:, self.g * BPT:(self.g + 1) * BPT, :].rearrange("p b e -> p (b e)"),
                    bank[b][:, 0:BPT * EXPERTS]))

        affine = None

        cent_set = columns_set = None

        def prepare_parameters():
            nonlocal cent_set, columns_set
            b = FOLD_BANKS[0]
            wait(pe, params_in, bank_free[b])
            pe.transpose(bank[b][:, 0:n_g], staged[0:n_g, 0:P], ident[0:n_g, 0:n_g])
            pe.transpose(bank[b][:, n_g:2 * n_g], staged[0:n_g, P:2 * P], ident[0:n_g, 0:n_g])
            pe.transpose(bank[b][:, 2 * n_g:2 * n_g + n_f], staged[0:n_f, 2 * P:3 * P], ident[0:n_f, 0:n_f])
            for c in range(KC):
                o = 2 * n_g + n_f + c * EXPERTS
                mm = pe.transpose(bank[b][:, o:o + EXPERTS], staged[0:EXPERTS, (3 + c) * P:(4 + c) * P],
                                  ident[0:EXPERTS, 0:EXPERTS])
            turned = by_pe.done(mm)
            wait(dve, turned)
            columns_set = by_dve.done(dve.tensor_copy(columns[:, :], bank[b][:, 0:2 * n_g + n_f]))
            cent_set = bank_free[b] = by_dve.done(dve.tensor_copy(
                cent_t[:, :, :].rearrange("p c e -> p (c e)"),
                bank[b][:, 2 * n_g + n_f:2 * n_g + n_f + KC * EXPERTS]))
            yield

        wvt_marks, bv_marks = [], []

        def prepare_values():
            wait(pe, channel_in)
            for h in range(H1):
                b = FOLD_BANKS[h // 2 % 2]
                if h % 2 == 0:
                    wait(pe, bank_free[b])
                for c in range(KC):
                    mm = pe.transpose(bank[b][0:DX, (h % 2) * D + c * P:(h % 2) * D + (c + 1) * P],
                                      wv[:, c, h * DX:(h + 1) * DX], ident[:, :])
                if h % 2:
                    turned = by_pe.done(mm)
                    wait(act, turned)
                    bank_free[b] = by_act.done(act.activation(wv_t[:, h - 1:h + 1, :].rearrange("p h n -> p (h n)"),
                                                              bank[b][0:DX, :], ACTF.Copy))
                    wvt_marks.append(bank_free[b])
                    yield
            b = FOLD_BANKS[0]
            wait(pe, bank_free[b])
            for h in range(H1):
                mm = pe.matmul(bank[b][0:DX, h:h + 1], bv[:, h * DX:(h + 1) * DX], ones[0:1, 0:1], start=True, stop=True)
            turned = by_pe.done(mm)
            wait(dve, turned)
            bank_free[b] = by_dve.done(dve.tensor_copy(bv_t[:, :], bank[b][0:DX, 0:H1]))
            bv_marks.append(bank_free[b])
            bv_marks.append(by_dve.done(dve.memset(gram_row[:, D:D + 1], float(LENGTH))))
            yield

        gram_read = {}

        def fold_channel(batch):
            b0, b1 = FOLD_BANKS
            wait(pe, bank_free[b0], bank_free[b1], ones_column)
            for i in range(BPB):
                blk = batch * BPB + i
                if i % BPT == 0:
                    wait(pe, x2_done[blk // BPT])
                for m, b in enumerate(FOLD_BANKS):
                    mm = pe.matmul(bank[b][:, 0:D + 1], tok[:, blk, m * P:(m + 1) * P], tok[:, blk, 0:D + 1],
                                   start=(i == 0), stop=(i == BPB - 1))
                if i % 2:
                    if i == BPB - 1:
                        gram_read[batch] = summed = by_pe.done(mm)
                    yield
            wait(dve, summed)
            wait(act, summed)
            gram0 = by_dve.done(dve.tensor_copy(gram[:, 0, :], bank[b0][:, 0:D + 1]))
            gram1 = by_act.done(act.activation(gram[:, 1, :], bank[b1][:, 0:D + 1], ACTF.Copy))
            yield
            wait(pe, gram0, gram1)
            for m in range(KC):
                mm = pe.matmul(bank[b0][0:1, m * P:(m + 1) * P], gram[:, m, D:D + 1], ident[:, :], start=True, stop=True)
            rowed = by_pe.done(mm)
            wait(dve, rowed)
            row_set = by_dve.done(dve.tensor_copy(gram_row[:, 0:D], bank[b0][0:1, 0:D]))
            yield
            hk = slice(H1 * DX, 2 * H1 * DX)
            gram_k_marks = []
            for m, b in ((0, b1), (1, b0), (2, b1)):
                rows = P if m < KC else 1
                cols = slice(m * P, m * P + rows)
                wait(pe, row_set, *bv_marks, *gram_k_marks[0:1] if m == 2 else ())
                for c in range(KC):
                    pe.matmul(bank[b][0:rows, :], gram[:, c, cols], wqk[:, c, hk], start=(c == 0), stop=False)
                mm = pe.matmul(bank[b][0:rows, :], gram_row[:, cols], bqk[:, hk], start=False, stop=True)
                multiplied = by_pe.done(mm)
                wait(dve, multiplied)
                gram_k_marks.append(by_dve.done(dve.tensor_copy(
                    gram_k[:, m, :] if m < KC else gram_k_row, bank[b][0:rows, :])))
                yield
            wait(pe, *gram_k_marks)
            for h in range(H1):
                cols = slice(h * DX, (h + 1) * DX)
                for c in range(KC):
                    pe.matmul(bank[b0][0:DX, cols], wqk[:, c, cols], gram_k[:, c, cols], start=(c == 0), stop=False)
                mm = pe.matmul(bank[b0][0:DX, cols], bqk[:, cols], gram_k_row[:, cols], start=False, stop=True)
            scored = by_pe.done(mm)
            yield
            view = bank[b0][0:DX, :].rearrange("p (h n) -> p h n", h=H1)
            wait(dve, scored)
            most = by_dve.done(dve.tensor_reduce(scores1_stat[:, 0, :], view, X, ALU.max))
            wait(dve, most)
            below = by_dve.done(dve.tensor_tensor(attn1[:, :, :], view, scores1_stat[:, 0, :].unsqueeze(2)
                                                  .broadcast_to([DX, H1, DX]), ALU.subtract))
            wait(act, below)
            exped = by_act.done(act.activation(attn1[:, :, :], attn1[:, :, :], ACTF.Exp, scale=1.0 / DX ** 0.5))
            yield
            wait(dve, exped)
            total = by_dve.done(dve.tensor_reduce(scores1_stat[:, 1, :], attn1[:, :, :], X, ALU.add))
            wait(dve, total)
            inverse = by_dve.done(dve.reciprocal(scores1_stat[:, 2, :], scores1_stat[:, 1, :]))
            wait(dve, inverse)
            attended = by_dve.done(dve.tensor_tensor(attn1[:, :, :], attn1[:, :, :], scores1_stat[:, 2, :].unsqueeze(2)
                                                     .broadcast_to([DX, H1, DX]), ALU.mult))
            yield
            wait(pe, attended)
            for h in range(H1):
                mm = pe.transpose(bank[b1][0:DX, h * DX:(h + 1) * DX], attn1[:, h, :], ident[0:DX, 0:DX])
            turned = by_pe.done(mm)
            wait(dve, turned)
            attn_t_set = by_dve.done(dve.tensor_copy(attn1_t[:, :, :].rearrange("p h n -> p (h n)"),
                                                     bank[b1][0:DX, :]))
            yield
            fc_marks = [attn_t_set]
            for h in range(H1):
                b = FOLD_BANKS[h // 2 % 2]
                wait(pe, attn_t_set, *fc_marks[:-1], *wvt_marks)
                mm = pe.matmul(bank[b][0:DX, (h % 2) * D:(h % 2 + 1) * D], attn1_t[:, h, :], wfc[:, h, :],
                               start=True, stop=True)
                if h % 2:
                    multiplied = by_pe.done(mm)
                    wait(act, multiplied)
                    fc_marks.append(by_act.done(act.activation(
                        folded_fc[:, h - 1:h + 1, :].rearrange("p h n -> p (h n)"), bank[b][0:DX, :], ACTF.Copy)))
                    yield
            wait(pe, *fc_marks)
            for m, b in ((0, b0), (1, b1)):
                for h in range(H1):
                    mm = pe.matmul(bank[b][:, 0:D], wv_t[:, h, m * P:(m + 1) * P], folded_fc[:, h, :],
                                   start=(h == 0), stop=(h == H1 - 1))
                folded = by_pe.done(mm)
                wait(dve, folded)
                copied = by_dve.done(dve.tensor_copy(channel[batch][:, m, :], bank[b][:, 0:D]))
                wait(dve, copied)
                identity_added = by_dve.done(dve.tensor_tensor(channel[batch][:, m, m * P:(m + 1) * P],
                                                               channel[batch][:, m, m * P:(m + 1) * P], ident[:, :],
                                                               ALU.add))
                if m == 0:
                    copied0 = copied
                yield
            wait(pe, copied0)
            for h in range(H1):
                mm = pe.matmul(bank[b0][0:1, 0:D], bv_t[:, h:h + 1], folded_fc[:, h, :],
                               start=(h == 0), stop=(h == H1 - 1))
            folded = by_pe.done(mm)
            wait(dve, folded)
            row_added = by_dve.done(dve.tensor_tensor(gram_row[:, 0:D], bank[b0][0:1, 0:D], fc_bias[:, :], ALU.add))
            yield
            wait(pe, row_added, identity_added)
            spread = by_pe.done(pe.matmul(bank[b1][:, 0:D], ones[0:1, :], gram_row[:, 0:D], start=True, stop=True))
            wait(dve, spread)
            bank_free[b0] = bank_free[b1] = by_dve.done(dve.tensor_copy(channel_bias[batch], bank[b1][:, 0:D]))
            channel_ready[batch] = bank_free[b1]
            yield

        def pull(source, n, until=lambda: False):
            for _ in range(n):
                if until() or next(source, StopIteration) is StopIteration:
                    return

        def all_folds():
            yield from prepare_parameters()
            yield from prepare_values()
            for batch in range(BATCHES):
                last_group = (batch + 1) * TILES // BATCHES - 1
                while last_group not in x2_done:
                    yield
                yield from fold_channel(batch)

        jobs = []
        for g in range(TILES + 2):
            jobs += [OutputProjection(g)] if g < TILES else []
            jobs += [SpectralMap(g - 2)] if g >= 2 else []
        firsts = [ChannelMap(g) for g in range(TILES)]
        for g in range(TILES + 4):
            jobs += [firsts[g]] if g < TILES else []
            jobs += [SecondNorm(firsts[g - 1])] if 1 <= g <= TILES else []
            jobs += [Affinities(g - 3)] if 3 <= g < TILES + 3 else []
        folds = all_folds()
        turning = [j for j in jobs if not isinstance(j, SecondNorm)]
        turning[0].turn()
        n_turned = 1
        experts_early = None
        for n, job in enumerate(jobs):
            if not isinstance(job, SecondNorm):
                if n_turned < len(turning):
                    turning[n_turned].turn()
                    n_turned += 1
            job.rest()
            if n == 4:
                experts_early = load_experts(True)
            pull(folds, FOLD_PULL)
        x3_all = [x3_done[g] for g in range(TILES)]
        folded_all = channel_ready[BATCHES - 1]

        wait(sp, folded_all, *[f.scaled for f in firsts], *[f.shifted for f in firsts])
        b2_all = carve(AT_V + VBYTES - 8192, [EXPERTS, D])
        b2_in = load(b2_all[:, :, :], t["L1_ffn_b2"].unsqueeze(0).broadcast_to([P, EXPERTS, D]), "b2_in")
        rank, k128, earlier, numbers = small[:, 0:8], small[:, 8:40], small[:, 40:104], small[:, 104:144]
        AT_E = AT_V + 8192
        flat = [carve(AT_E + i * 1024, [BLOCKS, EXPERTS]) for i in range(6)]
        best, order, tiles_of, first_tile = (carve(AT_E + 6144 + i * 128, [n]) for i, n in
                                             enumerate((BLOCKS, BLOCKS, EXPERTS, EXPERTS)))
        over = carve(AT_E + 6656, [40, EXPERTS])
        tile_f = carve(AT_E + 6656 + 1280, [40])
        used = carve(AT_E + 6656 + 1440, [EXPERTS, 32])
        before = carve(AT_E + 6656 + 2464, [P])
        wait(sp, affine)
        before_in = load(before, t["c_before"], "before_in")
        last = None

        def step(ins):
            nonlocal last
            last = by_dve.done(ins)
            wait(dve, last)
            return last

        def wide(ap, shape, axis):
            return ap.unsqueeze(axis).broadcast_to(shape)

        all_b = [P, BLOCKS, EXPERTS]
        wait(dve, affine, channel_in, turn_free[0], turn_free[1], *x3_all)
        step(dve.tensor_reduce(best, affinity[:, :, :], X, ALU.max))
        best_set = last
        step(dve.tensor_tensor(flat[0][:, :, :], affinity[:, :, :], wide(best, all_b, 2), ALU.is_equal))
        step(dve.tensor_tensor(flat[0][:, :, :], flat[0][:, :, :], wide(rank, all_b, 1), ALU.mult))
        step(dve.tensor_reduce(order, flat[0][:, :, :], X, ALU.max))
        onehot = flat[1]
        step(dve.tensor_tensor(onehot[:, :, :], wide(rank, all_b, 1), wide(order, all_b, 2), ALU.is_equal))
        onehot_set = last
        wait(sp, onehot_set)
        experts_in = load_experts(False)
        wait(act, best_set)
        exped = by_act.done(act.activation(flat[5][:, 0:4, :].rearrange("p a e -> p (a e)"), best, ACTF.Exp, scale=-1.0))
        wait(dve, exped)
        step(dve.tensor_scalar(flat[5][:, 0:4, :], flat[5][:, 0:4, :], 1.0, 2.0, ALU.add, ALU.mult))
        step(dve.reciprocal(tok[:, :, D], flat[5][:, 0:4, :].rearrange("p a e -> p (a e)")))
        gate_set = last
        wait(pool, *x3_all)
        numbered = by_pool.done(pool.iota(tok[:, :, D + 1].bitcast(I32), pattern=[[P, BLOCKS]], base=0,
                                          channel_multiplier=1))
        wait(pe, onehot_set, before_in, bank_free[0], bank_free[1])
        hot = onehot[:, :, :].rearrange("p b e -> p (b e)")
        pe.matmul(bank[0][:, 0:BLOCKS * EXPERTS], before, hot, start=True, stop=True)
        counted = by_pe.done(pe.matmul(bank[1][:, 0:BLOCKS * EXPERTS], ones[:, :], hot, start=True, stop=True))
        wait(dve, counted)
        sums_a, sums_b = flat[2], flat[3]
        step(dve.tensor_copy(sums_a[:, :, :].rearrange("p b e -> p (b e)"), bank[1][:, 0:BLOCKS * EXPERTS]))
        by = 1
        while by < BLOCKS:
            step(dve.tensor_copy(sums_b[:, 0:by, :], sums_a[:, 0:by, :]))
            step(dve.tensor_tensor(sums_b[:, by:, :], sums_a[:, by:, :], sums_a[:, :BLOCKS - by, :], ALU.add))
            sums_a, sums_b = sums_b, sums_a
            by *= 2
        shape = [P, EXPERTS, 32]
        step(dve.tensor_tensor(used[:, :, :], wide(sums_a[:, BLOCKS - 1, :], shape, 2), wide(k128, shape, 1), ALU.is_gt))
        step(dve.tensor_reduce(tiles_of, used[:, :, :], X, ALU.add))
        shape = [P, EXPERTS, EXPERTS]
        cross = sums_b[:, 0:EXPERTS, :]
        step(dve.tensor_tensor(cross, wide(tiles_of, shape, 1), earlier.rearrange("p (a b) -> p a b", a=EXPERTS),
                               ALU.mult))
        step(dve.tensor_reduce(first_tile, cross, X, ALU.add))
        step(dve.tensor_tensor(tiles_of, tiles_of, first_tile, ALU.add))
        shape = [P, 40, EXPERTS]
        step(dve.tensor_tensor(over[:, :, :], wide(tiles_of, shape, 1), wide(numbers, shape, 2), ALU.is_le))
        step(dve.tensor_reduce(tile_f, over[:, :, :], X, ALU.add))
        expert_set = step(dve.tensor_scalar(tile_expert[:, :], tile_f[0:1, :], float(EXPERTS - 1), None, ALU.min))
        step(dve.tensor_scalar(first_tile, first_tile, float(P), None, ALU.mult))
        place = flat[4]
        step(dve.tensor_copy(place[:, 0, :], first_tile))
        step(dve.tensor_tensor(place[:, 1:, :], sums_a[:, :BLOCKS - 1, :], wide(first_tile, [P, BLOCKS - 1, EXPERTS], 1),
                               ALU.add))
        step(dve.tensor_tensor(place[:, :, :], bank[0][:, 0:BLOCKS * EXPERTS].rearrange("p (b e) -> p b e", e=EXPERTS),
                               place[:, :, :], ALU.add))
        step(dve.tensor_tensor(place[:, :, :], place[:, :, :], onehot[:, :, :], ALU.mult))
        step(dve.tensor_reduce(best, place[:, :, :], X, ALU.add))
        placed = step(dve.tensor_copy(position[:, :], best))
        wait(pool, placed, gate_set, numbered, padded)
        scatter = signal("scatter", 16)
        for blk in range(BLOCKS):
            scattered = scatter.done(pool.indirect_dma_start(
                routed_dram, bass.IndirectOffsetOnAxis(ap=position[:, blk:blk + 1], axis=0), tok[:, blk, :], None))

        at = AT_V
        xs = [carve(at + i * ROW * 4, [ROW]) for i in range(4)]
        at += 4 * ROW * 4
        xn = [carve(at + i * 1024, [D]) for i in range(2)]
        at += 2048
        xln_t = [carve(at + i * 1024, [KC, P]) for i in range(2)]
        at += 2048
        hidden_t = [carve(at + i * 4096, [FC, P]) for i in range(2)]
        at += 8192
        mixed = [carve(at + i * 1024, [D]) for i in range(2)]
        at += 2048
        final = [carve(at + i * 1024, [D]) for i in range(2)]
        at += 2048
        assert at <= AT_V + VBYTES - 8192
        tok_flat = tok[:, :, :].rearrange("p b n -> p (b n)")
        w1_now = [tok_flat[:, i * KC * FF:(i + 1) * KC * FF].rearrange("p (c f) -> p c f", c=KC) for i in range(2)]
        out_rows = out.rearrange("b n d -> (b n) d")
        xs_sig = [signal(f"rows_in{i}", 16) for i in range(4)]
        w1_sig = [signal(f"w1_now{i}", 16) for i in range(2)]
        xs_in, w1_in, turned_at, hidt_at, hid_at, norm_at = {}, {}, {}, {}, {}, {}
        xs_free, w1_free, xln_free, hidt_free, final_free = ([placed] * 4, [None] * 2, [None] * 2, [None] * 2,
                                                             [None] * 2)
        for b in range(8):
            bank_free[b] = placed
        out_sig = [signal(f"out{i}", 16) for i in range(2)]
        regs = {}

        def expert(engine, name, i):
            if (name, i) not in regs:
                wait(engine, expert_set)
                regs[name, i] = engine.value_load(tile_expert[0:1, i:i + 1], min_val=0, max_val=EXPERTS - 1)
            return regs[name, i]

        def fetch(i):
            wait(sp, scattered, xs_free[i % 4])
            xs_in[i] = xs_sig[i % 4].done(sp.dma_start(xs[i % 4], routed_dram[i * P:(i + 1) * P, :]))

        def fetch_w1(i):
            s = i % 2
            e = expert(sp, "sp", i)
            wait(sp, scattered, experts_early, experts_in, w1_free[s])
            w1_in[i] = w1_sig[s].done(sp.dma_start(
                w1_now[s][:, :, :].rearrange("p c f -> p (c f)"),
                w1[:, bass.ds(e, 1), :, :].rearrange("p a c f -> p (a c f)")))

        def normalise(i):
            norm_at[i] = layer_norm([xs[i % 4][:, 0:D]], [xn[i % 2]], 0, xs_in[i], dve)

        def turn_tile(i):
            s = i % 2
            b = s
            wait(pe, bank_free[b], norm_at[i])
            for c in range(KC):
                mm = pe.transpose(bank[b][:, c * P:(c + 1) * P], xn[s][:, c * P:(c + 1) * P], ident[:, :])
            turned = by_pe.done(mm)
            e = expert(dve, "dve", i)
            wait(dve, turned, xln_free[s])
            cols_g = columns[:, 0:n_g].rearrange("p (e c) -> p c e", c=KC)
            cols_b = columns[:, n_g:2 * n_g].rearrange("p (e c) -> p c e", c=KC)
            for c in range(KC):
                bank_free[b] = by_dve.done(dve.tensor_scalar(
                    xln_t[s][:, c, :], bank[b][:, c * P:(c + 1) * P], cols_g[:, c, bass.ds(e, 1)],
                    cols_b[:, c, bass.ds(e, 1)], ALU.mult, ALU.add))
            turned_at[i] = bank_free[b]

        def hide(i):
            s = i % 2
            wait(pe, turned_at[i], w1_in[i])
            hid_at[i] = []
            for half in range(2):
                b = 2 + 2 * s + half
                wait(pe, bank_free[b])
                for j in range(FC // 2):
                    f = half * FC // 2 + j
                    for c in range(KC):
                        mm = pe.matmul(bank[b][:, j * P:(j + 1) * P], w1_now[s][:, c, f * P:(f + 1) * P],
                                       xln_t[s][:, c, :], start=(c == 0), stop=(c == KC - 1))
                hid_at[i].append(by_pe.done(mm))
            xln_free[s] = w1_free[s] = hid_at[i][1]

        def rectify(i):
            s = i % 2
            hidt_at[i] = []
            col = columns[:, 2 * n_g:2 * n_g + n_f].rearrange("p (e c) -> p c e", c=FC)
            for half in range(2):
                b = 2 + 2 * s + half
                for j in range(FC // 2):
                    f = half * FC // 2 + j
                    src = bank[b][:, j * P:(j + 1) * P]
                    if half:
                        e = expert(dve, "dve", i)
                        wait(dve, hid_at[i][half], hidt_free[s])
                        m = by_dve.done(dve.tensor_scalar(hidden_t[s][:, f, :], src, col[:, f, bass.ds(e, 1)], 0.0,
                                                          ALU.add, ALU.max))
                    else:
                        e = expert(act, "act", i)
                        wait(act, hid_at[i][half], hidt_free[s])
                        m = by_act.done(act.activation(hidden_t[s][:, f, :], src, ACTF.Relu,
                                                       bias=col[:, f, bass.ds(e, 1)]))
                bank_free[b] = m
                hidt_at[i].append(m)

        def unhide(i):
            s = i % 2
            b = 6 + s
            e = expert(pe, "pe", i)
            wait(pe, bank_free[b], *hidt_at[i], experts_in)
            for f in range(FC):
                mm = pe.matmul(bank[b][:, 0:D], hidden_t[s][:, f, :],
                               w2[:, bass.ds(e, 1), f, :].rearrange("p a n -> p (a n)"),
                               start=(f == 0), stop=(f == FC - 1))
            hidt_free[s] = by_pe.done(mm)
            return hidt_free[s]

        def finish(i, summed):
            s = i % 2
            row = xs[i % 4]
            e = expert(dve, "dve", i)
            wait(dve, summed, b2_in)
            biased = bank_free[6 + s] = by_dve.done(dve.tensor_tensor(
                mixed[s], bank[6 + s][:, 0:D], b2_all[:, bass.ds(e, 1), :].rearrange("p a n -> p (a n)"), ALU.add))
            wait(dve, biased)
            added = by_dve.done(dve.scalar_tensor_tensor(mixed[s], mixed[s], row[:, D:D + 1], row[:, 0:D],
                                                         ALU.mult, ALU.add))
            wait(dve, final_free[s])
            done = layer_norm([mixed[s]], [final[s]], 2, added, dve)
            wait(pool, done)
            final_free[s] = xs_free[i % 4] = out_sig[s].done(pool.indirect_dma_start(
                out_rows, bass.IndirectOffsetOnAxis(ap=row[:, D + 1:D + 2].bitcast(I32), axis=0), final[s], None,
                bounds_check=TOKENS - 1, oob_is_err=False))

        for i in range(2):
            fetch_w1(i)
        for i in range(4):
            fetch(i)
        for i in range(2):
            normalise(i)
            turn_tile(i)
        hide(0)
        rectify(0)
        fetch_w1(2)
        for i in range(SLOT_TILES):
            if i + 1 < SLOT_TILES:
                hide(i + 1)
            if i + 2 < SLOT_TILES:
                normalise(i + 2)
                turn_tile(i + 2)
            if i + 1 < SLOT_TILES:
                rectify(i + 1)
            finish(i, unhide(i))
            if i + 3 < SLOT_TILES:
                fetch_w1(i + 3)
            if i + 4 < SLOT_TILES:
                fetch(i + 4)
        wait(pool, *final_free)
        wait(sp, *final_free)


def bf16_bits(a):
    return (np.ascontiguousarray(a, np.float32).view(np.uint32) >> 16).astype(np.uint16)


def bf16_parts(a):
    out = []
    for _ in range(3):
        part = (np.asarray(a, np.float32).view(np.uint32) & np.uint32(0xFFFF0000)).view(np.float32)
        out.append(part)
        a = (np.asarray(a, np.float32) - part).astype(np.float32)
    return out


def constants():
    i = np.arange(P)
    slopes = np.array([(2.0 ** (-8.0 / HEADS)) ** (h + 1) for h in range(HEADS)], np.float32)
    position = np.arange(LENGTH)
    key_rows = np.zeros((EXTRA, LENGTH), np.float32)
    query_rows = np.zeros((EXTRA, HEADS, LENGTH), np.float32)
    for n, part in enumerate(bf16_parts(slopes)):
        key_rows[2 * n] = position // P * P
        query_rows[2 * n] = part[:, None]
        key_rows[2 * n + 1] = 1.0
        key_rows[6 + n] = position % P
        query_rows[6 + n] = part[:, None]
    angle = 2 * np.pi * (np.outer(np.arange(D), np.arange(D)) % D) / D
    small = np.zeros((P, 8 + 32 + 64 + 40), np.float32)
    small[:, 0:8] = 8 - np.arange(8)
    small[:, 8:40] = P * np.arange(32)
    small[:, 40:104] = (np.arange(8)[None, :] < np.arange(8)[:, None]).reshape(-1)
    small[:, 104:144] = np.arange(40)
    return {
        "c_ident": np.eye(P, dtype=np.float32),
        "c_ident_b": bf16_bits(np.eye(P)),
        "c_masks": bf16_bits(np.stack([np.where(i[:, None] > i[None, :], MASKED, 0.0),
                                       np.where(i[None, :] > i[:, None], MASKED, 0.0)])),
        "c_key_rows": bf16_bits(key_rows), "c_query_rows": bf16_bits(query_rows.reshape(EXTRA, GROUPS, GH, QT, TILE).transpose(0, 1, 3, 2, 4)),
        "c_cos": np.cos(angle).astype(np.float32), "c_sin": np.sin(angle).astype(np.float32),
        "c_nsin": (-np.sin(angle)).astype(np.float32),
        "c_before": (i[:, None] < i[None, :]).astype(np.float32), "c_small": small,
    }


def kernel(**inputs):
    import numpy as _np
    import concourse.bacc as _bacc
    from concourse.bass_utils import run_bass_kernel_spmd as _run

    nc = _bacc.Bacc("TRN2", target_bir_lowering=False, num_devices=1)
    arrays, t = {}, {}
    for name, a in {**inputs, **constants()}.items():
        arrays[f"in_{name}"] = a = _np.ascontiguousarray(a)
        t[name] = nc.dram_tensor(f"in_{name}", a.shape, mybir.dt.from_np(a.dtype), kind="ExternalInput").ap()
    out = nc.dram_tensor("out", (BATCHES, LENGTH, D), F32, kind="ExternalOutput").ap()
    program(nc, t, out)
    r = _run(nc, [arrays], core_ids=[0])
    return r.results[0]["out"]
```

```python
from contextlib import ExitStack
import functools

import numpy as np
import concourse.bass as bass
from concourse import mybir

F32 = mybir.dt.float32
BF16 = mybir.dt.bfloat16
I32 = mybir.dt.int32
ALU = mybir.AluOpType
ACTF = mybir.ActivationFunctionType
X = mybir.AxisListType.X

P = 128
BATCHES, LENGTH, D = 2, 2048, 256
TOKENS = BATCHES * LENGTH
KC = D // P
BLOCKS = TOKENS // P
TILE = 512
BPT = TILE // P
TILES = TOKENS // TILE
HEADS, HD = 16, 16
GH = 4
GROUPS = HEADS // GH
BPB = LENGTH // P
QT = LENGTH // TILE
EXTRA = 32
TERMS = [(0, 0), (0, 1), (0, 2), (1, 0), (1, 1), (2, 0)]
MAX_ROWS = (1, 3, 5)
H1, DX = 8, 64
PAIRS = H1 * DX // P
EXPERTS, FF = 8, 1024
FC = FF // P
SLOT_TILES = BLOCKS + EXPERTS - 1
ROW = D + 2
MASKED = -1e30
GRAM_STEP = 2
FOLD_LAG = 3
C_ORDER = "O0 O1 O2 O3 S0 S1 O4 S2 S3 O5 O6 S4 O7 S5 S6 S7"
ROUTE_LAG = 1
FOLD_PULL, ROUTE_PULL = 1, 1
TURN_LAG = 6
PULL_A, PULL_B = 3, 1.75
NO_TOKEN = 1 << 20
REGION = TOKENS + P
SMALL = 8 + 32 + 64 + 40 + 40 + 8
ROWS_AHEAD, W1_AHEAD = 6, 3


class Signal:

    def __init__(self, nc, ctx, name, step=1):
        self.sem, self.step, self.n = ctx.enter_context(nc.semaphore(name)), step, 0

    def done(self, ins):
        ins.then_inc(self.sem, self.step)
        self.n += self.step
        return (self, self.n)


class Waits:

    def __init__(self):
        self.seen = {}

    def __call__(self, engine, *marks):
        need = {}
        for signal, n in [m for m in marks if m is not None]:
            need[signal] = max(n, need.get(signal, 0))
        for signal, n in need.items():
            if self.seen.get((id(engine), signal), 0) < n:
                engine.wait_ge(signal.sem, n)
                self.seen[(id(engine), signal)] = n


def program(nc, t, out):
    ctx = ExitStack()
    with ctx:
        pe, act, dve, pool, sp = nc.tensor, nc.scalar, nc.vector, nc.gpsimd, nc.sync
        wait = Waits()

        def signal(name, step=1):
            return Signal(nc, ctx, name, step)

        def sb(name, shape, dt=F32):
            return ctx.enter_context(nc.sbuf_tensor(name, shape, dt))

        by_pe, by_act, by_dve, by_pool = (signal(n) for n in ("by_pe", "by_act", "by_dve", "by_pool"))

        OPS = 2 * GH * LENGTH * 2
        PRING = 2 * GH
        VBYTES = BLOCKS * HEADS * (HD + 1) * 4
        big = sb("big", [P, (3 * OPS + PRING * 4096 + VBYTES) // 4])

        def carve(at, shape, dt=F32, parts=P):
            size = 2 if dt == BF16 else 4
            n = int(np.prod(shape))
            assert at % 4 == 0 and at + n * size <= 3 * OPS + PRING * 4096 + VBYTES
            v = big[0:parts, at // 4:(at + n * size) // 4]
            if dt != F32:
                v = v.bitcast(dt)
            if len(shape) > 1:
                names = " ".join(f"a{i}" for i in range(len(shape)))
                v = v.rearrange(f"p ({names}) -> p {names}", **{f"a{i}": s for i, s in enumerate(shape)})
            return v

        AT_P, AT_V = 3 * OPS, 3 * OPS + PRING * 4096
        tok = sb("tok", [P, BLOCKS, ROW])
        v_aug = carve(AT_V, [BLOCKS, HEADS, HD + 1])
        q_op = [carve(s * OPS, [QT, GH, TILE], BF16) for s in range(3)]
        k_op = [carve(s * OPS + OPS // 2, [GH, LENGTH], BF16) for s in range(3)]
        p_ring = [carve(AT_P + i * 4096, [1024]) for i in range(PRING)]

        ident = sb("ident", [P, P])
        ident_b = sb("ident_b", [P, P], BF16)
        masks = sb("masks", [P, 2, P], BF16)
        ones = sb("ones", [P, P])
        eps_col = sb("eps_col", [P, 3])
        spectral = sb("spectral", [P, KC, D])
        acc_t = [sb(f"acc_t{i}", [P, TILE]) for i in range(2)]
        part_max = [sb(f"part_max{i}", [P, BPT, GH, 4]) for i in range(2)]
        neg_max = sb("neg_max", [P, GH * BPT])
        max_rest = sb("max_rest", [P, GH * BPT])
        max_parts = [sb(f"max_parts{i}", [P, 3, GH * BPT], BF16) for i in range(2)]
        max_t = [sb(f"max_t{i}", [3 * GH * BPT, P], BF16) for i in range(2)]
        recip_l = sb("recip_l", [P, BPT, GH])
        stats = sb("stats", [P, 2, BPT, 6])
        moments = sb("moments", [P, 2, BPT, 2])
        std = sb("std", [P, 2, BPT])
        rstd = sb("rstd", [P, 2, BPT])

        pair = [ctx.enter_context(nc.psum_tensor(f"pair{i}", [P, 2 * TILE], F32)) for i in range(3)]
        single = [ctx.enter_context(nc.psum_tensor(f"single{i}", [P, TILE], F32)) for i in range(2)]
        bank = [half for p in pair for half in (p[:, 0:TILE], p[:, TILE:])] + [s[:, :] for s in single]

        split_dram = nc.dram_tensor("split_dram", [2, 3, D, TOKENS], BF16).ap()
        routed_dram = nc.dram_tensor("routed_dram", [EXPERTS * REGION + P, ROW], F32).ap()

        def load(dst, src, name, engine=sp):
            s = signal(name, 16)
            return s.done(engine.dma_start(dst, src))

        x_view = t["L0_attn_x"].rearrange("b (n p) d -> p (b n) d", p=P)
        ident_in = load(ident[:, :], t["c_ident"], "ident_in")
        x_in = [load(tok[:, i * BPT:(i + 1) * BPT, 0:D], x_view[:, i * BPT:(i + 1) * BPT, :], f"x_in{i}")
                for i in range(TILES)]
        AT_A = 2 * OPS
        w_qkv0 = [carve(AT_A + i * 2048, [KC, D]) for i in range(3)]
        w0_in = [load(w_qkv0[i][:, :, :], t[n].rearrange("(c p) n -> p c n", p=P), f"w0_in{i}", act)
                 for i, n in enumerate(("L0_attn_q_w", "L0_attn_k_w", "L0_attn_v_w"))]
        identb_in = load(ident_b[:, :], t["c_ident_b"].bitcast(BF16), "identb_in", act)
        masks_in = load(masks[:, :, :], t["c_masks"].bitcast(BF16).rearrange("a p n -> p a n"), "masks_in", act)
        AT_SPEC = OPS
        cos_m, sin_m, nsin_m, wr_m, wi_m, art_m, ait_m = (carve(AT_SPEC + i * 2048, [KC, D]) for i in range(7))
        spec_in = signal("spec_in", 16)
        for dst, src in ((cos_m, "c_cos"), (sin_m, "c_sin"), (nsin_m, "c_nsin"), (wr_m, "L0_ffn_w_freq_real"),
                         (wi_m, "L0_ffn_w_freq_imag")):
            spec_loaded = spec_in.done(act.dma_start(dst[:, :, :], t[src].rearrange("(c p) n -> p c n", p=P)))

        ones_set = by_dve.done(dve.memset(ones[:, :], 1.0))
        by_dve.done(dve.memset(eps_col[:, 0:1], 1e-5))
        by_dve.done(dve.memset(eps_col[:, 1:2], 1e-6))
        eps_set = by_dve.done(dve.memset(eps_col[:, 2:3], 1e-5 / 4))
        pad_row = carve(2 * OPS + 26624, [ROW])
        by_pool.done(pool.memset(pad_row[:, 0:D + 1], 0.0))
        pad_set = by_pool.done(pool.memset(pad_row[:, D + 1:ROW].bitcast(I32), NO_TOKEN))
        numbered = by_pool.done(pool.iota(tok[:, :, D + 1].bitcast(I32), pattern=[[P, BLOCKS]], base=0,
                                          channel_multiplier=1))
        ones_column = by_pool.done(pool.memset(tok[:, :, D:D + 1], 1.0))
        v_ones = by_pool.done(pool.memset(v_aug[:, :, :, :], 1.0))

        x_t = carve(AT_P, [KC, TOKENS])
        parts = [carve(AT_A + 6144 + i * 3072, [3, TILE], BF16) for i in range(4)]
        rest = [carve(AT_A + 6144 + 12288 + i * 2048, [TILE]) for i in range(4)]
        part_free = [None] * 4
        store_sig = [signal(f"split_store{i}", 16) for i in range(4)]
        stored = {}
        xt_copied = {}
        bank_free = [None] * 8
        PROJECT_BANKS = (2, 3, 7)
        v_ready, projected_at, part_last = {}, {}, None
        n_split = 0
        n_bank = 0

        def transpose_x(tile):
            for half in range(2):
                b = half
                wait(pe, x_in[tile], ident_in, bank_free[b])
                for j in range(2):
                    blk = tile * BPT + half * 2 + j
                    for c in range(KC):
                        o = (j * KC + c) * P
                        mm = pe.transpose(bank[b][:, o:o + P], tok[:, blk, c * P:(c + 1) * P], ident[:, :])
                turned = by_pe.done(mm)
                t0 = (tile * BPT + half * 2) * P
                src = bank[b].rearrange("p (j c n) -> p c j n", j=2, c=KC)
                dst = x_t[:, :, t0:t0 + 2 * P].rearrange("p c (j n) -> p c j n", j=2)
                if half == 0:
                    wait(act, turned)
                    xt_copied[tile, half] = bank_free[b] = by_act.done(act.activation(dst, src, ACTF.Copy))
                else:
                    wait(dve, turned)
                    xt_copied[tile, half] = bank_free[b] = by_dve.done(dve.tensor_copy(dst, src))

        def fold_spectral():
            wait(pe, spec_loaded, *[bank_free[b] for b in (2, 3, 7)])
            folds = []
            for dst, terms, b in ((art_m, ((wr_m, cos_m), (wi_m, sin_m)), 2), (ait_m, ((wi_m, cos_m), (wr_m, nsin_m)), 3)):
                for m in range(KC):
                    for i, (l, r) in enumerate(terms):
                        for c in range(KC):
                            mm = pe.matmul(bank[b][:, m * D:(m + 1) * D], l[:, c, m * P:(m + 1) * P], r[:, c, :],
                                           start=(i == 0 and c == 0), stop=(i == 1 and c == KC - 1))
                folded = by_pe.done(mm)
                wait(dve, folded)
                folds.append(by_dve.done(dve.tensor_scalar(dst[:, :, :].rearrange("p c n -> p (c n)"), bank[b], 1.0 / D,
                                                           None, ALU.mult)))
            wait(pe, *folds)
            for m in range(KC):
                for i, (l, r) in enumerate(((art_m, cos_m), (ait_m, nsin_m))):
                    for c in range(KC):
                        mm = pe.matmul(bank[7][:, m * D:(m + 1) * D], l[:, c, m * P:(m + 1) * P], r[:, c, :],
                                       start=(i == 0 and c == 0), stop=(i == 1 and c == KC - 1))
            folded = by_pe.done(mm)
            wait(dve, folded, ident_in)
            spec_copied = by_dve.done(dve.tensor_copy(spectral[:, :, :].rearrange("p c n -> p (c n)"), bank[7]))
            wait(dve, spec_copied)
            for m in range(KC):
                spectral_ready = by_dve.done(dve.tensor_tensor(spectral[:, m, m * P:(m + 1) * P],
                                                               spectral[:, m, m * P:(m + 1) * P], ident[:, :], ALU.add))
            for b in (2, 3, 7):
                bank_free[b] = spec_copied
            return spectral_ready

        def project_tile(tile):
            nonlocal n_split, n_bank, part_last
            cols = slice(tile * TILE, (tile + 1) * TILE)
            transpose_x(tile)
            wait(pe, xt_copied[tile, 0], xt_copied[tile, 1], *w0_in)
            for side, scale in ((0, 1.0 / np.sqrt(HD)), (1, 1.0)):
                for m in range(KC):
                    b = PROJECT_BANKS[n_bank % 3]
                    n_bank += 1
                    wait(pe, bank_free[b])
                    for c in range(KC):
                        mm = pe.matmul(bank[b], w_qkv0[side][:, c, m * P:(m + 1) * P], x_t[:, c, cols],
                                       start=(c == 0), stop=(c == KC - 1))
                    projected = by_pe.done(mm)
                    s = n_split % 4
                    n_split += 1
                    wait(act, projected, part_free[s])
                    high = by_act.done(act.activation(parts[s][:, 0, :], bank[b], ACTF.Copy, scale=float(scale)))
                    wait(dve, high, part_free[s])
                    rested = by_dve.done(dve.scalar_tensor_tensor(rest[s][:, :], bank[b], float(scale),
                                                                  parts[s][:, 0, :], ALU.mult, ALU.subtract))
                    bank_free[b] = rested
                    wait(act, rested)
                    middle = by_act.done(act.activation(parts[s][:, 1, :], rest[s][:, :], ACTF.Copy))
                    wait(pool, middle)
                    low = by_pool.done(pool.tensor_tensor(parts[s][:, 2, :], rest[s][:, :], parts[s][:, 1, :],
                                                          ALU.subtract))
                    wait(sp, low)
                    part_free[s] = store_sig[s].done(sp.dma_start(
                        split_dram[side, :, m * P:(m + 1) * P, cols].rearrange("a p n -> p a n"), parts[s][:, :, :]))
                    stored[side, m, tile] = part_free[s]
                    part_last = low
                    yield
            for half in range(2):
                b = PROJECT_BANKS[n_bank % 3]
                n_bank += 1
                wait(pe, bank_free[b])
                for j in range(2):
                    blk = tile * BPT + half * 2 + j
                    for c in range(KC):
                        mm = pe.matmul(bank[b][:, j * D:(j + 1) * D], x_t[:, c, blk * P:(blk + 1) * P],
                                       w_qkv0[2][:, c, :], start=(c == 0), stop=(c == KC - 1))
                projected = by_pe.done(mm)
                blk = tile * BPT + half * 2
                src = bank[b].rearrange("p (j h d) -> p j h d", j=2, h=HEADS)
                wait(act, projected, v_ones)
                v_ready[tile] = bank_free[b] = by_act.done(act.activation(v_aug[:, blk:blk + 2, :, 0:HD], src, ACTF.Copy))
                projected_at[tile] = projected
                yield

        units = [(b, g) for b in range(BATCHES) for g in range(GROUPS)]
        op_sig = [signal(f"op_in{s}", 16) for s in range(3)]
        op_free = [None] * 3
        op_ready = {}

        def load_operands(u):
            b, g = units[u]
            s = u % 3
            chunk = g * GH * HD // P
            first_tile = b * LENGTH // TILE
            wait(sp, *[stored[side, chunk, first_tile + i] for side in range(2) for i in range(LENGTH // TILE)])
            if u < 3:
                if s == 1:
                    wait(sp, spectral_ready)
                if s == 2:
                    wait(sp, projected_at[TILES - 1], *part_free, v_ready[TILES - 1], part_last, padded)
                sp_src = t["c_key_rows"].bitcast(BF16)
                for h in range(GH):
                    op_sig[s].done(sp.dma_start(k_op[s][0:EXTRA, h, :], sp_src))
            else:
                wait(sp, op_free[s])
            op_sig[s].done(sp.dma_start(q_op[s][0:EXTRA, :, :, :], t["c_query_rows"].bitcast(BF16)[:, g, :, :, :]))
            for i, (q_part, k_part) in enumerate(TERMS):
                rows = slice(EXTRA + i * HD, EXTRA + (i + 1) * HD)
                q_src, k_src = (split_dram[side, part, g * GH * HD:(g + 1) * GH * HD, b * LENGTH:(b + 1) * LENGTH]
                                .rearrange("(h r) n -> r h n", h=GH) for side, part in ((0, q_part), (1, k_part)))
                op_sig[s].done(sp.dma_start(k_op[s][rows, :, :], k_src))
                for qt in range(QT):
                    op_ready[u] = op_sig[s].done(sp.dma_start(q_op[s][rows, qt, :, :],
                                                              q_src[:, :, qt * TILE:(qt + 1) * TILE]))

        ring_free = [None] * 4
        ring_at = 0
        ring_slots = [0, 1, 2]

        def ring():
            nonlocal ring_at
            i = ring_slots[ring_at % len(ring_slots)]
            ring_at += 1
            wait(pe, ring_free[i])
            return 4 + i, i

        max_sig = [signal(f"max_rows{s}", 16) for s in range(2)]
        max_rows_in = {}
        max_t_free = [None, None]
        parts_read = [None, None]
        later = []
        n_max = max_unit = 0
        last_low = None

        def max_chunks(u):
            nonlocal n_max, last_low, max_unit
            max_unit = u
            s = u % 3
            for qt in range(QT):
                pm = part_max[n_max % 2]
                reduced = None
                for r in range(BPT):
                    qb = qt * BPT + r
                    left = (r + 1) * P
                    per = max(1, TILE // left)
                    pieces = [([h], c, TILE) for h in range(GH) for c in range(qt)]
                    pieces += [(list(range(h, h + per)), qt, left) for h in range(0, GH, per)] if per in (1, 2, 4) \
                        else [([h], qt, left) for h in range(GH)]
                    for heads, c, width in pieces:
                        b, i = ring()
                        wait(pe, op_ready[u], masks_in, identb_in)
                        for n, h in enumerate(heads):
                            mm = pe.matmul(bank[b][:, n * width:(n + 1) * width],
                                           q_op[s][:, qt, h, r * P:(r + 1) * P],
                                           k_op[s][:, h, c * TILE:c * TILE + width], start=True, stop=True)
                            if c == qt:
                                mm = pe.matmul(bank[b][:, (n + 1) * width - P:(n + 1) * width], ident_b[:, :],
                                               masks[:, 1, :], start=False, stop=True, skip_group_check=True)
                        scored = by_pe.done(mm)
                        wait(dve, scored)
                        reduced = ring_free[i] = by_dve.done(dve.tensor_reduce(
                            pm[:, r, heads[0]:heads[0] + len(heads), c],
                            bank[b][:, 0:len(heads) * width].rearrange("p (h n) -> p h n", n=width), X, ALU.max))
                        for n in [n for n, (at, _) in enumerate(later) if at <= ring_at][::-1]:
                            later.pop(n)[1]()
                        yield
                wait(dve, reduced, last_low)
                m = n_max % 2
                n_max += 1
                negated = by_dve.done(dve.tensor_reduce(
                    neg_max[:, :].rearrange("p (h r) -> p r h", h=GH), pm[:, :, :, 0:qt + 1], X, ALU.max, negate=True))
                mp = max_parts[m]
                wait(dve, negated)
                wait(pool, negated, parts_read[m])
                high = by_pool.done(pool.tensor_copy(mp[:, 0, :], neg_max[:, :]))
                wait(pool, high)
                rested = by_pool.done(pool.tensor_tensor(max_rest[:, :], neg_max[:, :], mp[:, 0, :], ALU.subtract))
                wait(pool, rested)
                middle = by_pool.done(pool.tensor_copy(mp[:, 1, :], max_rest[:, :]))
                wait(pool, middle)
                low = last_low = by_pool.done(pool.tensor_tensor(mp[:, 2, :], max_rest[:, :], mp[:, 1, :],
                                                                 ALU.subtract))
                later.append((ring_at + TURN_LAG, functools.partial(send_maxima, u, qt, m, low)))

        def send_maxima(u, qt, m, low):
            b, i = ring()
            wait(pe, low)
            n = 3 * GH * BPT
            turned = parts_read[m] = by_pe.done(pe.transpose(bank[b].bitcast(BF16)[0:n, 0:P],
                                                             max_parts[m][:, :, :].rearrange("p a n -> p (a n)"),
                                                             ident_b[:, :]))
            wait(dve, turned, max_t_free[m])
            copied = ring_free[i] = by_dve.done(dve.tensor_copy(max_t[m][:, :], bank[b].bitcast(BF16)[0:n, 0:P]))
            wait(sp, copied)
            for a, row in enumerate(MAX_ROWS):
                dst = q_op[u % 3][row:row + 1, qt, :, :].rearrange("o h n -> o (h n)")
                sent = max_sig[m].done(sp.dma_start(dst, max_t[m][a * GH * BPT:(a + 1) * GH * BPT, :]))
            max_rows_in[u, qt] = max_t_free[m] = sent

        pairs_used = [0, 1]
        pair_free = [None] * 3
        p_free = [None] * PRING
        sums = bank[7]
        sums_free = None
        acc_free = [None, None]
        n_pair = n_p = n_acc = 0
        last_normalized = None
        normalized = {}

        def pairs_of(qt):
            out = [[(2 * i, 0, 0), (2 * i + 1, 0, TILE)] for i in range(2 * qt)]
            k = qt * BPT
            return out + [[(k, 0, 0), (k + 1, P, TILE)], [(k + 2, 2 * P, 2 * P), (k + 3, 3 * P, TILE)]]

        def pull(source, n):
            for _ in range(n):
                if next(source, StopIteration) is StopIteration:
                    return

        def products(job):
            nonlocal sums_free
            u, qt, pieces, tiles, exps, first, last = job
            b, g = units[u]
            if first:
                wait(pe, sums_free)
            for n, (kb, q0, at) in enumerate(pieces):
                wait(pe, *exps)
                for h in range(GH):
                    mm = pe.matmul(sums[32 * h:32 * h + HD + 1, q0:TILE], v_aug[:, b * BPB + kb, g * GH + h, :],
                                   p_ring[tiles[h]][:, at:at + TILE - q0], start=(first and n == 0),
                                   stop=(last and n == 1), skip_group_check=True)
                done = by_pe.done(mm)
                if n == 1:
                    for i in tiles:
                        p_free[i] = done
                    if last:
                        finish_tile(u, qt, done)
                yield

        def finish_tile(u, qt, summed):
            nonlocal sums_free, n_acc
            b, g = units[u]
            a = n_acc % 2
            n_acc += 1
            wait(act, summed, acc_free[a])
            sums_free = copied = by_act.done(act.activation(acc_t[a][:, :], sums, ACTF.Copy))
            put_off.append([3, functools.partial(divide_tile, u, qt, a, copied)])

        def divide_tile(u, qt, a, copied):
            nonlocal last_normalized
            b, g = units[u]
            bk, i = ring()
            wait(pe, copied)
            for r in range(BPT):
                mm = pe.transpose(bank[bk][:, r * P:(r + 1) * P], acc_t[a][:, r * P:(r + 1) * P], ident[:, :])
            turned = acc_free[a] = by_pe.done(mm)
            wait(dve, turned, last_normalized)
            view = bank[bk].rearrange("p (r h n) -> p r h n", r=BPT, h=GH)
            inverse = by_dve.done(dve.reciprocal(recip_l[:, :, :], view[:, :, :, HD]))
            wait(dve, inverse)
            blk = b * BPB + qt * BPT
            dst = tok[:, blk:blk + BPT, g * GH * HD:(g + 1) * GH * HD].rearrange("p r (h n) -> p r h n", h=GH)
            normalized[u, qt] = last_normalized = ring_free[i] = by_dve.done(dve.tensor_tensor(
                dst, view[:, :, :, 0:HD], recip_l[:, :, :].unsqueeze(3).broadcast_to([P, BPT, GH, HD]), ALU.mult))

        def all_max_chunks():
            for u in range(len(units)):
                yield from max_chunks(u)
            while later:
                later.pop(0)[1]()

        def run_put_off(force=False):
            for entry in list(put_off):
                entry[0] -= 1
                if force or entry[0] <= 0:
                    put_off.remove(entry)
                    entry[1]()

        for tile in range(QT):
            for _ in project_tile(tile):
                pass
        load_operands(0)
        spectral_ready = fold_spectral()
        load_operands(1)
        ahead = all_max_chunks()
        for tile in range(QT, TILES):
            for _ in project_tile(tile):
                pull(ahead, PULL_A)
        wait(sp, pad_set)
        padded = load(routed_dram[EXPERTS * REGION:, :], pad_row, "padded")

        load_operands(2)
        wait(dve, bank_free[7])
        sums_free = by_dve.done(dve.memset(sums, 0.0))
        for i in range(PRING):
            p_free[i] = v_ready[TILES - 1]
        for b in range(4):
            wait(pe, bank_free[b])
        spectral_bias = sb("spectral_bias", [P, D])
        ow = carve(AT_V + 4096, [KC, D])
        res = [carve(AT_V + 6144 + i * 4096, [BPT, D]) for i in range(2)]
        res_sig = [signal(f"res_in{i}", 16) for i in range(2)]
        res_in = {}

        def load_x(g):
            res_in[g] = res_sig[g % 2].done(sp.dma_start(res[g % 2][:, :, :], x_view[:, g * BPT:(g + 1) * BPT, :]))

        waiting, put_off = None, []
        owed = 0.0
        for u in range(len(units)):
            s = u % 3
            for qt in range(QT):
                while (u, qt) not in max_rows_in:
                    pull(ahead, 1)
                if (len(units) - 1, QT - 1) in max_rows_in and len(pairs_used) == 2:
                    pairs_used.append(2)
                    ring_slots[:] = [2]
                    wait(pe, *ring_free[0:2])
                pairs = pairs_of(qt)
                for n_pairs, pieces in enumerate(pairs):
                    lo, hi = pieces[0][2], pieces[1][2] + TILE - pieces[1][1]
                    work = products(waiting) if waiting else iter(())
                    tiles, exps = [], []
                    for h in range(GH):
                        ps = pairs_used[n_pair % len(pairs_used)]
                        n_pair += 1
                        wait(pe, pair_free[ps], max_rows_in[u, qt])
                        for kb, q0, at in pieces:
                            mm = pe.matmul(pair[ps][:, at:at + TILE - q0], k_op[s][:, h, kb * P:(kb + 1) * P],
                                           q_op[s][:, qt, h, q0:TILE], start=True, stop=True)
                            if kb >= qt * BPT:
                                mm = pe.matmul(pair[ps][:, at:at + P], ident_b[:, :], masks[:, 0, :],
                                               start=False, stop=True, skip_group_check=True)
                        scored = by_pe.done(mm)
                        pt = n_p % PRING
                        n_p += 1
                        wait(act, scored, p_free[pt])
                        pair_free[ps] = by_act.done(act.activation(p_ring[pt][:, lo:hi], pair[ps][:, lo:hi], ACTF.Exp))
                        tiles.append(pt)
                        exps.append(pair_free[ps])
                        owed += PULL_B
                        while owed >= 1:
                            if max_unit <= u + 1:
                                pull(ahead, 1)
                            owed -= 1
                        run_put_off()
                        if h % 2:
                            pull(work, 1)
                    pull(work, 10)
                    waiting = (u, qt, pieces, tiles, exps, n_pairs == 0, n_pairs == len(pairs) - 1)
            op_free[s] = scored
            if u + 3 < len(units):
                load_operands(u + 3)
            if u == GROUPS + 1:
                wait(sp, normalized[GROUPS - 1, QT - 1])
                load_x(0)
                load_x(1)
                ow_in = load(ow[:, :, :], t["L0_attn_o_w"].rearrange("(c p) n -> p c n", p=P), "ow_in")
                bias_in = load(spectral_bias[:, :], t["L0_ffn_bias"].unsqueeze(0).broadcast_to([P, D]), "bias_in")
        pull(products(waiting), 10)
        run_put_off(True)
        attention_done = normalized[len(units) - 1, QT - 1]
        by_pe_last = acc_free[(n_acc - 1) % 2]

        small = sb("small", [P, SMALL])
        fc_bias = sb("fc_bias", [1, D])
        columns = sb("columns", [P, 2 * EXPERTS * KC + EXPERTS * FC])
        cent_t = sb("cent_t", [P, KC, EXPERTS])
        tile_expert = sb("tile_expert", [1, 40], I32)
        position = sb("position", [P, BLOCKS], I32)
        tile_row = sb("tile_row", [1, 40], I32)
        pad_at = sb("pad_at", [1, EXPERTS], I32)
        scores1_stat = sb("scores1_stat", [P, 3, PAIRS])
        shift = sb("shift", [P, 2, BPT])

        W_BYTES = EXPERTS * KC * FF * 4
        w1 = carve(0, [EXPERTS, KC, FF])
        w2 = carve(W_BYTES, [EXPERTS, FC, D])
        AT_X = AT_P - W_BYTES // EXPERTS
        EARLY = (AT_X - W_BYTES) * EXPERTS // W_BYTES
        attn1 = carve(AT_X, [PAIRS, P])
        attn1_t = carve(AT_X + 2048, [PAIRS, P])
        bv_wide = carve(AT_X + 4096, [PAIRS, P])
        staged = carve(AT_X + 6144, [P])
        wqk = carve(AT_P, [KC, 2 * H1 * DX])
        wfc = carve(AT_P + 8192, [PAIRS, D])
        folded_fc = carve(AT_P + 12288, [PAIRS, D])
        wv = carve(AT_P + 16384, [KC, H1 * DX])
        gram_k_row = carve(AT_P + 20480, [H1 * DX], parts=1)
        gram_k = carve(AT_P + 22528, [KC, H1 * DX])
        gram = carve(AT_P + 26624, [KC, D + 1])
        turned_x = [carve(AT_V + at, [KC, TILE]) for at in (0, 14336)]
        gamma = carve(AT_V + 4096, [D])
        beta = carve(AT_V + 5120, [D])
        channel = [carve(AT_V + 18432 + b * 2048, [KC, D]) for b in range(BATCHES)]
        pad_tile = carve(AT_V + 18432, [ROW])
        wv_t = carve(AT_V + 22528, [PAIRS, D])
        bq = carve(AT_V + 26624, [H1 * DX], parts=1)
        bk_wide = carve(AT_V + 28672, [H1 * DX])
        b2_all = carve(AT_V + VBYTES - 8192, [EXPERTS, D])
        channel_bias = [acc_t[1][:, b * D:(b + 1) * D] for b in range(BATCHES)]
        scratch = acc_t[0]
        before = scratch[:, 320:384].bitcast(BF16)
        ones_b = scratch[:, 384:448].bitcast(BF16)

        wait(sp, attention_done, by_pe_last)
        stage_in = signal("stage_in", 16)
        n_g, n_f = EXPERTS * KC, EXPERTS * FC
        rows = 0
        for src in (t["L1_ffn_ln_g"].rearrange("e (c p) -> (e c) p", p=P),
                    t["L1_ffn_ln_b"].rearrange("e (c p) -> (e c) p", p=P),
                    t["L1_ffn_b1"].rearrange("e (c p) -> (e c) p", p=P),
                    t["L1_ffn_centroids"].rearrange("e (c p) -> (e c) p", p=P),
                    t["L1_attn_b_qkv"][2 * H1 * DX:].rearrange("(a p) -> a p", p=P)):
            params_in = stage_in.done(sp.dma_start(staged[rows:rows + src.shape[0], :], src))
            rows += src.shape[0]
        n_staged = rows
        ch_in = signal("channel_in", 16)
        w_qkv1 = t["L1_attn_w_qkv"].rearrange("(c p) n -> p c n", p=P)
        b_qkv1 = t["L1_attn_b_qkv"].unsqueeze(0)
        ch_in.done(sp.dma_start(wv[:, :, :], w_qkv1[:, :, 2 * H1 * DX:]))
        ch_in.done(sp.dma_start(wqk[:, :, :], w_qkv1[:, :, 0:2 * H1 * DX]))
        ch_in.done(sp.dma_start(wfc[:, :, :], t["L1_attn_w_fc"].rearrange("(h e) n -> e h n", e=P)))
        ch_in.done(sp.dma_start(bq, b_qkv1[:, 0:H1 * DX]))
        ch_in.done(sp.dma_start(bk_wide, b_qkv1[:, H1 * DX:2 * H1 * DX].broadcast_to([P, H1 * DX])))
        ch_in.done(sp.dma_start(fc_bias[:, :], t["L1_attn_b_fc"].unsqueeze(0)))
        ch_in.done(sp.dma_start(before, t["c_before"].bitcast(BF16)))
        channel_in = ch_in.done(sp.dma_start(small[:, :], t["c_small"]))
        w_sig = signal("experts_in", 16)
        w2_view = t["L1_ffn_w2"].rearrange("e (c p) n -> p e c n", p=P)

        def load_experts(first):
            mark = None
            if first:
                for e in range(EXPERTS):
                    mark = w_sig.done(sp.dma_start(w1[:, e, :, :],
                                                   t["L1_ffn_w1"][e].rearrange("(c p) f -> p c f", p=P)))
            for e in range(EARLY) if first else range(EARLY, EXPERTS):
                mark = w_sig.done(sp.dma_start(w2[:, e, :, :], w2_view[:, e, :, :]))
            return mark

        TURN_BANKS, PRODUCT_BANKS, ROUTE_BANK, FOLD_BANKS = (0, 1), (2, 3, 4), 5, (6, 7)
        turn_free = [None, None]
        n_turn = n_mult = n_norm = 0
        for b in range(8):
            bank_free[b] = attention_done

        def product_bank():
            nonlocal n_mult
            n_mult += 1
            return PRODUCT_BANKS[n_mult % len(PRODUCT_BANKS)]

        def turn(g, ready):
            nonlocal n_turn
            slot = n_turn % 2
            n_turn += 1
            wait(pe, ready)
            for c, b in enumerate(TURN_BANKS):
                wait(pe, bank_free[b])
                for r in range(BPT):
                    mm = pe.transpose(bank[b][:, r * P:(r + 1) * P], tok[:, g * BPT + r, c * P:(c + 1) * P], ident[:, :])
                turned = by_pe.done(mm)
                wait(act, turned, turn_free[slot])
                bank_free[b] = by_act.done(act.activation(turned_x[slot][:, c, :], bank[b], ACTF.Copy))
            return slot, bank_free[TURN_BANKS[1]]

        def multiply(turned, weight, *ready):
            slot, copied = turned
            banks = [product_bank() for _ in range(2)]
            wait(pe, copied, *ready)
            marks = []
            for half, b in enumerate(banks):
                wait(pe, bank_free[b])
                for j in range(2):
                    r = 2 * half + j
                    for c in range(KC):
                        mm = pe.matmul(bank[b][:, j * D:(j + 1) * D], turned_x[slot][:, c, r * P:(r + 1) * P],
                                       weight[:, c, :], start=(c == 0), stop=(c == KC - 1))
                marks.append(by_pe.done(mm))
            turn_free[slot] = marks[-1]
            return banks, marks

        def add_to(dst, banks, summed, addend, *ready):
            for half, b in enumerate(banks):
                wait(dve, summed[half], *ready)
                bank_free[b] = by_dve.done(dve.tensor_tensor(
                    dst[:, 2 * half:2 * half + 2, :], bank[b].rearrange("p (j n) -> p j n", j=2), addend(half), ALU.add))
            return bank_free[banks[1]]

        def norm_begin(srcs, eps, ready):
            nonlocal n_norm
            m = n_norm % 2
            n_norm += 1
            n = len(srcs)
            wait(dve, ready)
            for r in range(n):
                stat = by_dve.done(dve.bn_stats(stats[:, m, r, :], srcs[r]))
            wait(dve, stat)
            for r in range(n):
                moment = by_dve.done(dve.bn_aggr(moments[:, m, r, :], stats[:, m, r, :]))
            wait(act, moment, eps_set)
            return m, by_act.done(act.activation(std[:, m, 0:n], moments[:, m, 0:n, 1], ACTF.Sqrt,
                                                 bias=eps_col[:, eps:eps + 1]))

        def norm_end(begun, srcs, dsts, engine):
            m, rooted = begun
            n = len(srcs)
            wait(dve, rooted)
            inverse = by_dve.done(dve.reciprocal(rstd[:, m, 0:n], std[:, m, 0:n]))
            wait(dve, inverse)
            if engine is dve:
                for r in range(n):
                    mark = by_dve.done(dve.tensor_scalar(dsts[r], srcs[r], moments[:, m, r, 0:1], rstd[:, m, r:r + 1],
                                                         ALU.subtract, ALU.mult))
                return mark
            shifted = by_dve.done(dve.scalar_tensor_tensor(shift[:, m, 0:n], moments[:, m, 0:n, 0], -1.0,
                                                           rstd[:, m, 0:n], ALU.mult, ALU.mult))
            wait(act, shifted)
            for r in range(n):
                mark = by_act.done(act.activation(dsts[r], srcs[r], ACTF.Identity, bias=shift[:, m, r:r + 1],
                                                  scale=rstd[:, m, r:r + 1]))
            return mark

        begun_norms = []

        def norm_later(rows, eps, ready, then):
            begun_norms.append((norm_begin(rows, eps, ready), rows, then))

        def end_norms():
            while begun_norms:
                begun, rows, then = begun_norms.pop(0)
                then(norm_end(begun, rows, rows, act))

        def group_of(g):
            return tok[:, g * BPT:(g + 1) * BPT, 0:D]

        def blocks(g):
            return [tok[:, g * BPT + r, 0:D] for r in range(BPT)]

        x1_done, x2_done, x3_done, x2_job, n_job = {}, {}, {}, {}, 0
        channel_ready = {}
        res_free = [None, None]

        class OutputProjection:
            def __init__(self, g):
                self.g = g

            def turn(self):
                self.turned = turn(self.g, attention_done)

            def rest(self):
                g = self.g
                banks, summed = multiply(self.turned, ow, ow_in)
                added = add_to(group_of(g), banks, summed, lambda h: res[g % 2][:, 2 * h:2 * h + 2, :], res_in[g])
                if g + 2 < TILES:
                    wait(sp, added)
                    load_x(g + 2)
                res_free[g % 2] = added
                norm_later(blocks(g), 0, added, lambda mark: x1_done.update({g: mark}))

        class SpectralMap:
            def __init__(self, g):
                self.g = g

            def turn(self):
                if self.g not in x1_done:
                    end_norms()
                self.turned = turn(self.g, x1_done[self.g])

            def rest(self):
                g = self.g
                banks, summed = multiply(self.turned, spectral, spectral_ready)
                added = add_to(group_of(g), banks, summed,
                               lambda h: spectral_bias[:, :].unsqueeze(1).broadcast_to([P, 2, D]), bias_in, x1_done[g])
                norm_later(blocks(g), 0, added, lambda mark: (x2_done.update({g: mark}), x2_job.update({g: n_job})))

        class ChannelMap:
            def __init__(self, g):
                self.g, self.batch = g, g * TILE // LENGTH

            def turn(self):
                if self.g not in x2_done:
                    end_norms()
                if self.batch not in channel_ready:
                    pull(folds, 10 ** 6, lambda: self.batch in channel_ready)
                self.turned = turn(self.g, x2_done[self.g])

            def rest(self):
                g, y = self.g, res[self.g % 2]
                banks, summed = multiply(self.turned, channel[self.batch], channel_ready[self.batch])
                added = add_to(y, banks, summed,
                               lambda h: channel_bias[self.batch].unsqueeze(1).broadcast_to([P, 2, D]), res_free[g % 2])
                wait(pool, summed[1], gram_read[self.batch], norm_params_in)
                self.shifted = by_pool.done(pool.tensor_tensor(group_of(g), group_of(g), beta.unsqueeze(1)
                                                               .broadcast_to([P, BPT, D]), ALU.add))
                norm_later([y[:, r, :] for r in range(BPT)], 1, added, self.scale)

            def scale(self, normed):
                self.normed = normed

        class SecondNorm:
            def __init__(self, first):
                self.first = first

            def rest(self):
                g = self.first.g
                wait(dve, self.first.normed, norm_params_in)
                scaled = by_dve.done(dve.tensor_tensor(res[g % 2][:, :, :], res[g % 2][:, :, :], gamma.unsqueeze(1)
                                                       .broadcast_to([P, BPT, D]), ALU.mult))
                wait(dve, scaled, self.first.shifted)
                res_free[g % 2] = added = by_dve.done(dve.tensor_tensor(group_of(g), group_of(g), res[g % 2][:, :, :],
                                                                        ALU.add))
                norm_later(blocks(g), 0, added, lambda mark: x3_done.update({g: mark}))

        class Affinities:
            def __init__(self, g):
                self.g = g

            def turn(self):
                if self.g not in x3_done:
                    end_norms()
                self.turned = turn(self.g, x3_done[self.g])

            def rest(self):
                nonlocal n_job
                g = self.g
                if g and g - 1 not in affine_read:
                    n_job += ROUTE_LAG
                    pull(routes, 10 ** 6, lambda: g - 1 in affine_read)
                slot, copied = self.turned
                b = product_bank()
                wait(pe, copied, bank_free[b], cent_set)
                for c in range(KC):
                    mm = pe.matmul(bank[b][0:EXPERTS, :], cent_t[:, c, :], turned_x[slot][:, c, :],
                                   start=(c == 0), stop=(c == KC - 1))
                turn_free[slot] = multiplied = by_pe.done(mm)
                wait(act, multiplied, affine_read.get(g - 1))
                affine_job[g] = n_job
                affine[g] = bank_free[b] = by_act.done(act.activation(aff_t, bank[b][0:EXPERTS, :], ACTF.Copy))

        affine, affine_job, affine_read, placed = {}, {}, {}, {}
        aff_t = spectral[0:EXPERTS, :, :].rearrange("p c n -> p (c n)")

        cent_set = columns_set = None

        def prepare_parameters():
            nonlocal cent_set, columns_set
            b = FOLD_BANKS[0]
            wait(pe, params_in, bank_free[b])
            turned = by_pe.done(pe.transpose(bank[b][:, 0:n_staged], staged[0:n_staged, :], ident[0:n_staged, 0:n_staged]))
            wait(dve, turned)
            o = 2 * n_g + n_f
            columns_set = by_dve.done(dve.tensor_copy(columns[:, :], bank[b][:, 0:o]))
            cent_set = by_dve.done(dve.tensor_copy(
                cent_t[:, :, :].rearrange("p c e -> p e c"), bank[b][:, o:o + n_g].rearrange("p (e c) -> p e c", c=KC)))
            bank_free[b] = by_dve.done(dve.tensor_copy(
                bv_wide[:, :, :], bank[b][:, o + n_g:o + n_g + PAIRS].unsqueeze(2).broadcast_to([P, PAIRS, P])))
            fold_ready.append(bank_free[b])
            fold_ready.append(by_pool.done(pool.memset(attn1[:, :, :], 0.0)))
            yield

        fold_ready = []

        def prepare_values():
            wait(pe, channel_in)
            for half, b in enumerate(FOLD_BANKS):
                wait(pe, bank_free[b])
                for j in range(2):
                    h = half * 2 + j
                    for c in range(KC):
                        mm = pe.transpose(bank[b][:, j * D + c * P:j * D + (c + 1) * P], wv[:, c, h * P:(h + 1) * P],
                                          ident[:, :])
                turned = by_pe.done(mm)
                wait(act, turned)
                bank_free[b] = by_act.done(act.activation(wv_t[:, half * 2:half * 2 + 2, :].rearrange("p h n -> p (h n)"),
                                                          bank[b], ACTF.Copy))
                fold_ready.append(bank_free[b])
                yield

        gram_read = {}

        def fold_channel(batch):
            b0, b1 = FOLD_BANKS
            wait(pe, bank_free[b0], bank_free[b1], ones_column)
            for i in range(BPB):
                blk = batch * BPB + i
                while x2_job.get(blk // BPT, n_job) + FOLD_LAG > n_job:
                    yield
                wait(pe, x2_done[blk // BPT])
                for m, b in enumerate(FOLD_BANKS):
                    mm = pe.matmul(bank[b][:, 0:D + 1], tok[:, blk, m * P:(m + 1) * P], tok[:, blk, 0:D + 1],
                                   start=(i == 0), stop=(i == BPB - 1))
                if i == BPB - 1:
                    gram_read[batch] = summed = by_pe.done(mm)
                if i % GRAM_STEP == GRAM_STEP - 1:
                    yield
            wait(dve, summed)
            wait(act, summed)
            gram0 = by_dve.done(dve.tensor_copy(gram[:, 0, :], bank[b0][:, 0:D + 1]))
            gram1 = by_act.done(act.activation(gram[:, 1, :], bank[b1][:, 0:D + 1], ACTF.Copy))
            yield
            wk = wqk[:, :, H1 * DX:]
            wait(pe, gram0, gram1, *fold_ready)
            gram_k_marks = []
            for m, b in ((KC, b0), (0, b1), (1, b0)):
                cols, rows = (slice(m * P, (m + 1) * P), P) if m < KC else (slice(D, D + 1), 1)
                wait(pe, *(gram_k_marks[0:1] if m == 1 else ()))
                for c in range(KC):
                    mm = pe.matmul(bank[b][0:rows, :], gram[:, c, cols], wk[:, c, :], start=(c == 0), stop=(c == KC - 1))
                multiplied = by_pe.done(mm)
                wait(dve, multiplied)
                gram_k_marks.append(by_dve.done(dve.scalar_tensor_tensor(
                    gram_k[:, m, :] if m < KC else gram_k_row, bk_wide[0:rows, :],
                    gram[:, m, D:D + 1] if m < KC else float(LENGTH), bank[b][0:rows, :], ALU.mult, ALU.add)))
                yield
            wait(pe, *gram_k_marks)
            for h in range(PAIRS):
                cols = slice(h * P, (h + 1) * P)
                for c in range(KC):
                    pe.matmul(bank[b1][:, cols], wqk[:, c, cols], gram_k[:, c, cols], start=(c == 0), stop=False)
                mm = pe.matmul(bank[b1][:, cols], bq[:, cols], gram_k_row[:, cols], start=False, stop=True)
            scored = by_pe.done(mm)
            yield
            halves = (slice(0, DX), slice(DX, P))

            def each(fn, *ready):
                wait(dve, *ready)
                for rows in halves:
                    mark = by_dve.done(fn(rows, bank[b1][rows, :].rearrange("p (h n) -> p h n", h=PAIRS)[:, :, rows],
                                          attn1[rows, :, rows]))
                return mark

            def spread(rows, which):
                return scores1_stat[rows, which, :].unsqueeze(2).broadcast_to([DX, PAIRS, DX])

            most = each(lambda rows, src, dst: dve.tensor_reduce(scores1_stat[rows, 0, :], src, X, ALU.max), scored)
            below = each(lambda rows, src, dst: dve.tensor_tensor(dst, src, spread(rows, 0), ALU.subtract), most)
            wait(act, below)
            for rows in halves:
                exped = by_act.done(act.activation(attn1[rows, :, rows], attn1[rows, :, rows], ACTF.Exp,
                                                   scale=1.0 / DX ** 0.5))
            yield
            wait(pe, exped)
            for h in range(PAIRS):
                mm = pe.transpose(bank[b0][:, h * P:(h + 1) * P], attn1[:, h, :], ident[:, :])
            turned = by_pe.done(mm)
            total = each(lambda rows, src, dst: dve.tensor_reduce(scores1_stat[rows, 1, :], dst, X, ALU.add), exped)
            wait(dve, total)
            inverse = by_dve.done(dve.reciprocal(scores1_stat[:, 2, :], scores1_stat[:, 1, :]))
            wait(dve, turned)
            attn_t_set = by_dve.done(dve.tensor_copy(attn1_t[:, :, :].rearrange("p h n -> p (h n)"), bank[b0]))
            yield
            wait(pe, attn_t_set)
            for half, b in enumerate((b1, b0)):
                for j in range(2):
                    h = half * 2 + j
                    mm = pe.matmul(bank[b][:, j * D:(j + 1) * D], attn1_t[:, h, :], wfc[:, h, :], start=True, stop=True)
                multiplied = by_pe.done(mm)
                for j in range(2):
                    h = half * 2 + j
                    dst, src = folded_fc[:, h, :], bank[b][:, j * D:(j + 1) * D]
                    if half:
                        wait(dve, multiplied)
                        fc1 = by_dve.done(dve.tensor_scalar(dst, src, scores1_stat[:, 2, h:h + 1], None, ALU.mult))
                    else:
                        wait(act, multiplied, inverse)
                        fc0 = by_act.done(act.activation(dst, src, ACTF.Copy, scale=scores1_stat[:, 2, h:h + 1]))
            yield
            wait(pe, fc0, fc1)
            for m, b in ((0, b1), (1, b0)):
                for h in range(PAIRS):
                    mm = pe.matmul(bank[b][:, 0:D], wv_t[:, h, m * P:(m + 1) * P], folded_fc[:, h, :],
                                   start=(h == 0), stop=(h == PAIRS - 1))
                folded = by_pe.done(mm)
                wait(dve, folded)
                copied = by_dve.done(dve.tensor_copy(channel[batch][:, m, :], bank[b][:, 0:D]))
                wait(dve, copied)
                identity_added = by_dve.done(dve.tensor_tensor(channel[batch][:, m, m * P:(m + 1) * P],
                                                               channel[batch][:, m, m * P:(m + 1) * P], ident[:, :],
                                                               ALU.add))
                if m == 0:
                    copied0 = copied
                yield
            wait(pe, copied0)
            for h in range(PAIRS):
                pe.matmul(bank[b1][:, 0:D], bv_wide[:, h, :], folded_fc[:, h, :], start=(h == 0), stop=False)
            spread_bias = by_pe.done(pe.matmul(bank[b1][:, 0:D], ones[0:1, :], fc_bias[:, :], start=False, stop=True))
            wait(dve, spread_bias)
            bank_free[b0] = bank_free[b1] = by_dve.done(dve.tensor_copy(channel_bias[batch], bank[b1][:, 0:D]))
            channel_ready[batch] = bank_free[b1]
            yield

        C8, C32, CE = slice(0, EXPERTS), slice(8, 40), slice(40, 104)
        rank, k128, earlier = small[:, C8], small[:, C32], small[:, CE]
        numbers, slot_row, region = small[:, 104:144], small[:, 144:184], small[:, 184:192]

        class Place:
            def __init__(self, at):
                n = BPT * EXPERTS
                self.equal, self.place = (
                    scratch[:, at + i * n:at + (i + 1) * n].rearrange("p (b e) -> p b e", e=EXPERTS) for i in range(2))
                self.hot = scratch[:, at + 2 * n:at + 2 * n + n // 2].bitcast(BF16).rearrange("p (b e) -> p b e", e=EXPERTS)
                self.order, self.row = (scratch[:, at + 3 * n + i * BPT:at + 3 * n + (i + 1) * BPT] for i in range(2))

        places = [Place(i * 112) for i in range(2)]
        chosen = [scratch[:, 224 + i * 4:228 + i * 4].bitcast(BF16) for i in range(2)]
        chosen_g = scratch[:, 232:240]
        scatter = signal("scatter", 16)
        chosen_read = [None] * 2
        last = scattered = None

        def step(ins):
            nonlocal last
            last = by_dve.done(ins)
            wait(dve, last)
            return last

        def wide(ap, shape, axis):
            return ap.unsqueeze(axis).broadcast_to(shape)

        def route(g):
            nonlocal scattered
            w, b = places[g % 2], ROUTE_BANK
            shape = [P, BPT, EXPERTS]
            group = slice(g * BPT, (g + 1) * BPT)
            n = BPT * EXPERTS
            wait(pe, affine[g], bank_free[b])
            for i in range(BPT):
                mm = pe.transpose(bank[b][:, i * EXPERTS:(i + 1) * EXPERTS], aff_t[:, i * P:(i + 1) * P],
                                  ident[0:EXPERTS, 0:EXPERTS])
            affine_read[g] = by_pe.done(mm)
            affinity = bank[b][:, 0:n].rearrange("p (b e) -> p b e", e=EXPERTS)
            best = tok[:, group, D]
            wait(dve, affine_read[g], channel_in, gram_read[BATCHES - 1], placed.get(g - 2))
            best_set = step(dve.tensor_reduce(best, affinity, X, ALU.max))
            yield
            bank_free[b] = step(dve.tensor_tensor(w.equal, affinity, wide(best, shape, 2), ALU.is_equal))
            step(dve.tensor_tensor(w.equal, w.equal, wide(rank, shape, 1), ALU.mult))
            step(dve.tensor_reduce(w.order, w.equal, X, ALU.max))
            hot_set = step(dve.tensor_tensor(w.hot, wide(rank, shape, 1), wide(w.order, shape, 2), ALU.is_equal))
            wait(pe, hot_set, bank_free[b], onesb_set)
            flat_hot = w.hot.rearrange("p b e -> p (b e)")
            pe.matmul(bank[b][:, 0:n], before, flat_hot, start=True, stop=False)
            for i in range(BPT - 1):
                pe.matmul(bank[b][:, (i + 1) * EXPERTS:n], ones_b,
                          wide(w.hot[:, i, :], [P, BPT - 1 - i, EXPERTS], 1), start=False, stop=False)
            counted = by_pe.done(pe.matmul(bank[b][:, 0:n], ones_b, wide(chosen[g % 2], shape, 1),
                                           start=False, stop=True))
            chosen_read[g % 2] = counted
            yield
            step(dve.tensor_reduce(chosen_g, w.hot.rearrange("p b e -> p e b"), X, ALU.add))
            wait(dve, chosen_read[(g + 1) % 2])
            chosen_set[g + 1] = step(dve.tensor_tensor(chosen[(g + 1) % 2], chosen[g % 2], chosen_g, ALU.add))
            yield
            wait(dve, counted)
            counts = bank[b][:, 0:n].rearrange("p (b e) -> p b e", e=EXPERTS)
            bank_free[b] = step(dve.tensor_tensor(w.place, counts, wide(region, shape, 1), ALU.add))
            step(dve.tensor_tensor(w.place, w.place, w.hot, ALU.mult))
            step(dve.tensor_reduce(w.row, w.place, X, ALU.add))
            placed[g] = step(dve.tensor_copy(position[:, group], w.row))
            wait(pool, placed[g], numbered, x3_done[g])
            for blk in range(g * BPT, (g + 1) * BPT):
                scattered = scatter.done(pool.indirect_dma_start(
                    routed_dram, bass.IndirectOffsetOnAxis(ap=position[:, blk:blk + 1], axis=0), tok[:, blk, :], None))
            yield

        chosen_set = {0: by_dve.done(dve.memset(chosen[0], 0.0))}
        wait(dve, chosen_set[0])
        wait(pool, attention_done)
        onesb_set = by_pool.done(pool.memset(ones_b, 1.0))

        def all_routes():
            for g in range(TILES):
                while affine_job.get(g, n_job) + ROUTE_LAG > n_job:
                    yield
                yield from route(g)

        def pull(source, n, until=lambda: False):
            for _ in range(n):
                if until() or next(source, StopIteration) is StopIteration:
                    return

        def all_folds():
            yield from prepare_parameters()
            yield from prepare_values()
            for batch in range(BATCHES):
                yield from fold_channel(batch)

        jobs = []
        for name in C_ORDER.split():
            jobs.append((OutputProjection if name[0] == "O" else SpectralMap)(int(name[1:])))
        firsts = [ChannelMap(g) for g in range(TILES)]
        slots = list(range(TILES)) + [None] * 4
        for n, g in enumerate(slots):
            second, third = ([slots[n - k] if n >= k else None] for k in (2, 4))
            jobs += [SecondNorm(firsts[h]) for h in second if h is not None]
            jobs += [firsts[g]] if g is not None else []
            jobs += [Affinities(h) for h in third if h is not None]
        folds, routes = all_folds(), all_routes()
        turning = [j for j in jobs if not isinstance(j, SecondNorm)]
        turning[0].turn()
        n_turned = 1
        experts_early = experts_in = None
        for n, job in enumerate(jobs):
            n_job = n
            if not isinstance(job, SecondNorm):
                if n_turned < len(turning):
                    turning[n_turned].turn()
                    n_turned += 1
            pull(folds, FOLD_PULL)
            end_norms()
            job.rest()
            if n == 4:
                experts_early = load_experts(True)
            if isinstance(job, OutputProjection) and job.g == TILES - 1:
                wait(sp, *turn_free)
                par_in = signal("norm_params_in", 16)
                par_in.done(sp.dma_start(gamma, t["L1_attn_gamma"].unsqueeze(0).broadcast_to([P, D])))
                norm_params_in = par_in.done(sp.dma_start(beta, t["L1_attn_beta"].unsqueeze(0).broadcast_to([P, D])))
            pull(folds, FOLD_PULL)
            pull(routes, ROUTE_PULL)
            if isinstance(job, ChannelMap) and job.g == TILES // BATCHES:
                wait(pool, turn_free[0], turn_free[1])
                by_pool.done(pool.memset(pad_tile[:, 0:D + 1], 0.0))
                pad_tile_set = by_pool.done(pool.memset(pad_tile[:, D + 1:ROW].bitcast(I32), NO_TOKEN))
            if experts_in is None and BATCHES - 1 in channel_ready:
                wait(sp, channel_ready[BATCHES - 1])
                experts_in = load_experts(False)
                b2_in = load(b2_all[:, :, :], t["L1_ffn_b2"].unsqueeze(0).broadcast_to([P, EXPERTS, D]), "b2_in")
        n_job += ROUTE_LAG
        pull(routes, 10 ** 6)

        final_f = [carve(AT_V + i * 1280, [40, EXPERTS]) for i in range(2)]
        used = carve(AT_V + 2560, [EXPERTS, 32])
        cross = carve(AT_V + 3584, [EXPERTS, EXPERTS])
        tiles_of, first_tile, count, weight, ends = (carve(AT_V + 14336 + i * 32, [EXPERTS]) for i in range(5))
        tile_f, row_f = (carve(AT_V + 14496 + i * 160, [40]) for i in range(2))
        wait(pe, chosen_set[TILES], bank_free[ROUTE_BANK])
        counted = by_pe.done(pe.matmul(bank[ROUTE_BANK][:, 0:EXPERTS], ones_b, chosen[TILES % 2], start=True, stop=True))
        wait(dve, counted, *turn_free)
        step(dve.tensor_copy(count, bank[ROUTE_BANK][:, 0:EXPERTS]))
        pads_set = step(dve.tensor_tensor(pad_at[:, :], count[0:1, :], region[0:1, :], ALU.add))
        pad_sig = [signal(f"pads{i}", 16) for i in range(2)]
        pads = [None, None]
        for e in range(EXPERTS):
            queue = (sp, act)[e % 2]
            wait(queue, pads_set, pad_tile_set)
            at = queue.value_load(pad_at[0:1, e:e + 1], min_val=e * REGION, max_val=e * REGION + TOKENS)
            pads[e % 2] = pad_sig[e % 2].done(queue.dma_start(routed_dram[bass.ds(at, P), :], pad_tile[:, :]))
        shape = [P, EXPERTS, 32]
        step(dve.tensor_tensor(used[:, :, :], wide(count, shape, 2), wide(k128, shape, 1), ALU.is_gt))
        step(dve.tensor_reduce(tiles_of, used[:, :, :], X, ALU.add))
        shape = [P, EXPERTS, EXPERTS]
        step(dve.tensor_tensor(cross[:, :, :], wide(tiles_of, shape, 1), earlier.rearrange("p (a b) -> p a b", a=EXPERTS),
                               ALU.mult))
        step(dve.tensor_reduce(first_tile, cross[:, :, :], X, ALU.add))
        step(dve.tensor_tensor(ends, tiles_of, first_tile, ALU.add))
        shape = [P, 40, EXPERTS]
        over, weighed = final_f
        step(dve.tensor_tensor(over[:, :, :], wide(ends, shape, 1), wide(numbers, shape, 2), ALU.is_le))
        step(dve.tensor_reduce(tile_f, over[:, :, :], X, ALU.add))
        expert_set = step(dve.tensor_scalar(tile_expert[:, :], tile_f[0:1, :], float(EXPERTS - 1), None, ALU.min))
        step(dve.tensor_scalar(weight, tiles_of, -float(P), float(REGION), ALU.mult, ALU.add))
        step(dve.tensor_tensor(weighed[:, :, :], over[:, :, :], wide(weight, shape, 1), ALU.mult))
        step(dve.tensor_reduce(row_f, weighed[:, :, :], X, ALU.add))
        step(dve.tensor_tensor(row_f, row_f, slot_row, ALU.add))
        rows_set = step(dve.tensor_scalar(tile_row[:, :], row_f[0:1, :], float(EXPERTS * REGION), None, ALU.min))

        at = AT_V
        xs = [carve(at + i * ROW * 4, [ROW]) for i in range(ROWS_AHEAD)]
        at += ROWS_AHEAD * ROW * 4
        xn = [carve(at + i * 1024, [D]) for i in range(2)]
        at += 2048
        xln_t = [carve(at + i * 1024, [KC, P]) for i in range(2)]
        at += 2048
        hidden_t = [carve(at + i * 4096, [FC, P]) for i in range(2)]
        at += 8192
        mixed = [carve(at + i * 1024, [D]) for i in range(2)]
        at += 2048
        final = [carve(at + i * 1024, [D]) for i in range(2)]
        at += 2048
        assert at <= AT_V + VBYTES - 8192
        tok_flat = tok[:, :, :].rearrange("p b n -> p (b n)")
        w1_now = [tok_flat[:, i * KC * FF:(i + 1) * KC * FF].rearrange("p (c f) -> p c f", c=KC) for i in range(W1_AHEAD)]
        out_rows = out.rearrange("b n d -> (b n) d")
        xs_sig = [signal(f"rows_in{i}", 16) for i in range(ROWS_AHEAD)]
        w1_sig = [signal(f"w1_now{i}", 16) for i in range(W1_AHEAD)]
        xs_in, w1_in, turned_at, hidt_at, hid_at, norm_at = {}, {}, {}, {}, {}, {}
        xs_free, w1_free, xln_free, hidt_free, final_free = ([rows_set] * ROWS_AHEAD, [None] * W1_AHEAD, [None] * 2, [None] * 2,
                                                             [None] * 2)
        for b in range(8):
            bank_free[b] = rows_set
        out_sig = [signal(f"out{i}", 16) for i in range(2)]
        regs = {}

        def expert(engine, name, i):
            if (name, i) not in regs:
                wait(engine, expert_set)
                regs[name, i] = engine.value_load(tile_expert[0:1, i:i + 1], min_val=0, max_val=EXPERTS - 1)
            return regs[name, i]

        def fetch(i):
            wait(sp, rows_set)
            at = sp.value_load(tile_row[0:1, i:i + 1], min_val=0, max_val=EXPERTS * REGION)
            wait(sp, scattered, padded, *pads, xs_free[i % ROWS_AHEAD])
            xs_in[i] = xs_sig[i % ROWS_AHEAD].done(sp.dma_start(xs[i % ROWS_AHEAD], routed_dram[bass.ds(at, P), :]))

        def fetch_w1(i):
            s = i % W1_AHEAD
            e = expert(sp, "sp", i)
            wait(sp, scattered, experts_early, experts_in, w1_free[s])
            w1_in[i] = w1_sig[s].done(sp.dma_start(
                w1_now[s][:, :, :].rearrange("p c f -> p (c f)"),
                w1[:, bass.ds(e, 1), :, :].rearrange("p a c f -> p (a c f)")))

        gate = recip_l[:, :, :].rearrange("p a b -> p (a b)")
        gate_at = {}

        def gates(tiles):
            for i in tiles:
                k = i % ROWS_AHEAD
                wait(act, xs_in[i], xs_free[k])
                exped = by_act.done(act.activation(gate[:, k:k + 1], xs[k][:, D:D + 1], ACTF.Exp, scale=-1.0))
            for i in tiles:
                k = i % ROWS_AHEAD
                wait(dve, exped)
                doubled = by_dve.done(dve.tensor_scalar(gate[:, k:k + 1], gate[:, k:k + 1], 1.0, 2.0, ALU.add, ALU.mult))
                wait(dve, doubled)
                gate_at[i] = by_dve.done(dve.reciprocal(gate[:, k:k + 1], gate[:, k:k + 1]))

        def normalise(i):
            rows = [xs[i % ROWS_AHEAD][:, 0:D]]
            norm_at[i] = norm_end(norm_begin(rows, 0, xs_in[i]), rows, [xn[i % 2]], dve)

        def turn_tile(i):
            s = i % 2
            b = s
            wait(pe, bank_free[b], norm_at[i])
            for c in range(KC):
                mm = pe.transpose(bank[b][:, c * P:(c + 1) * P], xn[s][:, c * P:(c + 1) * P], ident[:, :])
            turned = by_pe.done(mm)
            e = expert(dve, "dve", i)
            wait(dve, turned, xln_free[s])
            cols_g = columns[:, 0:n_g].rearrange("p (e c) -> p c e", c=KC)
            cols_b = columns[:, n_g:2 * n_g].rearrange("p (e c) -> p c e", c=KC)
            for c in range(KC):
                bank_free[b] = by_dve.done(dve.tensor_scalar(
                    xln_t[s][:, c, :], bank[b][:, c * P:(c + 1) * P], cols_g[:, c, bass.ds(e, 1)],
                    cols_b[:, c, bass.ds(e, 1)], ALU.mult, ALU.add))
            turned_at[i] = bank_free[b]

        def hide(i):
            s = i % 2
            wait(pe, turned_at[i], w1_in[i])
            hid_at[i] = []
            for half in range(2):
                b = 2 + 2 * s + half
                wait(pe, bank_free[b])
                for j in range(FC // 2):
                    f = half * FC // 2 + j
                    for c in range(KC):
                        mm = pe.matmul(bank[b][:, j * P:(j + 1) * P], w1_now[i % W1_AHEAD][:, c, f * P:(f + 1) * P],
                                       xln_t[s][:, c, :], start=(c == 0), stop=(c == KC - 1))
                hid_at[i].append(by_pe.done(mm))
            xln_free[s] = w1_free[i % W1_AHEAD] = hid_at[i][1]

        def rectify(i):
            s = i % 2
            hidt_at[i] = []
            col = columns[:, 2 * n_g:2 * n_g + n_f].rearrange("p (e c) -> p c e", c=FC)
            for half in range(2):
                b = 2 + 2 * s + half
                for j in range(FC // 2):
                    f = half * FC // 2 + j
                    src = bank[b][:, j * P:(j + 1) * P]
                    if half:
                        e = expert(dve, "dve", i)
                        wait(dve, hid_at[i][half], hidt_free[s])
                        m = by_dve.done(dve.tensor_scalar(hidden_t[s][:, f, :], src, col[:, f, bass.ds(e, 1)], 0.0,
                                                          ALU.add, ALU.max))
                    else:
                        e = expert(act, "act", i)
                        wait(act, hid_at[i][half], hidt_free[s])
                        m = by_act.done(act.activation(hidden_t[s][:, f, :], src, ACTF.Relu,
                                                       bias=col[:, f, bass.ds(e, 1)]))
                bank_free[b] = m
                hidt_at[i].append(m)

        def unhide(i):
            s = i % 2
            b = 6 + s
            e = expert(pe, "pe", i)
            wait(pe, bank_free[b], *hidt_at[i], experts_in)
            for f in range(FC):
                mm = pe.matmul(bank[b][:, 0:D], hidden_t[s][:, f, :],
                               w2[:, bass.ds(e, 1), f, :].rearrange("p a n -> p (a n)"),
                               start=(f == 0), stop=(f == FC - 1))
            hidt_free[s] = by_pe.done(mm)
            return hidt_free[s]

        def finish(i, summed):
            s = i % 2
            row = xs[i % ROWS_AHEAD]
            e = expert(dve, "dve", i)
            wait(dve, summed, b2_in)
            biased = bank_free[6 + s] = by_dve.done(dve.tensor_tensor(
                mixed[s], bank[6 + s][:, 0:D], b2_all[:, bass.ds(e, 1), :].rearrange("p a n -> p (a n)"), ALU.add))
            wait(dve, biased, gate_at[i])
            added = by_dve.done(dve.scalar_tensor_tensor(mixed[s], mixed[s], gate[:, i % ROWS_AHEAD:i % ROWS_AHEAD + 1], row[:, 0:D],
                                                         ALU.mult, ALU.add))
            wait(dve, final_free[s])
            done = norm_end(norm_begin([mixed[s]], 2, added), [mixed[s]], [final[s]], dve)
            wait(pool, done)
            final_free[s] = xs_free[i % ROWS_AHEAD] = out_sig[s].done(pool.indirect_dma_start(
                out_rows, bass.IndirectOffsetOnAxis(ap=row[:, D + 1:D + 2].bitcast(I32), axis=0), final[s], None,
                bounds_check=TOKENS - 1, oob_is_err=False))

        for i in range(ROWS_AHEAD):
            fetch(i)
            if i < W1_AHEAD:
                fetch_w1(i)
        normalise(0)
        turn_tile(0)
        normalise(1)
        hide(0)
        turn_tile(1)
        gates([0])
        rectify(0)
        normalise(2)
        fetch_w1(W1_AHEAD)
        for i in range(SLOT_TILES):
            for name, engine in (("pe", pe), ("act", act), ("dve", dve)):
                if i + 1 < SLOT_TILES:
                    expert(engine, name, i + 1)
            if i + 1 < SLOT_TILES:
                hide(i + 1)
            if i + 2 < SLOT_TILES:
                turn_tile(i + 2)
            summed = unhide(i)
            if i + 1 < SLOT_TILES:
                rectify(i + 1)
            if i + 3 < SLOT_TILES:
                normalise(i + 3)
            finish(i, summed)
            if i % 3 == 0:
                gates([j for j in range(i + 1, i + 4) if j < SLOT_TILES])
            if i + 1 + W1_AHEAD < SLOT_TILES:
                fetch_w1(i + 1 + W1_AHEAD)
            if i + ROWS_AHEAD < SLOT_TILES:
                fetch(i + ROWS_AHEAD)
        wait(pool, *final_free)
        wait(sp, *final_free)


def bf16_bits(a):
    return (np.ascontiguousarray(a, np.float32).view(np.uint32) >> 16).astype(np.uint16)


def bf16_parts(a):
    out = []
    for _ in range(3):
        part = (np.asarray(a, np.float32).view(np.uint32) & np.uint32(0xFFFF0000)).view(np.float32)
        out.append(part)
        a = (np.asarray(a, np.float32) - part).astype(np.float32)
    return out


def constants():
    i = np.arange(P)
    slopes = np.array([(2.0 ** (-8.0 / HEADS)) ** (h + 1) for h in range(HEADS)], np.float32)
    position = np.arange(LENGTH)
    key_rows = np.zeros((EXTRA, LENGTH), np.float32)
    query_rows = np.zeros((EXTRA, HEADS, LENGTH), np.float32)
    for n, part in enumerate(bf16_parts(slopes)):
        key_rows[2 * n] = position // P * P
        query_rows[2 * n] = part[:, None]
        key_rows[2 * n + 1] = 1.0
        key_rows[6 + n] = position % P
        query_rows[6 + n] = part[:, None]
    angle = 2 * np.pi * (np.outer(np.arange(D), np.arange(D)) % D) / D
    small = np.zeros((P, SMALL), np.float32)
    small[:, 0:8] = 8 - np.arange(8)
    small[:, 8:40] = P * np.arange(32)
    small[:, 40:104] = (np.arange(8)[None, :] < np.arange(8)[:, None]).reshape(-1)
    small[:, 104:144] = np.arange(40)
    small[:, 144:184] = P * np.arange(40)
    small[:, 184:192] = REGION * np.arange(8)
    return {
        "c_ident": np.eye(P, dtype=np.float32),
        "c_ident_b": bf16_bits(np.eye(P)),
        "c_masks": bf16_bits(np.stack([np.where(i[:, None] > i[None, :], MASKED, 0.0),
                                       np.where(i[None, :] > i[:, None], MASKED, 0.0)])),
        "c_key_rows": bf16_bits(key_rows), "c_query_rows": bf16_bits(query_rows.reshape(EXTRA, GROUPS, GH, QT, TILE).transpose(0, 1, 3, 2, 4)),
        "c_cos": np.cos(angle).astype(np.float32), "c_sin": np.sin(angle).astype(np.float32),
        "c_nsin": (-np.sin(angle)).astype(np.float32),
        "c_before": bf16_bits(i[:, None] < i[None, :]), "c_small": small,
    }


def kernel(**inputs):
    import numpy as _np
    import concourse.bacc as _bacc
    from concourse.bass_utils import run_bass_kernel_spmd as _run

    nc = _bacc.Bacc("TRN2", target_bir_lowering=False, num_devices=1)
    arrays, t = {}, {}
    for name, a in {**inputs, **constants()}.items():
        arrays[f"in_{name}"] = a = _np.ascontiguousarray(a)
        t[name] = nc.dram_tensor(f"in_{name}", a.shape, mybir.dt.from_np(a.dtype), kind="ExternalInput").ap()
    out = nc.dram_tensor("out", (BATCHES, LENGTH, D), F32, kind="ExternalOutput").ap()
    program(nc, t, out)
    r = _run(nc, [arrays], core_ids=[0])
    return r.results[0]["out"]
```
